# Optimizing a Trainium2 kernel written in Bass

```python
import numpy as np
import jax
import jax.numpy as jnp

def _softmax(x, axis=-1):
    return jax.nn.softmax(x, axis=axis)

def _gelu(x):
    return jax.nn.gelu(x, approximate=True)

def _silu(x):
    return jax.nn.silu(x)

def _sigmoid(x):
    return jax.nn.sigmoid(x)

def _layernorm(x, axis=-1, eps=1e-05):
    m = jnp.mean(x, axis=axis, keepdims=True)
    v = jnp.var(x, axis=axis, keepdims=True)
    return (x - m) / jnp.sqrt(v + eps)

def _scatter_add(tgt, idx, src, axis=0):
    return tgt.at[idx].add(src)

def _segment_sum(src, seg, n):
    return jax.ops.segment_sum(src, seg, n)
kernel_name = 'mk_vit_tower_cls_d2_tok_img1024_r4_8c9fb9'

def setup_inputs(seed: int=0):
    np.random.seed(seed)
    _w = jnp.asarray

    def _rec_inputs():
        import jax
        import jax.numpy as jnp
        _rk = jax.random.key(seed)
        x = -0.00016672 + 0.999947 * jax.random.normal(jax.random.fold_in(_rk, 1), (64, 3, 96, 96), jnp.float32)
        cls_tok = 0.02 * jax.random.normal(jax.random.fold_in(_rk, 5), (1, 1, 256), jnp.float32)
        return (x, cls_tok)
    x, cls_tok = _rec_inputs()

    def _L0_tok_setup():
        import jax, jax.numpy as jnp
        import numpy as np
        B, C, H, Wd = (64, 3, 96, 96)
        PH, PW, D = (16, 16, 256)
        PATCH_DIM = C * PH * PW
        N_TOK = H // PH * (Wd // PW)
        key = jax.random.key(seed)
        k1, k2, k3, k4, k5 = jax.random.split(key, 5)
        x = jax.random.normal(k1, (B, C, H, Wd), dtype=jnp.float32)
        W = jax.random.normal(k2, (D, PATCH_DIM), dtype=jnp.float32) * PATCH_DIM ** (-0.5)
        b = jax.random.normal(k3, (D,), dtype=jnp.float32) * 0.02
        cls_token = jax.random.normal(k4, (1, 1, D), dtype=jnp.float32)
        pos_embedding = jax.random.normal(k5, (1, N_TOK + 1, D), dtype=jnp.float32) * 0.02
        return {'x': x, 'W': W, 'b': b, 'cls_token': cls_token, 'pos_embedding': pos_embedding}
    _L0_tok_all = _L0_tok_setup()
    _L0_tok_in = {k: v for k, v in _L0_tok_all.items() if k in ('W', 'b', 'cls_token', 'pos_embedding')}
    del _L0_tok_all

    def _L0_attn_setup():
        import jax, jax.numpy as jnp
        import numpy as np
        EMBED_DIM = 256
        NUM_HEADS = 16
        HEAD_DIM = EMBED_DIM // NUM_HEADS
        ROPE_BASE = 10000.0

        def _rope(t):
            hd = t.shape[-1]
            half = hd // 2
            S = t.shape[2]
            inv_freq = 1.0 / ROPE_BASE ** (jnp.arange(half, dtype=jnp.float32) / half)
            ang = jnp.arange(S, dtype=jnp.float32)[:, None] * inv_freq[None, :]
            cos, sin = (jnp.cos(ang), jnp.sin(ang))
            t1, t2 = (t[..., :half], t[..., half:])
            return jnp.concatenate([t1 * cos - t2 * sin, t1 * sin + t2 * cos], axis=-1)

        def _attention_mc(x, Wq, Wk, Wv, Wo):
            B, S, D = x.shape
            H, hd = (NUM_HEADS, HEAD_DIM)
            q = (x @ Wq.T).reshape(B, S, H, hd).transpose(0, 2, 1, 3)
            k = (x @ Wk.T).reshape(B, S, H, hd).transpose(0, 2, 1, 3)
            v = (x @ Wv.T).reshape(B, S, H, hd).transpose(0, 2, 1, 3)
            q = _rope(q)
            k = _rope(k)
            scale = 1.0 / jnp.sqrt(jnp.float32(hd))
            scores = jnp.einsum('bhqd,bhkd->bhqk', q, k) * scale
            causal = jnp.tril(jnp.ones((S, S), dtype=bool))
            scores = jnp.where(causal, scores, jnp.finfo(scores.dtype).min)
            attn = jax.nn.softmax(scores, axis=-1)
            out = jnp.einsum('bhqk,bhkd->bhqd', attn, v)
            out = out.transpose(0, 2, 1, 3).reshape(B, S, D)
            return out @ Wo.T
        key = jax.random.key(seed)
        ks = jax.random.split(key, 5)
        B, S, D = (2, 512, EMBED_DIM)
        bound = 1.0 / np.sqrt(D)
        x = jax.random.normal(ks[0], (B, S, D), dtype=jnp.float32)
        Wq = jax.random.uniform(ks[1], (D, D), dtype=jnp.float32, minval=-bound, maxval=bound)
        Wk = jax.random.uniform(ks[2], (D, D), dtype=jnp.float32, minval=-bound, maxval=bound)
        Wv = jax.random.uniform(ks[3], (D, D), dtype=jnp.float32, minval=-bound, maxval=bound)
        Wo = jax.random.uniform(ks[4], (D, D), dtype=jnp.float32, minval=-bound, maxval=bound)
        return {'x': x, 'Wq': Wq, 'Wk': Wk, 'Wv': Wv, 'Wo': Wo}
    _L0_attn_all = _L0_attn_setup()
    _L0_attn_in = {k: v for k, v in _L0_attn_all.items() if k in ('Wq', 'Wk', 'Wv', 'Wo')}
    del _L0_attn_all

    def _L0_ffn_setup():
        import jax, jax.numpy as jnp
        import numpy as np
        TOP_P = 0.8
        B, T, H, F, E = (2, 512, 256, 1024, 8)
        key = jax.random.key(seed)
        k0, k1, k2, k3 = jax.random.split(key, 4)
        x = jax.random.normal(k0, (B, T, H), jnp.float32)
        Wr = jax.random.normal(k1, (H, E), jnp.float32) * 0.02
        br = jnp.zeros((E,), jnp.float32)
        W1 = jax.random.normal(k2, (E, H, F), jnp.float32) * 0.02
        b1 = jnp.zeros((E, F), jnp.float32)
        W2 = jax.random.normal(k3, (E, F, H), jnp.float32) * 0.02
        b2 = jnp.zeros((E, H), jnp.float32)
        return {'x': x, 'Wr': Wr, 'br': br, 'W1': W1, 'b1': b1, 'W2': W2, 'b2': b2}
    _L0_ffn_all = _L0_ffn_setup()
    _L0_ffn_in = {k: v for k, v in _L0_ffn_all.items() if k in ('Wr', 'br', 'W1', 'b1', 'W2', 'b2')}
    del _L0_ffn_all

    def _L1_attn_setup():
        import jax, jax.numpy as jnp
        import numpy as np
        B, N, D, H = (2, 512, 256, 16)
        HD = D // H

        def l2norm(x, eps=1e-12):
            n = jnp.sqrt(jnp.sum(x * x, axis=-1, keepdims=True))
            return x / jnp.maximum(n, eps)

        def dplr_delta_rule(q, k, v, a, gk):
            qm, km, vm, am, gm = (jnp.moveaxis(t, 1, 0) for t in (q, k, v, a, gk))

            def step(S, inp):
                qt, kt, vt, at, gkt = inp
                Sp = S * jnp.exp(gkt)[..., None]
                u = jnp.einsum('bhk,bhkv->bhv', at, Sp) + vt
                S = Sp + jnp.einsum('bhk,bhv->bhkv', kt, u)
                o = jnp.einsum('bhk,bhkv->bhv', qt, S)
                return (S, o)
            S0 = jnp.zeros((q.shape[0], q.shape[2], q.shape[3], v.shape[3]), q.dtype)
            _, o = jax.lax.scan(step, S0, (qm, km, vm, am, gm))
            return jnp.moveaxis(o, 0, 1)

        def _forward(x, Wq, Wk, Wv, Wgamma, Wf, Wg1, Wg2, Wo, norm_w):
            b, n, d = x.shape
            silu = jax.nn.silu
            q = silu(x @ Wq)
            k = silu(x @ Wk)
            v = silu(x @ Wv)
            log_f = jax.nn.log_sigmoid(x @ Wf)
            gamma = -jax.nn.sigmoid(x @ Wgamma)
            q = q.reshape(b, n, H, HD)
            k = l2norm(k.reshape(b, n, H, HD))
            v = v.reshape(b, n, H, HD)
            gk = jnp.broadcast_to(log_f[..., None], (b, n, H, HD))
            a = k * gamma[..., None] * jnp.exp(gk)
            out = dplr_delta_rule(q, k, v, a, gk)
            out = out.reshape(b, n, d)
            gate = jax.nn.sigmoid(x @ Wg1 @ Wg2)
            out = out * gate
            mu = jnp.mean(out, axis=-1, keepdims=True)
            var = jnp.mean(jnp.square(out - mu), axis=-1, keepdims=True)
            out = (out - mu) * jax.lax.rsqrt(var + 1e-05) * norm_w
            return out @ Wo
        key = jax.random.key(seed)
        ks = jax.random.split(key, 10)
        s = 0.02
        return {'x': jax.random.normal(ks[0], (B, N, D), jnp.float32), 'Wq': jax.random.normal(ks[1], (D, D), jnp.float32) * s, 'Wk': jax.random.normal(ks[2], (D, D), jnp.float32) * s, 'Wv': jax.random.normal(ks[3], (D, D), jnp.float32) * s, 'Wgamma': jax.random.normal(ks[4], (D, H), jnp.float32) * s, 'Wf': jax.random.normal(ks[5], (D, H), jnp.float32) * s, 'Wg1': jax.random.normal(ks[6], (D, HD), jnp.float32) * s, 'Wg2': jax.random.normal(ks[7], (HD, D), jnp.float32) * s, 'Wo': jax.random.normal(ks[8], (D, D), jnp.float32) * s, 'norm_w': jnp.ones((D,), jnp.float32)}
    _L1_attn_all = _L1_attn_setup()
    _L1_attn_in = {k: v for k, v in _L1_attn_all.items() if k in ('Wq', 'Wk', 'Wv', 'Wgamma', 'Wf', 'Wg1', 'Wg2', 'Wo', 'norm_w')}
    del _L1_attn_all

    def _L1_ffn_setup():
        import jax, jax.numpy as jnp
        import numpy as np
        EMB = 256
        FF = 4 * EMB

        def _ternary(w):
            scale = jnp.maximum(jnp.mean(jnp.abs(w)), 1e-08)
            w_t = jnp.clip(jnp.round(w / scale), -1.0, 1.0)
            return w + jax.lax.stop_gradient(w_t - w)
        key = jax.random.key(seed)
        kx, k1, k2, kb1, kb2 = jax.random.split(key, 5)
        x = jax.random.normal(kx, (4, 512, EMB), dtype=jnp.float32)
        lim1 = 1.0 / np.sqrt(EMB)
        lim2 = 1.0 / np.sqrt(FF)
        W1 = jax.random.uniform(k1, (FF, EMB), jnp.float32, -lim1, lim1)
        b1 = jax.random.uniform(kb1, (FF,), jnp.float32, -lim1, lim1)
        W2 = jax.random.uniform(k2, (EMB, FF), jnp.float32, -lim2, lim2)
        b2 = jax.random.uniform(kb2, (EMB,), jnp.float32, -lim2, lim2)
        return {'x': x, 'W1': W1, 'b1': b1, 'W2': W2, 'b2': b2}
    _L1_ffn_all = _L1_ffn_setup()
    _L1_ffn_in = {k: v for k, v in _L1_ffn_all.items() if k in ('W1', 'b1', 'W2', 'b2')}
    del _L1_ffn_all
    return {'x': x, 'cls_tok': cls_tok, 'L0_tok_W': _L0_tok_in['W'], 'L0_tok_b': _L0_tok_in['b'], 'L0_tok_cls_token': _L0_tok_in['cls_token'], 'L0_tok_pos_embedding': _L0_tok_in['pos_embedding'], 'L0_attn_Wq': _L0_attn_in['Wq'], 'L0_attn_Wk': _L0_attn_in['Wk'], 'L0_attn_Wv': _L0_attn_in['Wv'], 'L0_attn_Wo': _L0_attn_in['Wo'], 'L0_ffn_Wr': _L0_ffn_in['Wr'], 'L0_ffn_br': _L0_ffn_in['br'], 'L0_ffn_W1': _L0_ffn_in['W1'], 'L0_ffn_b1': _L0_ffn_in['b1'], 'L0_ffn_W2': _L0_ffn_in['W2'], 'L0_ffn_b2': _L0_ffn_in['b2'], 'L1_attn_Wq': _L1_attn_in['Wq'], 'L1_attn_Wk': _L1_attn_in['Wk'], 'L1_attn_Wv': _L1_attn_in['Wv'], 'L1_attn_Wgamma': _L1_attn_in['Wgamma'], 'L1_attn_Wf': _L1_attn_in['Wf'], 'L1_attn_Wg1': _L1_attn_in['Wg1'], 'L1_attn_Wg2': _L1_attn_in['Wg2'], 'L1_attn_Wo': _L1_attn_in['Wo'], 'L1_attn_norm_w': _L1_attn_in['norm_w'], 'L1_ffn_W1': _L1_ffn_in['W1'], 'L1_ffn_b1': _L1_ffn_in['b1'], 'L1_ffn_W2': _L1_ffn_in['W2'], 'L1_ffn_b2': _L1_ffn_in['b2']}

def reference(x, cls_tok, L0_tok_W, L0_tok_b, L0_tok_cls_token, L0_tok_pos_embedding, L0_attn_Wq, L0_attn_Wk, L0_attn_Wv, L0_attn_Wo, L0_ffn_Wr, L0_ffn_br, L0_ffn_W1, L0_ffn_b1, L0_ffn_W2, L0_ffn_b2, L1_attn_Wq, L1_attn_Wk, L1_attn_Wv, L1_attn_Wgamma, L1_attn_Wf, L1_attn_Wg1, L1_attn_Wg2, L1_attn_Wo, L1_attn_norm_w, L1_ffn_W1, L1_ffn_b1, L1_ffn_W2, L1_ffn_b2):
    import jax
    import jax.numpy as jnp

    def _L0_tok_ref(x, W, b, cls_token, pos_embedding):
        import jax, jax.numpy as jnp
        import numpy as np
        B, C, H, Wd = (64, 3, 96, 96)
        PH, PW, D = (16, 16, 256)
        PATCH_DIM = C * PH * PW
        N_TOK = H // PH * (Wd // PW)
        Bc = x.shape[0]
        nh, nw = (H // PH, Wd // PW)
        patches = x.reshape(Bc, C, nh, PH, nw, PW)
        patches = patches.transpose(0, 2, 4, 1, 3, 5).reshape(Bc, nh * nw, PATCH_DIM)
        tokens = jnp.einsum('bnp,dp->bnd', patches, W) + b
        cls = jnp.broadcast_to(cls_token, (Bc, 1, D))
        tokens = jnp.concatenate([cls, tokens], axis=1)
        return tokens + pos_embedding

    def _L0_attn_ref(x, Wq, Wk, Wv, Wo):
        import jax, jax.numpy as jnp
        import numpy as np
        EMBED_DIM = 256
        NUM_HEADS = 16
        HEAD_DIM = EMBED_DIM // NUM_HEADS
        ROPE_BASE = 10000.0

        def _rope(t):
            hd = t.shape[-1]
            half = hd // 2
            S = t.shape[2]
            inv_freq = 1.0 / ROPE_BASE ** (jnp.arange(half, dtype=jnp.float32) / half)
            ang = jnp.arange(S, dtype=jnp.float32)[:, None] * inv_freq[None, :]
            cos, sin = (jnp.cos(ang), jnp.sin(ang))
            t1, t2 = (t[..., :half], t[..., half:])
            return jnp.concatenate([t1 * cos - t2 * sin, t1 * sin + t2 * cos], axis=-1)

        def _attention_mc(x, Wq, Wk, Wv, Wo):
            B, S, D = x.shape
            H, hd = (NUM_HEADS, HEAD_DIM)
            q = (x @ Wq.T).reshape(B, S, H, hd).transpose(0, 2, 1, 3)
            k = (x @ Wk.T).reshape(B, S, H, hd).transpose(0, 2, 1, 3)
            v = (x @ Wv.T).reshape(B, S, H, hd).transpose(0, 2, 1, 3)
            q = _rope(q)
            k = _rope(k)
            scale = 1.0 / jnp.sqrt(jnp.float32(hd))
            scores = jnp.einsum('bhqd,bhkd->bhqk', q, k) * scale
            causal = jnp.tril(jnp.ones((S, S), dtype=bool))
            scores = jnp.where(causal, scores, jnp.finfo(scores.dtype).min)
            attn = jax.nn.softmax(scores, axis=-1)
            out = jnp.einsum('bhqk,bhkd->bhqd', attn, v)
            out = out.transpose(0, 2, 1, 3).reshape(B, S, D)
            return out @ Wo.T
        return _attention_mc(x, Wq, Wk, Wv, Wo)

    def _L0_ffn_ref(x, Wr, br, W1, b1, W2, b2):
        import jax, jax.numpy as jnp
        import numpy as np
        TOP_P = 0.8
        B, T, H, F, E = (2, 512, 256, 1024, 8)
        probs = jax.nn.softmax(x @ Wr + br, axis=-1)
        sorted_idx = jnp.argsort(-probs, axis=-1)
        sorted_probs = jnp.take_along_axis(probs, sorted_idx, axis=-1)
        cum = jnp.cumsum(sorted_probs, axis=-1)
        mask = cum < TOP_P
        mask = mask.at[..., 0].set(True)
        inv = jnp.argsort(sorted_idx, axis=-1)
        keep = jnp.take_along_axis(mask, inv, axis=-1)
        gate = probs * keep
        h = jax.nn.relu(jnp.einsum('bth,ehf->betf', x, W1) + b1[None, :, None, :])
        y = jnp.einsum('betf,efh->beth', h, W2) + b2[None, :, None, :]
        return jnp.einsum('bte,beth->bth', gate, y)

    def _L1_attn_ref(x, Wq, Wk, Wv, Wgamma, Wf, Wg1, Wg2, Wo, norm_w):
        import jax, jax.numpy as jnp
        import numpy as np
        B, N, D, H = (2, 512, 256, 16)
        HD = D // H

        def l2norm(x, eps=1e-12):
            n = jnp.sqrt(jnp.sum(x * x, axis=-1, keepdims=True))
            return x / jnp.maximum(n, eps)

        def dplr_delta_rule(q, k, v, a, gk):
            qm, km, vm, am, gm = (jnp.moveaxis(t, 1, 0) for t in (q, k, v, a, gk))

            def step(S, inp):
                qt, kt, vt, at, gkt = inp
                Sp = S * jnp.exp(gkt)[..., None]
                u = jnp.einsum('bhk,bhkv->bhv', at, Sp) + vt
                S = Sp + jnp.einsum('bhk,bhv->bhkv', kt, u)
                o = jnp.einsum('bhk,bhkv->bhv', qt, S)
                return (S, o)
            S0 = jnp.zeros((q.shape[0], q.shape[2], q.shape[3], v.shape[3]), q.dtype)
            _, o = jax.lax.scan(step, S0, (qm, km, vm, am, gm))
            return jnp.moveaxis(o, 0, 1)

        def _forward(x, Wq, Wk, Wv, Wgamma, Wf, Wg1, Wg2, Wo, norm_w):
            b, n, d = x.shape
            silu = jax.nn.silu
            q = silu(x @ Wq)
            k = silu(x @ Wk)
            v = silu(x @ Wv)
            log_f = jax.nn.log_sigmoid(x @ Wf)
            gamma = -jax.nn.sigmoid(x @ Wgamma)
            q = q.reshape(b, n, H, HD)
            k = l2norm(k.reshape(b, n, H, HD))
            v = v.reshape(b, n, H, HD)
            gk = jnp.broadcast_to(log_f[..., None], (b, n, H, HD))
            a = k * gamma[..., None] * jnp.exp(gk)
            out = dplr_delta_rule(q, k, v, a, gk)
            out = out.reshape(b, n, d)
            gate = jax.nn.sigmoid(x @ Wg1 @ Wg2)
            out = out * gate
            mu = jnp.mean(out, axis=-1, keepdims=True)
            var = jnp.mean(jnp.square(out - mu), axis=-1, keepdims=True)
            out = (out - mu) * jax.lax.rsqrt(var + 1e-05) * norm_w
            return out @ Wo
        return _forward(x, Wq, Wk, Wv, Wgamma, Wf, Wg1, Wg2, Wo, norm_w)

    def _L1_ffn_ref(x, W1, b1, W2, b2):
        import jax, jax.numpy as jnp
        import numpy as np
        EMB = 256
        FF = 4 * EMB

        def _ternary(w):
            scale = jnp.maximum(jnp.mean(jnp.abs(w)), 1e-08)
            w_t = jnp.clip(jnp.round(w / scale), -1.0, 1.0)
            return w + jax.lax.stop_gradient(w_t - w)
        h = jnp.einsum('bsd,fd->bsf', x, _ternary(W1)) + b1
        h = jax.nn.gelu(h, approximate=False)
        out = jnp.einsum('bsf,df->bsd', h, _ternary(W2)) + b2
        return out
    h = _L0_tok_ref(x, L0_tok_W, L0_tok_b, L0_tok_cls_token, L0_tok_pos_embedding)
    h = jnp.concatenate([jnp.broadcast_to(cls_tok, (h.shape[0], 1, h.shape[2])), h], axis=1)
    h = h + _L0_attn_ref(_layernorm(h, axis=-1), L0_attn_Wq, L0_attn_Wk, L0_attn_Wv, L0_attn_Wo)
    h = h + _L0_ffn_ref(_layernorm(h, axis=-1), L0_ffn_Wr, L0_ffn_br, L0_ffn_W1, L0_ffn_b1, L0_ffn_W2, L0_ffn_b2)
    h = h + _L1_attn_ref(_layernorm(h, axis=-1), L1_attn_Wq, L1_attn_Wk, L1_attn_Wv, L1_attn_Wgamma, L1_attn_Wf, L1_attn_Wg1, L1_attn_Wg2, L1_attn_Wo, L1_attn_norm_w)
    h = h + _L1_ffn_ref(_layernorm(h, axis=-1), L1_ffn_W1, L1_ffn_b1, L1_ffn_W2, L1_ffn_b2)
    return h

_drawn_inputs = setup_inputs


def setup_inputs(seed=0):
    import zlib

    import numpy as np

    out = dict(_drawn_inputs(seed))
    spreads = {'L0_ffn_br': (0.0, 0.1),
     'L0_ffn_b1': (0.0, 0.321),
     'L0_ffn_b2': (0.0, 0.1),
     'L1_attn_norm_w': (1.0, 0.2)}
    factors = {'L1_attn_Wgamma': 52.548,
     'L1_attn_Wg1': 8.0,
     'L1_attn_Wg2': 8.0,
     'L1_ffn_b1': 22.643,
     'L1_ffn_b2': 64.0}
    for name, (base, spread) in spreads.items():
        noise = np.random.default_rng([zlib.crc32(name.encode()), seed]).standard_normal(out[name].shape)
        drawn = base * np.exp(spread * noise) if base else spread * noise
        out[name] = jnp.asarray(drawn.astype(out[name].dtype))
    for name, factor in factors.items():
        out[name] = (out[name] * factor).astype(out[name].dtype)
    return out
```

```python
from contextlib import ExitStack, contextmanager

import numpy as np

import concourse.bass as bass
from concourse import mybir

F32 = mybir.dt.float32
F32R = mybir.dt.float32r
BF16 = mybir.dt.bfloat16
ALU = mybir.AluOpType
ACT = mybir.ActivationFunctionType
AX = mybir.AxisListType

P = 128
IMAGES = 64
SEQ = 38
PATCHES = SEQ - 2
D = 256
HALVES = D // P
HEADS = 16
PAIRS = HEADS // 2
HPH = HEADS // HALVES
PPH = PAIRS // HALVES
HD = D // HEADS
PAD = 64
TOKENS = IMAGES * SEQ
TILES = TOKENS // P
CHUNKS = 8
CB = IMAGES // CHUNKS
CT = CB * SEQ
CP = CB * PATCHES
IP = CB // 2
KP = 768 // P
EXPERTS = 8
FF = 1024
FB = FF // P
MT = 4
EPS = 1e-5
MASKED = -1e30


@contextmanager
def stage(nc, *names):
    with ExitStack() as own:
        sems = [own.enter_context(nc.semaphore(n)) for n in names]
        with nc.Block() as block:
            yield (block, *sems)
        for s in sems:
            nc.gpsimd.sem_clear(s)
        nc.all_engine_barrier()


def spread(ap, axis, n):
    wide = ap.unsqueeze(axis)
    shape = list(wide.shape)
    shape[axis] = n
    return wide.broadcast_to(shape)


def split_products(hi_l, lo_l, hi_r, lo_r):
    return ((hi_l, hi_r), (hi_l, lo_r), (lo_l, hi_r))


def layer_norm_turn(nc, bank, RES, STD, MV, XN, XH, XL, ident, name):
    xh = XH[:, :, 0:TOKENS]
    xl = XL[:, :, 0:TOKENS]
    with stage(nc, name + "_var", name + "_std", name + "_inv", name + "_normed", name + "_turned",
               name + "_hi", name + "_lo") as (block, var_ready, std_ready, inv_ready, normed,
                                               turned, hi_ready, lo_ready):
        @block.vector
        def _(dve):
            nc.vector.tensor_scalar(STD[:, 0, :], MV[:, :, 1], EPS, None, ALU.add).then_inc(var_ready, 1)
            dve.wait_ge(std_ready, 1)
            nc.vector.reciprocal(STD[:, 2, :], STD[:, 1, :]).then_inc(inv_ready, 1)
            dve.wait_ge(inv_ready, 1)

            def low_part(t):
                dve.wait_ge(hi_ready, t + 1)
                nc.vector.tensor_tensor(
                    xl[:, :, t * P:(t + 1) * P], bank[t % 4][:, 0:D].rearrange("p (m t) -> p m t", m=HALVES),
                    xh[:, :, t * P:(t + 1) * P].bitcast(F32), ALU.subtract).then_inc(lo_ready, 1)

            for t in range(TILES):
                if t >= 4:
                    dve.wait_ge(turned, t - 3)
                nc.vector.tensor_scalar(XN[:, t % 4, :], RES[:, t, :], MV[:, t, 0:1], STD[:, 2, t:t + 1],
                                        ALU.subtract, ALU.mult).then_inc(normed, 1)
                if t >= 2:
                    low_part(t - 2)
            low_part(TILES - 2)
            low_part(TILES - 1)

        @block.scalar
        def _(act):
            act.wait_ge(var_ready, 1)
            nc.scalar.activation(STD[:, 1, :], STD[:, 0, :], ACT.Sqrt).then_inc(std_ready, 1)
            for t in range(TILES):
                act.wait_ge(turned, t + 1)
                nc.scalar.activation(xh[:, :, t * P:(t + 1) * P],
                                     bank[t % 4][:, 0:D].rearrange("p (m t) -> p m t", m=HALVES),
                                     ACT.Copy).then_inc(hi_ready, 1)

        @block.tensor
        def _(pe):
            for t in range(TILES):
                pe.wait_ge(normed, t + 1)
                if t >= 4:
                    pe.wait_ge(lo_ready, t - 3)
                for m in range(HALVES):
                    turn = nc.tensor.transpose(bank[t % 4][:, m * P:(m + 1) * P],
                                               XN[:, t % 4, m * P:(m + 1) * P], ident[:, :])
                turn.then_inc(turned, 1)


def split_weights(nc, name, pairs):
    with stage(nc, name + "_hi", name + "_lo") as (block, hi_ready, lo_ready):
        @block.scalar
        def _(act):
            for raw, hi, lo in pairs:
                nc.scalar.activation(hi, raw, ACT.Copy).then_inc(hi_ready, 1)

        @block.vector
        def _(dve):
            for n, (raw, hi, lo) in enumerate(pairs):
                dve.wait_ge(hi_ready, n + 1)
                nc.vector.tensor_tensor(lo, raw, hi.bitcast(F32), ALU.subtract).then_inc(lo_ready, 1)


def add_product_and_stats(nc, bank, RES, BN, MV, OH, OL, wh, wl, name):
    oh = OH[:, :, 0:TOKENS]
    ol = OL[:, :, 0:TOKENS]
    with stage(nc, name + "_product", name + "_sum", name + "_bn", name + "_mv") as (
            block, product, summed, bn_ready, mv_ready):
        @block.tensor
        def _(pe):
            for t in range(TILES):
                if t >= 4:
                    pe.wait_ge(summed, t - 3)
                passes = [x for k in range(HALVES) for x in split_products(
                    oh[:, k, t * P:(t + 1) * P], ol[:, k, t * P:(t + 1) * P], wh[:, k, :], wl[:, k, :])]
                for n, (left, right) in enumerate(passes):
                    mm = nc.tensor.matmul(bank[t % 4][:, 0:D], left, right,
                                          start=(n == 0), stop=(n == len(passes) - 1))
                mm.then_inc(product, 1)

        @block.vector
        def _(dve):
            for t in range(TILES + 2):
                if t < TILES:
                    dve.wait_ge(product, t + 1)
                    nc.vector.tensor_tensor(RES[:, t, :], RES[:, t, :], bank[t % 4][:, 0:D],
                                            ALU.add).then_inc(summed, 1)
                if 1 <= t <= TILES:
                    dve.wait_ge(summed, t)
                    nc.vector.bn_stats(BN[:, t - 1, :], RES[:, t - 1, :]).then_inc(bn_ready, 1)
                if t >= 2:
                    dve.wait_ge(bn_ready, t - 1)
                    nc.vector.bn_aggr(MV[:, t - 2, :], BN[:, t - 2, :]).then_inc(mv_ready, 1)




def build_tower(nc, ins, out, stop=None):
    with ExitStack() as whole:
        def sb(ctx, name, shape, dt=F32):
            return ctx.enter_context(nc.sbuf_tensor(name, shape, dt))

        bank = [whole.enter_context(nc.psum_tensor(f"bank{i}", [P, 512], F32)) for i in range(8)]
        RES = sb(whole, "residual", [P, TILES, D])
        XH = sb(whole, "x_hi", [P, HALVES, TOKENS], F32R)
        XL = sb(whole, "x_lo", [P, HALVES, TOKENS], F32R)
        BN = sb(whole, "bn", [P, TILES, 6])
        MV = sb(whole, "mean_var", [P, TILES, 2])
        STD = sb(whole, "std", [P, 3, TILES])
        XN = sb(whole, "normed_tiles", [P, 4, D])
        ident = sb(whole, "ident", [P, P])
        identb = sb(whole, "ident_bf16", [P, P], BF16)
        hmask = sb(whole, "head_mask", [P, HPH])
        xh_c = XH[:, :, :].rearrange("p m (c t) -> p m c t", c=CHUNKS)
        xl_c = XL[:, :, :].rearrange("p m (c t) -> p m c t", c=CHUNKS)

        tokens_stage(nc, sb, bank, ins, RES, BN, MV, ident, identb, hmask)
        if stop == 0:
            return dump(nc, out, RES)
        layer_norm_turn(nc, bank, RES, STD, MV, XN, XH, XL, ident, "ln0")
        softmax_attention(nc, sb, bank, ins, RES, BN, MV, XH, XL, xh_c, xl_c, ident, identb, hmask)
        if stop == 1:
            return dump(nc, out, RES)
        layer_norm_turn(nc, bank, RES, STD, MV, XN, XH, XL, ident, "ln1")
        mixture(nc, sb, bank, ins, RES, BN, MV, XH, XL, ident)
        tile_stats(nc, RES, BN, MV, "moe")
        if stop == 2:
            return dump(nc, out, RES)
        layer_norm_turn(nc, bank, RES, STD, MV, XN, XH, XL, ident, "ln2")
        delta_attention(nc, sb, bank, ins, RES, BN, MV, STD, XN, XH, XL, xh_c, xl_c, ident, identb, hmask)
        if stop == 3:
            return dump(nc, out, RES)
        layer_norm_turn(nc, bank, RES, STD, MV, XN, XH, XL, ident, "ln3")
        ternary_ffn(nc, sb, bank, ins, RES, XH, XL, out)


def dump(nc, out, RES):
    with stage(nc, "stored") as (block, stored):
        @block.sync
        def _(sp):
            sp.dma_start(out.rearrange("(t p) d -> p t d", p=P), RES[:, :, :]).then_inc(stored, 16)
            sp.wait_ge(stored, 16)


def tokens_stage(nc, sb, bank, ins, RES, BN, MV, ident, identb, hmask):
    with ExitStack() as ctx:
        x = sb(ctx, "patches", [P, CHUNKS, KP, CP])
        w = sb(ctx, "tok_w", [P, KP, D])
        wh = sb(ctx, "tok_wh", [P, KP, D], F32R)
        wl = sb(ctx, "tok_wl", [P, KP, D], F32R)
        xh = sb(ctx, "patch_hi", [P, KP, CP], F32R)
        xl = sb(ctx, "patch_lo", [P, KP, CP], F32R)
        table = sb(ctx, "tok_bias", [P, HALVES, SEQ])
        pos = sb(ctx, "tok_pos", [P, HALVES, SEQ - 1])
        ET = sb(ctx, "tokens_t", [P, HALVES, CHUNKS, CB, SEQ])

        with stage(nc, "loaded", "table_ready") as (block, loaded, table_ready):
            @block.sync
            def _(sp):
                for dst, src in ((w, "tok_w"), (table, "tok_bias"), (pos, "tok_pos"), (ident, "ident"),
                                 (identb, "ident_bf16"), (hmask, "head_mask")):
                    sp.dma_start(dst[:], ins[src]).then_inc(loaded, 16)
                for c in range(0, CHUNKS, 2):
                    sp.dma_start(x[:, c], ins["patches"][c]).then_inc(loaded, 16)

            @block.scalar
            def _(act):
                for c in range(1, CHUNKS, 2):
                    act.dma_start(x[:, c], ins["patches"][c]).then_inc(loaded, 16)

            @block.vector
            def _(dve):
                dve.wait_ge(loaded, 16 * (6 + CHUNKS))
                nc.vector.tensor_tensor(table[:, :, 1:SEQ], table[:, :, 1:SEQ], pos[:, :, :],
                                        ALU.add).then_inc(table_ready, 1)
                dve.wait_ge(table_ready, 1)
                for m in range(HALVES):
                    nc.vector.tensor_copy(
                        ET[:, m].rearrange("p c b s -> p (c b) s")[:, :, 0:2],
                        spread(table[:, m, 0:2], 1, IMAGES)).then_inc(table_ready, 1)
        split_weights(nc, "tokw", [(w[:], wh[:], wl[:])])

        with nc.Fori(0, CHUNKS) as c:
            with stage(nc, "patch_hi", "patch_lo", "tok_product", "tok_done") as (
                    block, hi_ready, lo_ready, product, done):
                @block.scalar
                def _(act):
                    for k in range(KP):
                        nc.scalar.activation(xh[:, k, :], x[:, c, k, :], ACT.Copy).then_inc(hi_ready, 1)

                @block.vector
                def _(dve):
                    for k in range(KP):
                        dve.wait_ge(hi_ready, k + 1)
                        nc.vector.tensor_tensor(xl[:, k, :], x[:, c, k, :], xh[:, k, :].bitcast(F32),
                                                ALU.subtract).then_inc(lo_ready, 1)
                    for m in range(HALVES):
                        dve.wait_ge(product, m + 1)
                        nc.vector.tensor_tensor(
                            ET[:, m, c, :, 2:SEQ], bank[m][:, 0:CP].rearrange("p (b s) -> p b s", b=CB),
                            spread(table[:, m, 2:SEQ], 1, CB), ALU.add).then_inc(done, 1)

                @block.tensor
                def _(pe):
                    for k in range(KP):
                        pe.wait_ge(lo_ready, k + 1)
                        for m in range(HALVES):
                            for n, (left, right) in enumerate(split_products(
                                    wh[:, k, m * P:(m + 1) * P], wl[:, k, m * P:(m + 1) * P],
                                    xh[:, k, :], xl[:, k, :])):
                                mm = nc.tensor.matmul(bank[m][:, 0:CP], left, right,
                                                      start=(k == 0 and n == 0), stop=(k == KP - 1 and n == 2))
                            if k == KP - 1:
                                mm.then_inc(product, 1)

        et = [ET[:, m].rearrange("p c b s -> p (c b s)") for m in range(HALVES)]
        with stage(nc, "tok_turned", "tok_res", "tok_bn", "tok_mv") as (
                block, turned, res_ready, bn_ready, mv_ready):
            @block.tensor
            def _(pe):
                for t in range(TILES):
                    if t >= 4:
                        pe.wait_ge(res_ready, t - 3)
                    for m in range(HALVES):
                        turn = nc.tensor.transpose(bank[t % 4][:, m * P:(m + 1) * P],
                                                   et[m][:, t * P:(t + 1) * P], ident[:, :])
                    turn.then_inc(turned, 1)

            @block.scalar
            def _(act):
                for t in range(TILES):
                    act.wait_ge(turned, t + 1)
                    nc.scalar.activation(RES[:, t, :], bank[t % 4][:, 0:D], ACT.Copy).then_inc(res_ready, 1)

            @block.vector
            def _(dve):
                for t in range(TILES + 1):
                    if t < TILES:
                        dve.wait_ge(res_ready, t + 1)
                        nc.vector.bn_stats(BN[:, t, :], RES[:, t, :]).then_inc(bn_ready, 1)
                    if t >= 1:
                        dve.wait_ge(bn_ready, t)
                        nc.vector.bn_aggr(MV[:, t - 1, :], BN[:, t - 1, :]).then_inc(mv_ready, 1)


def softmax_attention(nc, sb, bank, ins, RES, BN, MV, XH, XL, xh_c, xl_c, ident, identb, hmask):
    Q, QS, K, KS, V = range(5)
    with ExitStack() as ctx:
        w = sb(ctx, "att_w", [P, 6, HALVES, D])
        wh = sb(ctx, "att_wh", [P, 6, HALVES, D], F32R)
        wl = sb(ctx, "att_wl", [P, 6, HALVES, D], F32R)
        cos = sb(ctx, "cos", [P, SEQ])
        sin = sb(ctx, "sin", [P, SEQ])
        causal = sb(ctx, "causal", [P, SEQ], BF16)
        SH = sb(ctx, "chunk_hi", [P, HALVES, CB, PAD], F32R)
        SL = sb(ctx, "chunk_lo", [P, HALVES, CB, PAD], F32R)
        RC = sb(ctx, "rope_cos", [P, 2, CB, SEQ])
        RS = sb(ctx, "rope_sin", [P, 2, CB, SEQ])
        QT = sb(ctx, "q_t", [P, HALVES, CB, PAD])
        KT = sb(ctx, "k_t", [P, HALVES, CB, SEQ])
        KX = sb(ctx, "k_by_head", [P, HALVES, CB, HPH, SEQ])
        VB = sb(ctx, "v_pairs", [P, CB, PAIRS, 2 * HD])
        PR = sb(ctx, "probs", [P, 2, HEADS, PAD])
        PT = sb(ctx, "probs_t", [P, PAIRS, P])
        MX = sb(ctx, "row_max", [P, 2, HEADS])
        SM = sb(ctx, "row_sum", [P, 2, HEADS])
        RI = sb(ctx, "row_inv", [P, 2, HEADS])

        with stage(nc, "att_loaded", "att_zero") as (block, loaded, zeroed):
            @block.sync
            def _(sp):
                for dst, src in ((w, "att_w"), (cos, "cos"), (sin, "sin"), (causal, "causal")):
                    sp.dma_start(dst[:], ins[src]).then_inc(loaded, 16)
                sp.wait_ge(loaded, 64)

            @block.gpsimd
            def _(pool):
                for t in (SH[:].bitcast(F32), SL[:].bitcast(F32), QT[:], VB[:], PR[:]):
                    nc.gpsimd.memset(t, 0.0).then_inc(zeroed, 1)
        split_weights(nc, "attw", [(w[:, n], wh[:, n], wl[:, n]) for n in range(6)])

        def half(s):
            return slice(s * PAD, (s + 1) * PAD)

        with nc.Fori(0, CHUNKS) as c:
            with stage(nc, "in_hi", "in_lo", "proj", "roped_c", "roped_s", "roped", "k_wide_v", "k_wide_a",
                       "v_proj", "v_out", "scores", "maxed", "shifted", "exped", "summed", "inverted",
                       "normed", "p_turned", "p_out", "out_t", "out_hi", "out_lo") as (
                    block, in_hi, in_lo, proj, roped_c, roped_s, roped, k_wide_v, k_wide_a,
                    v_proj, v_out, scores, maxed, shifted, exped, summed, inverted,
                    normed, p_turned, p_out, out_t, out_hi, out_lo):

                @block.tensor
                def _(pe):
                    pe.wait_ge(in_hi, HALVES)
                    pe.wait_ge(in_lo, HALVES)
                    for n, (tensor, m) in enumerate(((Q, 0), (QS, 0), (K, 0), (KS, 0),
                                                     (Q, 1), (QS, 1), (K, 1), (KS, 1))):
                        if n >= 4:
                            pe.wait_ge(roped_c if n % 2 == 0 else roped_s, (n - 4) // 2 + 1)
                        passes = [x for k in range(HALVES) for x in split_products(
                            wh[:, tensor, k, m * P:(m + 1) * P], wl[:, tensor, k, m * P:(m + 1) * P],
                            SH[:, k, :, 0:SEQ], SL[:, k, :, 0:SEQ])]
                        for i, (left, right) in enumerate(passes):
                            mm = nc.tensor.matmul(bank[n % 4][:, 0:CT], left, right,
                                                  start=(i == 0), stop=(i == len(passes) - 1))
                        mm.then_inc(proj, 1)
                    for p in range(IP):
                        if p >= 2:
                            pe.wait_ge(v_out, 4 * (p - 1))
                        passes = [x for k in range(HALVES) for x in split_products(
                            SH[:, k, 2 * p:2 * p + 2, :].rearrange("p b s -> p (b s)"),
                            SL[:, k, 2 * p:2 * p + 2, :].rearrange("p b s -> p (b s)"),
                            wh[:, V, k, :], wl[:, V, k, :])]
                        for i, (left, right) in enumerate(passes):
                            mm = nc.tensor.matmul(bank[4 + p % 2][:, 0:D], left, right,
                                                  start=(i == 0), stop=(i == len(passes) - 1))
                        mm.then_inc(v_proj, 1)

                    def score(p):
                        for m in range(HALVES):
                            b = bank[2 * (p % 2) + m]
                            if p == 0:
                                pe.wait_ge(k_wide_v if m == 0 else k_wide_a, HPH)
                                pe.wait_ge(roped_c, 4)
                                pe.wait_ge(roped_s, 4)
                                pe.wait_ge(roped, 4)
                            if p >= 2:
                                pe.wait_ge(shifted, HALVES * (p - 2) + m + 1)
                            nc.tensor.matmul(b[:, 0:CT], identb[:, :], spread(causal[:, :], 1, HPH),
                                             start=True, stop=True)
                            for s in range(2):
                                mm = nc.tensor.matmul(b[half(s), 0:CT], QT[:, m, 2 * p + s, :],
                                                      KX[:, m, 2 * p + s].rearrange("p h s -> p (h s)"),
                                                      start=False, stop=True, skip_group_check=True)
                            mm.then_inc(scores, 1)

                    def turn(p):
                        pe.wait_ge(normed, p + 1)
                        if p == 0:
                            pe.wait_ge(v_out, 4 * IP)
                        else:
                            pe.wait_ge(p_out, 2 * p)
                        for g in range(PAIRS):
                            mm = nc.tensor.transpose(
                                bank[4 + g // 4][:, (g % 4) * P:(g % 4 + 1) * P],
                                PR[:, p % 2, 2 * g:2 * g + 2, :].rearrange("p h k -> p (h k)"), ident[:, :])
                            if g % 4 == 3:
                                mm.then_inc(p_turned, 1)

                    def attend(p):
                        pe.wait_ge(p_out, 2 * p + 2)
                        if p >= 2:
                            pe.wait_ge(out_lo, p - 1)
                        for s in range(2):
                            for m in range(HALVES):
                                for g in range(PPH):
                                    mm = nc.tensor.matmul(
                                        bank[6 + p % 2][32 * g:32 * g + 32, (2 * m + s) * SEQ:(2 * m + s + 1) * SEQ],
                                        VB[:, 2 * p + s, PPH * m + g, :], PT[:, PPH * m + g, s * PAD:s * PAD + SEQ],
                                        start=True, stop=True)
                        mm.then_inc(out_t, 1)

                    score(0)
                    for p in range(IP):
                        if p + 1 < IP:
                            score(p + 1)
                        turn(p)
                        attend(p)

                @block.vector
                def _(dve):
                    for m in range(HALVES):
                        nc.vector.tensor_copy(SL[:, m, :, 0:SEQ],
                                              xl_c[:, m, c, :].bitcast(F32).rearrange("p (b s) -> p b s", b=CB)
                                              ).then_inc(in_lo, 1)
                    for r in range(4):
                        if r >= 2:
                            dve.wait_ge(roped, r - 1)
                        dve.wait_ge(proj, 2 * r + 1)
                        nc.vector.tensor_tensor(RC[:, r % 2], bank[2 * (r % 2)][:, 0:CT].rearrange(
                            "p (b s) -> p b s", b=CB), spread(cos[:, :], 1, CB), ALU.mult).then_inc(roped_c, 1)
                        dve.wait_ge(proj, 2 * r + 2)
                        nc.vector.tensor_tensor(RS[:, r % 2], bank[2 * (r % 2) + 1][:, 0:CT].rearrange(
                            "p (b s) -> p b s", b=CB), spread(sin[:, :], 1, CB), ALU.mult).then_inc(roped_s, 1)
                    dve.wait_ge(roped, 2)
                    for h in range(HPH):
                        nc.vector.tensor_scalar(KX[:, 0, :, h, :], KT[:, 0], hmask[:, h:h + 1], None,
                                                ALU.mult).then_inc(k_wide_v, 1)
                    for p in range(IP):
                        for m in range(HALVES):
                            s3 = bank[2 * (p % 2) + m][:, 0:CT].rearrange("p (h k) -> p h k", h=HPH)
                            hs = slice(HPH * m, HPH * (m + 1))
                            dve.wait_ge(scores, HALVES * p + m + 1)
                            nc.vector.tensor_reduce(MX[:, p % 2, hs], s3, AX.X, ALU.max).then_inc(maxed, 1)
                            dve.wait_ge(maxed, HALVES * p + m + 1)
                            if p >= 2:
                                dve.wait_ge(p_turned, HALVES * (p - 1))
                            nc.vector.tensor_tensor(PR[:, p % 2, hs, 0:SEQ], s3,
                                                    spread(MX[:, p % 2, hs], 2, SEQ),
                                                    ALU.subtract).then_inc(shifted, 1)
                        dve.wait_ge(exped, p + 1)
                        nc.vector.tensor_reduce(SM[:, p % 2, :], PR[:, p % 2, :, 0:SEQ], AX.X,
                                                ALU.add).then_inc(summed, 1)
                        dve.wait_ge(summed, p + 1)
                        nc.vector.reciprocal(RI[:, p % 2, :], SM[:, p % 2, :]).then_inc(inverted, 1)
                        if p >= 1:
                            low_out(nc, dve, p - 1, out_hi, out_lo, bank, xh_c, xl_c, c)
                    low_out(nc, dve, IP - 1, out_hi, out_lo, bank, xh_c, xl_c, c)

                @block.scalar
                def _(act):
                    for m in range(HALVES):
                        nc.scalar.activation(SH[:, m, :, 0:SEQ],
                                             xh_c[:, m, c, :].bitcast(F32).rearrange("p (b s) -> p b s", b=CB),
                                             ACT.Copy).then_inc(in_hi, 1)
                    for p in range(IP):
                        act.wait_ge(v_proj, p + 1)
                        for s in range(2):
                            v4 = bank[4 + p % 2][half(s), 0:D].rearrange("p (g e d) -> p g e d", e=2, d=HD)
                            for e in range(2):
                                nc.scalar.activation(VB[half(e), 2 * p + s, :, e * HD:(e + 1) * HD],
                                                     v4[:, :, e, :], ACT.Copy).then_inc(v_out, 1)
                    act.wait_ge(roped, 4)
                    for h in range(HPH):
                        nc.scalar.activation(KX[:, 1, :, h, :], KT[:, 1], ACT.Copy,
                                             scale=hmask[:, h:h + 1]).then_inc(k_wide_a, 1)
                    for p in range(IP):
                        act.wait_ge(shifted, HALVES * (p + 1))
                        nc.scalar.activation(PR[:, p % 2, :, 0:SEQ], PR[:, p % 2, :, 0:SEQ], ACT.Exp,
                                             scale=HD ** -0.5).then_inc(exped, 1)
                        for q in range(2):
                            act.wait_ge(p_turned, 2 * p + q + 1)
                            if p >= 1:
                                act.wait_ge(out_t, p)
                            nc.scalar.activation(PT[:, 4 * q:4 * q + 4, :],
                                                 bank[4 + q][:, :].rearrange("p (g t) -> p g t", g=4),
                                                 ACT.Copy).then_inc(p_out, 1)
                        act.wait_ge(out_t, p + 1)
                        nc.scalar.activation(xh_c[:, :, c, 2 * p * SEQ:2 * (p + 1) * SEQ],
                                             bank[6 + p % 2][:, 0:4 * SEQ].rearrange("p (m t) -> p m t", m=HALVES),
                                             ACT.Copy).then_inc(out_hi, 1)

                @block.gpsimd
                def _(pool):
                    for r in range(4):
                        m = r // 2
                        dst = QT[:, m, :, 0:SEQ] if r % 2 == 0 else KT[:, m]
                        pool.wait_ge(roped_c, r + 1)
                        pool.wait_ge(roped_s, r + 1)
                        nc.gpsimd.tensor_tensor(dst, RC[:, r % 2], RS[:, r % 2], ALU.add).then_inc(roped, 1)
                    for p in range(IP):
                        pool.wait_ge(inverted, p + 1)
                        nc.gpsimd.tensor_tensor(PR[:, p % 2, :, 0:SEQ], PR[:, p % 2, :, 0:SEQ],
                                                spread(RI[:, p % 2, :], 2, SEQ), ALU.mult).then_inc(normed, 1)
        add_product_and_stats(nc, bank, RES, BN, MV, XH, XL, wh[:, 5], wl[:, 5], "att_o")


def low_out(nc, dve, p, out_hi, out_lo, bank, xh_c, xl_c, c):
    dve.wait_ge(out_hi, p + 1)
    ts = slice(2 * p * SEQ, 2 * (p + 1) * SEQ)
    nc.vector.tensor_tensor(xl_c[:, :, c, ts],
                            bank[6 + p % 2][:, 0:4 * SEQ].rearrange("p (m t) -> p m t", m=HALVES),
                            xh_c[:, :, c, ts].bitcast(F32), ALU.subtract).then_inc(out_lo, 1)


def mixture(nc, sb, bank, ins, RES, BN, MV, XH, XL, ident):
    with ExitStack() as ctx:
        G = sb(ctx, "gates", [P, TILES, EXPERTS])
        b1 = sb(ctx, "moe_b1", [P, EXPERTS, FB])
        w1 = sb(ctx, "moe_w1", [P, HALVES, FF])
        w2 = sb(ctx, "moe_w2", [P, FB, D])
        router(nc, sb, bank, ins, RES, G, XH, XL, ident, b1, w1, w2)
        w1h = sb(ctx, "moe_w1h", [P, HALVES, FF], F32R)
        w1l = sb(ctx, "moe_w1l", [P, HALVES, FF], F32R)
        w2h = sb(ctx, "moe_w2h", [P, FB, D], F32R)
        w2l = sb(ctx, "moe_w2l", [P, FB, D], F32R)
        H = sb(ctx, "hidden", [P, 4, MT * P])
        HH = sb(ctx, "hidden_hi", [P, 2, FB, MT * P], F32R)
        HL = sb(ctx, "hidden_lo", [P, 2, FB, MT * P], F32R)
        steps = [range(t, min(t + MT, TILES)) for t in range(0, TILES, MT)]
        cut = FF // 4

        with nc.Fori(0, EXPERTS) as e:
            with stage(nc, "w_next", "w1_hi", "w1_lo", "w2_hi", "w2_lo", "up", "act", "h_hi", "h_lo",
                       "down", "gated") as (block, w_next, w1_hi, w1_lo, w2_hi, w2_lo, up, acted, h_hi, h_lo,
                                            down, gated):
                @block.sync
                def _(sp):
                    following = (e + 1) % EXPERTS
                    sp.wait_ge(w1_lo, 4)
                    sp.dma_start(w1[:], ins["moe_w1"][following]).then_inc(w_next, 16)
                    sp.wait_ge(w2_lo, 4)
                    sp.dma_start(w2[:], ins["moe_w2"][following]).then_inc(w_next, 16)
                    sp.wait_ge(w_next, 32)

                @block.tensor
                def _(pe):
                    def hidden(c):
                        n = len(steps[c]) * P
                        ts = slice(steps[c][0] * P, steps[c][0] * P + n)
                        for f in range(FB):
                            i = FB * c + f
                            if c == 0 and f % 2 == 0:
                                pe.wait_ge(w1_lo, f // 2 + 1)
                            if i >= 4:
                                pe.wait_ge(acted, i - 3)
                            passes = [x for k in range(HALVES) for x in split_products(
                                w1h[:, k, f * P:(f + 1) * P], w1l[:, k, f * P:(f + 1) * P],
                                XH[:, k, ts], XL[:, k, ts])]
                            for j, (left, right) in enumerate(passes):
                                mm = nc.tensor.matmul(bank[i % 4][:, 0:n], left, right,
                                                      start=(j == 0), stop=(j == len(passes) - 1))
                            mm.then_inc(up, 1)

                    def output(c):
                        pe.wait_ge(h_lo, FB * (c + 1))
                        if c == 0:
                            pe.wait_ge(w2_lo, 4)
                        for j, t in enumerate(steps[c]):
                            if t >= 4:
                                pe.wait_ge(gated, t - 3)
                            js = slice(j * P, (j + 1) * P)
                            passes = [x for f in range(FB) for x in split_products(
                                HH[:, c % 2, f, js], HL[:, c % 2, f, js], w2h[:, f, :], w2l[:, f, :])]
                            for n, (left, right) in enumerate(passes):
                                mm = nc.tensor.matmul(bank[4 + t % 4][:, 0:D], left, right,
                                                      start=(n == 0), stop=(n == len(passes) - 1))
                            mm.then_inc(down, 1)

                    hidden(0)
                    for c in range(len(steps)):
                        if c + 1 < len(steps):
                            hidden(c + 1)
                        output(c)

                @block.scalar
                def _(act):
                    for q in range(4):
                        nc.scalar.activation(w1h[:, :, q * cut:(q + 1) * cut], w1[:, :, q * cut:(q + 1) * cut],
                                             ACT.Copy).then_inc(w1_hi, 1)
                    for q in range(4):
                        nc.scalar.activation(w2h[:, 2 * q:2 * q + 2, :], w2[:, 2 * q:2 * q + 2, :],
                                             ACT.Copy).then_inc(w2_hi, 1)
                    for c, step in enumerate(steps):
                        n = len(step) * P
                        for f in range(FB):
                            i = FB * c + f
                            act.wait_ge(up, i + 1)
                            if i >= 4:
                                act.wait_ge(h_lo, i - 3)
                            nc.scalar.activation(H[:, i % 4, 0:n], bank[i % 4][:, 0:n], ACT.Relu,
                                                 bias=b1[:, e, f:f + 1]).then_inc(acted, 1)

                @block.vector
                def _(dve):
                    def gate(c):
                        for t in steps[c]:
                            dve.wait_ge(down, t + 1)
                            nc.vector.scalar_tensor_tensor(
                                out=RES[:, t, :], in0=bank[4 + t % 4][:, 0:D], scalar=G[:, t, bass.ds(e, 1)],
                                in1=RES[:, t, :], op0=ALU.mult, op1=ALU.add).then_inc(gated, 1)

                    for q in range(4):
                        dve.wait_ge(w1_hi, q + 1)
                        qs = slice(q * cut, (q + 1) * cut)
                        nc.vector.tensor_tensor(w1l[:, :, qs], w1[:, :, qs], w1h[:, :, qs].bitcast(F32),
                                                ALU.subtract).then_inc(w1_lo, 1)
                    for q in range(4):
                        dve.wait_ge(w2_hi, q + 1)
                        qs = slice(2 * q, 2 * q + 2)
                        nc.vector.tensor_tensor(w2l[:, qs, :], w2[:, qs, :], w2h[:, qs, :].bitcast(F32),
                                                ALU.subtract).then_inc(w2_lo, 1)
                    for c, step in enumerate(steps):
                        n = len(step) * P
                        if c >= 2:
                            dve.wait_ge(down, steps[c - 2][-1] + 1)
                        for f in range(FB):
                            i = FB * c + f
                            dve.wait_ge(acted, i + 1)
                            nc.vector.tensor_copy(HH[:, c % 2, f, 0:n], H[:, i % 4, 0:n]).then_inc(h_hi, 1)
                            dve.wait_ge(h_hi, i + 1)
                            nc.vector.tensor_tensor(HL[:, c % 2, f, 0:n], H[:, i % 4, 0:n],
                                                    HH[:, c % 2, f, 0:n].bitcast(F32),
                                                    ALU.subtract).then_inc(h_lo, 1)
                        if c >= 1:
                            gate(c - 1)
                    gate(len(steps) - 1)


def router(nc, sb, bank, ins, RES, G, XH, XL, ident, b1, w1, w2):
    with ExitStack() as ctx:
        wr = sb(ctx, "wr", [P, HALVES, EXPERTS])
        wrh = sb(ctx, "wr_hi", [P, HALVES, EXPERTS], F32R)
        wrl = sb(ctx, "wr_lo", [P, HALVES, EXPERTS], F32R)
        br = sb(ctx, "br", [P, EXPERTS])
        b2 = sb(ctx, "moe_b2", [EXPERTS, D])
        ties = sb(ctx, "ties", [P, EXPERTS, EXPERTS])
        GT = sb(ctx, "gates_t", [EXPERTS, TILES, P])
        PB = sb(ctx, "router_probs", [P, TILES, EXPERTS])
        ST = sb(ctx, "router_stat", [P, 4, TILES])
        CUM = sb(ctx, "cumulated", [P, 2, TILES, EXPERTS])
        AH = sb(ctx, "ahead", [P, TILES, EXPERTS, EXPERTS])
        EQ = sb(ctx, "equal", [P, TILES, EXPERTS, EXPERTS])
        with stage(nc, "r_loaded", "r_w_next") as (block, loaded, w_next):
            @block.sync
            def _(sp):
                for dst, src in ((wr, "wr"), (br, "br"), (b2, "moe_b2"), (b1, "moe_b1")):
                    sp.dma_start(dst[:], ins[src]).then_inc(loaded, 16)
                sp.dma_start(ties[:].rearrange("p e j -> p (e j)"), ins["ties"]).then_inc(loaded, 16)
                sp.dma_start(w1[:], ins["moe_w1"][0]).then_inc(w_next, 16)
                sp.dma_start(w2[:], ins["moe_w2"][0]).then_inc(w_next, 16)
                sp.wait_ge(loaded, 80)
                sp.wait_ge(w_next, 32)
        split_weights(nc, "wr", [(wr[:], wrh[:], wrl[:])])

        with stage(nc, "logits", "r_step", "r_exp", "g_turned", "g_out", "b2_product", "b2_added") as (
                block, logits, step, exped, turned, g_out, product, added):
            @block.tensor
            def _(pe):
                def b2_term(t):
                    pe.wait_ge(g_out, t + 1)
                    if t >= 2:
                        pe.wait_ge(added, t - 1)
                    nc.tensor.matmul(bank[4 + t % 2][:, 0:D], GT[:, t, :], b2[:, :],
                                     start=True, stop=True).then_inc(product, 1)

                for t in range(TILES):
                    passes = [x for k in range(HALVES) for x in split_products(
                        XH[:, k, t * P:(t + 1) * P], XL[:, k, t * P:(t + 1) * P], wrh[:, k, :], wrl[:, k, :])]
                    for n, (left, right) in enumerate(passes):
                        mm = nc.tensor.matmul(bank[0][:, t * EXPERTS:(t + 1) * EXPERTS], left, right,
                                              start=(n == 0), stop=(n == len(passes) - 1))
                mm.then_inc(logits, 1)
                pe.wait_ge(step, 16)
                for t in range(TILES):
                    if t >= 2:
                        pe.wait_ge(g_out, t - 1)
                    nc.tensor.transpose(bank[1 + t % 2][0:EXPERTS, 0:P], G[:, t, :], ident[:, :]).then_inc(turned, 1)
                    if t >= 1:
                        b2_term(t - 1)
                b2_term(TILES - 1)

            @block.scalar
            def _(act):
                act.wait_ge(step, 3)
                nc.scalar.activation(PB[:], PB[:], ACT.Exp).then_inc(exped, 1)
                for t in range(TILES):
                    act.wait_ge(turned, t + 1)
                    nc.scalar.activation(GT[:, t, :], bank[1 + t % 2][0:EXPERTS, 0:P], ACT.Copy).then_inc(g_out, 1)

            @block.vector
            def _(dve):
                n = 0

                def then(ins):
                    nonlocal n
                    n += 1
                    ins.then_inc(step, 1)
                    dve.wait_ge(step, n)

                dve.wait_ge(logits, 1)
                then(nc.vector.tensor_tensor(PB[:], bank[0][:, 0:TILES * EXPERTS].rearrange(
                    "p (t e) -> p t e", e=EXPERTS), spread(br[:, :], 1, TILES), ALU.add))
                then(nc.vector.tensor_reduce(ST[:, 0, :], PB[:], AX.X, ALU.max))
                then(nc.vector.tensor_tensor(PB[:], PB[:], spread(ST[:, 0, :], 2, EXPERTS), ALU.subtract))
                dve.wait_ge(exped, 1)
                then(nc.vector.tensor_reduce(ST[:, 1, :], PB[:], AX.X, ALU.add))
                then(nc.vector.reciprocal(ST[:, 2, :], ST[:, 1, :]))
                then(nc.vector.tensor_tensor(PB[:], PB[:], spread(ST[:, 2, :], 2, EXPERTS), ALU.mult))
                other = spread(PB[:, :, :], 2, EXPERTS)
                own = spread(PB[:, :, :], 3, EXPERTS)
                then(nc.vector.tensor_tensor(EQ[:], other, own, ALU.is_equal))
                then(nc.vector.tensor_tensor(EQ[:], EQ[:], spread(ties[:, :, :], 1, TILES), ALU.mult))
                then(nc.vector.tensor_tensor(AH[:], other, own, ALU.is_gt))
                then(nc.vector.tensor_tensor(AH[:], AH[:], EQ[:], ALU.add))
                then(nc.vector.tensor_reduce(CUM[:, 0], AH[:], AX.X, ALU.add))
                then(nc.vector.tensor_scalar(CUM[:, 0], CUM[:, 0], 1.5, None, ALU.is_lt))
                then(nc.vector.tensor_tensor(AH[:], AH[:], other, ALU.mult))
                then(nc.vector.tensor_reduce(CUM[:, 1], AH[:], AX.X, ALU.add))
                then(nc.vector.scalar_tensor_tensor(out=CUM[:, 1].rearrange("p t e -> p (t e)"),
                                                    in0=CUM[:, 1].rearrange("p t e -> p (t e)"), scalar=0.8,
                                                    in1=CUM[:, 0].rearrange("p t e -> p (t e)"),
                                                    op0=ALU.is_lt, op1=ALU.max))
                then(nc.vector.tensor_tensor(G[:], PB[:], CUM[:, 1], ALU.mult))
                for t in range(TILES):
                    dve.wait_ge(product, t + 1)
                    nc.vector.tensor_tensor(RES[:, t, :], RES[:, t, :], bank[4 + t % 2][:, 0:D],
                                            ALU.add).then_inc(added, 1)


def tile_stats(nc, X, BN, MV, name):
    with stage(nc, name + "_bn", name + "_mv") as (block, bn_ready, mv_ready):
        @block.vector
        def _(dve):
            for t in range(TILES + 1):
                if t < TILES:
                    nc.vector.bn_stats(BN[:, t, :], X[:, t, :]).then_inc(bn_ready, 1)
                if t >= 1:
                    dve.wait_ge(bn_ready, t)
                    nc.vector.bn_aggr(MV[:, t - 1, :], BN[:, t - 1, :]).then_inc(mv_ready, 1)


QUARTER = IMAGES // 4
QC = QUARTER // CB


def delta_attention(nc, sb, bank, ins, RES, BN, MV, STD, XN, XH, XL, xh_c, xl_c, ident, identb, hmask):
    Q, K, GAMMA, F, V, O = range(6)
    with ExitStack() as ctx:
        wh = sb(ctx, "delta_wh", [P, 6, HALVES, D], F32R)
        wl = sb(ctx, "delta_wl", [P, 6, HALVES, D], F32R)
        wfh = sb(ctx, "delta_wfh", [P, HALVES, HEADS], F32R)
        wfl = sb(ctx, "delta_wfl", [P, HALVES, HEADS], F32R)
        wgh = sb(ctx, "delta_wgh", [P, HALVES, HD], F32R)
        wgl = sb(ctx, "delta_wgl", [P, HALVES, HD], F32R)
        wg2 = sb(ctx, "delta_wg2", [HD, D])
        identr = sb(ctx, "ident_r", [P, P], F32R)
        same = sb(ctx, "same_head", [P, P])
        after = sb(ctx, "after", [P, P])
        past = sb(ctx, "past", [P, SEQ], BF16)
        here = sb(ctx, "from_here", [P, SEQ])
        G1 = sb(ctx, "gate_low", [HD, TOKENS])
        delta_weights(nc, sb, ins, wh, wl, wfh, wfl, wgh, wgl, wg2, identr, same, after, past, here, ident)

        spans = [slice(t, min(t + 512, TOKENS)) for t in range(0, TOKENS, 512)]
        with stage(nc, "g1", "g1_out") as (block, g1_ready, g1_out):
            @block.tensor
            def _(pe):
                for i, ts in enumerate(spans):
                    if i >= 2:
                        pe.wait_ge(g1_out, i - 1)
                    passes = [x for k in range(HALVES) for x in split_products(
                        wgh[:, k, :], wgl[:, k, :], XH[:, k, ts], XL[:, k, ts])]
                    for n, (left, right) in enumerate(passes):
                        mm = nc.tensor.matmul(bank[i % 2][0:HD, 0:ts.stop - ts.start], left, right,
                                              start=(n == 0), stop=(n == len(passes) - 1))
                    mm.then_inc(g1_ready, 1)

            @block.scalar
            def _(act):
                for i, ts in enumerate(spans):
                    act.wait_ge(g1_ready, i + 1)
                    nc.scalar.activation(G1[:, ts], bank[i % 2][0:HD, 0:ts.stop - ts.start],
                                         ACT.Copy).then_inc(g1_out, 1)

        with ExitStack() as inner:
            PA = sb(inner, "qk_and_ak", [P, QUARTER, PAIRS, 2, SEQ])
            VH = sb(inner, "v_halves", [P, QUARTER, PAIRS, HD])
            with nc.Fori(0, 4) as quarter:
                delta_coefficients(nc, sb, bank, wh, wl, wfh, wfl, same, after, past, here, identb, hmask,
                                   xh_c, xl_c, PA, VH, quarter)
                delta_solve(nc, sb, bank, ident, PA, VH, XH, XL, quarter)

        Y = sb(ctx, "gated_out", [P, TILES, D])
        SG = sb(ctx, "gate", [P, 2, D])
        with stage(nc, "o_tile", "g_tile", "gate_ready", "y_ready", "y_bn", "y_mv") as (
                block, o_ready, g_ready, gate_ready, y_ready, bn_ready, mv_ready):
            @block.tensor
            def _(pe):
                for t in range(TILES):
                    ts = slice(t * P, (t + 1) * P)
                    if t >= 2:
                        pe.wait_ge(gate_ready, t - 1)
                    nc.tensor.matmul(bank[4 + t % 2][:, 0:D], G1[:, ts], wg2[:, :],
                                     start=True, stop=True).then_inc(g_ready, 1)
                    if t >= 2:
                        pe.wait_ge(y_ready, t - 1)
                    for m in range(HALVES):
                        nc.tensor.matmul(bank[t % 2][:, m * P:(m + 1) * P], XH[:, m, ts], identr[:, :],
                                         start=True, stop=False)
                        mm = nc.tensor.matmul(bank[t % 2][:, m * P:(m + 1) * P], XL[:, m, ts], identr[:, :],
                                              start=False, stop=True)
                    mm.then_inc(o_ready, 1)

            @block.scalar
            def _(act):
                for t in range(TILES):
                    act.wait_ge(g_ready, t + 1)
                    if t >= 2:
                        act.wait_ge(y_ready, t - 1)
                    nc.scalar.activation(SG[:, t % 2, :], bank[4 + t % 2][:, 0:D],
                                         ACT.Sigmoid).then_inc(gate_ready, 1)

            @block.vector
            def _(dve):
                for t in range(TILES + 2):
                    if t < TILES:
                        dve.wait_ge(o_ready, t + 1)
                        dve.wait_ge(gate_ready, t + 1)
                        nc.vector.tensor_tensor(Y[:, t, :], bank[t % 2][:, 0:D], SG[:, t % 2, :],
                                                ALU.mult).then_inc(y_ready, 1)
                    if 1 <= t <= TILES:
                        dve.wait_ge(y_ready, t)
                        nc.vector.bn_stats(BN[:, t - 1, :], Y[:, t - 1, :]).then_inc(bn_ready, 1)
                    if t >= 2:
                        dve.wait_ge(bn_ready, t - 1)
                        nc.vector.bn_aggr(MV[:, t - 2, :], BN[:, t - 2, :]).then_inc(mv_ready, 1)
        layer_norm_turn(nc, bank, Y, STD, MV, XN, XH, XL, ident, "lno")
        add_product_and_stats(nc, bank, RES, BN, MV, XH, XL, wh[:, O], wl[:, O], "delta_o")


def delta_weights(nc, sb, ins, wh, wl, wfh, wfl, wgh, wgl, wg2, identr, same, after, past, here, ident):
    with ExitStack() as ctx:
        w = sb(ctx, "delta_w", [P, 6, HALVES, D])
        wf = sb(ctx, "delta_wf", [P, HALVES, HEADS])
        wg = sb(ctx, "delta_wg1", [P, HALVES, HD])
        nw = sb(ctx, "norm_w", [P, HALVES])
        with stage(nc, "d_loaded", "scaled") as (block, loaded, scaled):
            @block.sync
            def _(sp):
                for dst, src in ((w, "delta_w"), (wf, "delta_wf"), (wg, "delta_wg1"), (wg2, "delta_wg2"),
                                 (nw, "norm_w"), (same, "same_head"), (after, "after"), (past, "past"),
                                 (here, "from_here")):
                    sp.dma_start(dst[:], ins[src]).then_inc(loaded, 16)

            @block.vector
            def _(dve):
                dve.wait_ge(loaded, 16 * 9)
                nc.vector.tensor_copy(identr[:, :], ident[:, :]).then_inc(scaled, 1)
                for m in range(HALVES):
                    nc.vector.tensor_scalar(w[:, 5, m, :], w[:, 5, m, :], nw[:, m:m + 1], None,
                                            ALU.mult).then_inc(scaled, 1)
        split_weights(nc, "dw", [(w[:, n], wh[:, n], wl[:, n]) for n in range(6)]
                      + [(wf[:], wfh[:], wfl[:]), (wg[:], wgh[:], wgl[:])])


def delta_coefficients(nc, sb, bank, wh, wl, wfh, wfl, same, after, past, here, identb, hmask,
                       xh_c, xl_c, PA, VH, quarter):
    Q, K, GAMMA, F, V, O = range(6)
    NR = 4
    with ExitStack() as ctx:
        SH = sb(ctx, "dchunk_hi", [P, HALVES, CB, PAD], F32R)
        SL = sb(ctx, "dchunk_lo", [P, HALVES, CB, PAD], F32R)
        QA = sb(ctx, "q_and_a", [P, HALVES, CB, 2, SEQ])
        KT = sb(ctx, "dk_t", [P, HALVES, CB, SEQ])
        KQ = sb(ctx, "k_square", [P, HALVES, CT])
        SQ = sb(ctx, "sig_qk", [P, HALVES, 2, CT])
        GM = sb(ctx, "sig_gamma", [P, HALVES, CT])
        FM = sb(ctx, "sig_f", [P, HALVES, CT])
        NK = sb(ctx, "k_norm", [P, HALVES, CT])
        KX = sb(ctx, "dk_by_head", [P, NR, PAIRS, 2, PAD])
        SV = sb(ctx, "sig_v", [P, 2, D])
        LZ = sb(ctx, "log_f", [P, 4, IP * HEADS])
        LF = sb(ctx, "log_f_pairs", [P, CB, PAIRS])
        MV = sb(ctx, "decay_steps", [P, 2, PAIRS, SEQ])
        DS = sb(ctx, "decay", [P, 2, PAIRS, SEQ])

        def half(s):
            return slice(s * PAD, (s + 1) * PAD)

        with stage(nc, "d_zero") as (block, zeroed):
            @block.gpsimd
            def _(pool):
                for t in (SH[:].bitcast(F32), SL[:].bitcast(F32), KX[:]):
                    nc.gpsimd.memset(t, 0.0).then_inc(zeroed, 1)

        with nc.Fori(0, QC) as r:
            c = quarter * QC + r
            with stage(nc, "din_hi", "din_lo", "dproj", "sig", "silu_q", "silu_k", "k_sq", "k_n2", "k_nrm",
                       "k_max", "k_inv", "k_unit", "gf", "qa_ready", "wide_v", "wide_p", "dv_proj", "dv_sig",
                       "dv_out", "z_proj", "z_step", "z_act", "lf_ready", "steps_ready", "d_log", "d_exp",
                       "dscores", "pa_ready") as (
                    block, in_hi, in_lo, proj, sig, silu_q, silu_k, k_sq, k_n2, k_nrm,
                    k_max, k_inv, k_unit, gf, qa_ready, wide_v, wide_p, v_proj, v_sig,
                    v_out, z_proj, z_step, z_act, lf_ready, steps_ready, d_log, d_exp,
                    dscores, pa_ready):

                @block.tensor
                def _(pe):
                    pe.wait_ge(in_hi, HALVES)
                    pe.wait_ge(in_lo, HALVES)

                    def pair(s, p, k):
                        return s[:, k, 2 * p:2 * p + 2, :].rearrange("p b s -> p (b s)")

                    for p in range(IP):
                        passes = [x for k in range(HALVES) for x in split_products(
                            pair(SH, p, k), pair(SL, p, k), wfh[:, k, :], wfl[:, k, :])]
                        for i, (left, right) in enumerate(passes):
                            mm = nc.tensor.matmul(bank[6][:, p * HEADS:(p + 1) * HEADS], left, right,
                                                  start=(i == 0), stop=(i == len(passes) - 1))
                    mm.then_inc(z_proj, 1)
                    for n in range(8):
                        m, tensor = n // 4, n % 4
                        if n == 4:
                            pe.wait_ge(silu_q, 1)
                        if n == 5:
                            pe.wait_ge(silu_k, 1)
                        if n >= 6:
                            pe.wait_ge(sig, n - 3)
                        passes = [x for k in range(HALVES) for x in split_products(
                            wh[:, tensor, k, m * P:(m + 1) * P], wl[:, tensor, k, m * P:(m + 1) * P],
                            SH[:, k, :, 0:SEQ], SL[:, k, :, 0:SEQ])]
                        for i, (left, right) in enumerate(passes):
                            mm = nc.tensor.matmul(bank[n % 4][:, 0:CT], left, right,
                                                  start=(i == 0), stop=(i == len(passes) - 1))
                        mm.then_inc(proj, 1)
                    for p in range(IP):
                        if p >= 1:
                            pe.wait_ge(v_out, 4 * p)
                        passes = [x for k in range(HALVES) for x in split_products(
                            pair(SH, p, k), pair(SL, p, k), wh[:, V, k, :], wl[:, V, k, :])]
                        for i, (left, right) in enumerate(passes):
                            mm = nc.tensor.matmul(bank[7][:, 0:D], left, right,
                                                  start=(i == 0), stop=(i == len(passes) - 1))
                        mm.then_inc(v_proj, 1)
                    for m in range(HALVES):
                        pe.wait_ge(k_sq, m + 1)
                        nc.tensor.matmul(bank[4 + m][:, 0:CT], same[:, :], KQ[:, m, :],
                                         start=True, stop=True).then_inc(k_n2, 1)

                    def decay(b):
                        pe.wait_ge(steps_ready, b + 1)
                        if b < 2:
                            pe.wait_ge(k_nrm, b + 1)
                        else:
                            pe.wait_ge(d_exp, b - 1)
                        nc.tensor.matmul(bank[4 + b % 2][:, 0:CT], identb[:, :], spread(past[:, :], 1, PAIRS),
                                         start=True, stop=False)
                        nc.tensor.matmul(bank[4 + b % 2][:, 0:CT], after[:, :],
                                         MV[:, b % 2].rearrange("p g t -> p (g t)"),
                                         start=False, stop=True).then_inc(d_log, 1)

                    decay(0)
                    for b in range(CB):
                        if b + 1 < CB:
                            decay(b + 1)
                        for m in range(HALVES):
                            if b == 0 and m == 0:
                                pe.wait_ge(qa_ready, HALVES)
                                pe.wait_ge(silu_q, HALVES)
                                pe.wait_ge(silu_k, HALVES)
                                pe.wait_ge(sig, 8)
                            pe.wait_ge(wide_v if m == 0 else wide_p, b + 1)
                            if b >= 2:
                                pe.wait_ge(pa_ready, HALVES * (b - 2) + m + 1)
                            for g in range(PPH):
                                mm = nc.tensor.matmul(
                                    bank[2 * (b % 2) + m][:, g * 2 * SEQ:(g + 1) * 2 * SEQ],
                                    KX[:, b % NR, PPH * m + g].rearrange("p e s -> p (e s)"),
                                    QA[:, m, b].rearrange("p x t -> p (x t)"), start=True, stop=True)
                            mm.then_inc(dscores, 1)

                @block.scalar
                def _(act):
                    for m in range(HALVES):
                        nc.scalar.activation(SH[:, m, :, 0:SEQ],
                                             xh_c[:, m, c, :].bitcast(F32).rearrange("p (b s) -> p b s", b=CB),
                                             ACT.Copy).then_inc(in_hi, 1)
                    for n in range(8):
                        m, tensor = n // 4, n % 4
                        act.wait_ge(proj, n + 1)
                        dst = (SQ[:, m, 0], SQ[:, m, 1], GM[:, m], FM[:, m])[tensor]
                        nc.scalar.activation(dst, bank[n % 4][:, 0:CT], ACT.Sigmoid).then_inc(sig, 1)
                    for p in range(IP):
                        act.wait_ge(v_proj, p + 1)
                        if p >= 2:
                            act.wait_ge(v_out, 4 * (p - 1))
                        nc.scalar.activation(SV[:, p % 2, :], bank[7][:, 0:D], ACT.Sigmoid).then_inc(v_sig, 1)
                    for m in range(HALVES):
                        act.wait_ge(k_n2, m + 1)
                        nc.scalar.activation(NK[:, m, :], bank[4 + m][:, 0:CT], ACT.Sqrt).then_inc(k_nrm, 1)
                    act.wait_ge(z_step, 1)
                    nc.scalar.activation(LZ[:, 1, :], bank[6][:, 0:IP * HEADS], ACT.Abs).then_inc(z_act, 1)
                    act.wait_ge(z_act, 1)
                    nc.scalar.activation(LZ[:, 1, :], LZ[:, 1, :], ACT.Exp, scale=-1.0).then_inc(z_act, 1)
                    act.wait_ge(z_step, 2)
                    nc.scalar.activation(LZ[:, 2, :], LZ[:, 2, :], ACT.Ln).then_inc(z_act, 1)
                    for b in range(CB):
                        act.wait_ge(d_log, b + 1)
                        if b >= 2:
                            act.wait_ge(pa_ready, HALVES * (b - 1))
                        nc.scalar.activation(DS[:, b % 2].rearrange("p g t -> p (g t)"),
                                             bank[4 + b % 2][:, 0:CT], ACT.Exp).then_inc(d_exp, 1)

                @block.vector
                def _(dve):
                    for m in range(HALVES):
                        nc.vector.tensor_copy(SL[:, m, :, 0:SEQ],
                                              xl_c[:, m, c, :].bitcast(F32).rearrange("p (b s) -> p b s", b=CB)
                                              ).then_inc(in_lo, 1)
                    dve.wait_ge(z_proj, 1)
                    z = bank[6][:, 0:IP * HEADS]
                    nc.vector.tensor_scalar(LZ[:, 0, :], z, 0.0, None, ALU.min).then_inc(z_step, 1)
                    for m in range(HALVES):
                        dve.wait_ge(sig, 4 * m + 1)
                        nc.vector.tensor_tensor(
                            QA[:, m, :, 0, :], bank[0][:, 0:CT].rearrange("p (b s) -> p b s", b=CB),
                            SQ[:, m, 0].rearrange("p (b s) -> p b s", b=CB), ALU.mult).then_inc(silu_q, 1)
                        dve.wait_ge(sig, 4 * m + 2)
                        nc.vector.tensor_tensor(
                            KT[:, m], bank[1][:, 0:CT].rearrange("p (b s) -> p b s", b=CB),
                            SQ[:, m, 1].rearrange("p (b s) -> p b s", b=CB), ALU.mult).then_inc(silu_k, 1)
                    for p in range(IP):
                        dve.wait_ge(v_sig, p + 1)
                        for s in range(2):
                            v4 = bank[7][half(s), 0:D].rearrange("p (g e d) -> p g e d", e=2, d=HD)
                            s4 = SV[half(s), p % 2, :].rearrange("p (g e d) -> p g e d", e=2, d=HD)
                            for e in range(2):
                                nc.vector.tensor_tensor(VH[half(e), r * CB + 2 * p + s], v4[:, :, e, :],
                                                        s4[:, :, e, :], ALU.mult).then_inc(v_out, 1)
                    dve.wait_ge(z_act, 2)
                    nc.vector.tensor_scalar(LZ[:, 2, :], LZ[:, 1, :], 1.0, None, ALU.add).then_inc(z_step, 1)
                    for m in range(HALVES):
                        dve.wait_ge(k_nrm, m + 1)
                        nc.vector.tensor_scalar(NK[:, m, :], NK[:, m, :], 1e-12, None, ALU.max).then_inc(k_max, 1)
                        dve.wait_ge(k_max, m + 1)
                        nc.vector.reciprocal(NK[:, m, :], NK[:, m, :]).then_inc(k_inv, 1)
                        dve.wait_ge(k_inv, m + 1)
                        dve.wait_ge(k_sq, m + 1)
                        nc.vector.tensor_tensor(KT[:, m].rearrange("p b s -> p (b s)"),
                                                KT[:, m].rearrange("p b s -> p (b s)"),
                                                NK[:, m, :], ALU.mult).then_inc(k_unit, 1)
                        dve.wait_ge(k_unit, m + 1)
                        dve.wait_ge(gf, m + 1)
                        nc.vector.scalar_tensor_tensor(
                            out=QA[:, m, :, 1, :], in0=KT[:, m], scalar=-1.0,
                            in1=GM[:, m].rearrange("p (b s) -> p b s", b=CB),
                            op0=ALU.mult, op1=ALU.mult).then_inc(qa_ready, 1)
                    dve.wait_ge(z_act, 3)
                    nc.vector.tensor_tensor(LZ[:, 3, :], LZ[:, 0, :], LZ[:, 2, :], ALU.subtract).then_inc(z_step, 1)
                    dve.wait_ge(z_step, 3)
                    for s in range(2):
                        lz = LZ[half(s), 3, :].rearrange("p (i g e) -> p i g e", i=IP, e=2)
                        for e in range(2):
                            nc.vector.tensor_copy(LF[half(e)].rearrange("p (i s) g -> p i s g", s=2)[:, :, s, :],
                                                  lz[:, :, :, e]).then_inc(lf_ready, 1)

                    def widen(b):
                        if b >= NR:
                            dve.wait_ge(dscores, HALVES * (b - NR) + 1)
                        nc.vector.tensor_tensor(
                            KX[:, b % NR, 0:PPH].rearrange("p g e s -> p (g e) s")[:, :, 0:SEQ],
                            spread(KT[:, 0, b, :], 1, HPH), spread(hmask[:, :], 2, SEQ),
                            ALU.mult).then_inc(wide_v, 1)

                    widen(0)
                    for b in range(CB):
                        if b + 1 < CB:
                            widen(b + 1)
                        dve.wait_ge(d_exp, b + 1)
                        for m in range(HALVES):
                            dve.wait_ge(dscores, HALVES * b + m + 1)
                            nc.vector.tensor_tensor(
                                PA[:, r * CB + b, PPH * m:PPH * (m + 1)],
                                bank[2 * (b % 2) + m][:, 0:CT].rearrange("p (g x t) -> p g x t", g=PPH, x=2),
                                spread(DS[:, b % 2, PPH * m:PPH * (m + 1)], 2, 2),
                                ALU.mult).then_inc(pa_ready, 1)

                @block.gpsimd
                def _(pool):
                    for m in range(HALVES):
                        pool.wait_ge(silu_k, m + 1)
                        flat = KT[:, m].rearrange("p b s -> p (b s)")
                        nc.gpsimd.tensor_tensor(KQ[:, m, :], flat, flat, ALU.mult).then_inc(k_sq, 1)
                    for m in range(HALVES):
                        pool.wait_ge(sig, 4 * m + 4)
                        nc.gpsimd.tensor_tensor(GM[:, m, :], GM[:, m, :], FM[:, m, :], ALU.mult).then_inc(gf, 1)

                    def steps(b):
                        if b >= 2:
                            pool.wait_ge(d_log, b - 1)
                        nc.gpsimd.tensor_tensor(MV[:, b % 2], spread(LF[:, b, :], 2, SEQ),
                                                spread(here[:, :], 1, PAIRS), ALU.mult).then_inc(steps_ready, 1)

                    pool.wait_ge(lf_ready, 4)
                    pool.wait_ge(k_unit, HALVES)
                    for b in range(CB):
                        steps(b)
                        if b >= NR:
                            pool.wait_ge(dscores, HALVES * (b - NR) + 2)
                        nc.gpsimd.tensor_tensor(
                            KX[:, b % NR, PPH:PAIRS].rearrange("p g e s -> p (g e) s")[:, :, 0:SEQ],
                            spread(KT[:, 1, b, :], 1, HPH), spread(hmask[:, :], 2, SEQ),
                            ALU.mult).then_inc(wide_p, 1)


def delta_solve(nc, sb, bank, ident, PA, VH, XH, XL, quarter):
    with ExitStack() as ctx:
        AS = sb(ctx, "a_rows", [P, SEQ, 2, SEQ])
        U = sb(ctx, "u", [P, 2, HD, PAD])
        UB = sb(ctx, "u_pairs", [P, QUARTER, PAIRS, 2 * HD])
        PD = sb(ctx, "products", [P, 2, HD, SEQ - 1])
        RD = sb(ctx, "sums", [P, 2, HD])
        a_cols = PA[:].rearrange("p i g x t -> p (i g) x t")
        v_cols = VH[:].rearrange("p i g d -> p (i g) d")
        xh_q = XH[:, :, :].rearrange("p m (q t) -> p m q t", q=4)
        xl_q = XL[:, :, :].rearrange("p m (q t) -> p m q t", q=4)
        VG = HD // 4
        AG = (SEQ + 3) // 4
        OG = QUARTER // 4
        with stage(nc, "u_zero", "turned_in", "taken_in", "multiplied", "reduced", "solved",
                   "u_turned", "u_back", "o_done", "o_hi", "o_lo") as (
                block, u_zero, turned_in, taken_in, multiplied, reduced, solved,
                u_turned, u_back, o_done, o_hi, o_lo):
            @block.tensor
            def _(pe):
                for i in range(VG + AG):
                    if i >= 4:
                        pe.wait_ge(taken_in, i - 3)
                    for j in range(4):
                        if i < VG:
                            col = v_cols[:, :, 4 * i + j]
                        else:
                            col = a_cols[:, :, 1, min(4 * (i - VG) + j, SEQ - 1)]
                        mm = nc.tensor.transpose(bank[i % 4][:, j * P:(j + 1) * P], col, ident[:, :])
                    mm.then_inc(turned_in, 1)
                pe.wait_ge(solved, SEQ - 1)
                pe.wait_ge(taken_in, VG + AG)
                for i in range(2 * VG):
                    if i >= 4:
                        pe.wait_ge(u_back, i - 3)
                    for j in range(4):
                        mm = nc.tensor.transpose(bank[i % 4][0:PAD, j * P:(j + 1) * P],
                                                 U[:, i // VG, 4 * (i % VG) + j, :], ident[:, :])
                    mm.then_inc(u_turned, 1)
                pe.wait_ge(u_back, 2 * VG)
                for o in range(OG):
                    if o >= 2:
                        pe.wait_ge(o_lo, o - 1)
                    for m in range(HALVES):
                        for j in range(4):
                            for g in range(PPH):
                                mm = nc.tensor.matmul(
                                    bank[4 + o % 2][32 * g:32 * g + 32, (4 * m + j) * SEQ:(4 * m + j + 1) * SEQ],
                                    UB[:, 4 * o + j, PPH * m + g, :], PA[:, 4 * o + j, PPH * m + g, 0, :],
                                    start=True, stop=True)
                    mm.then_inc(o_done, 1)

            @block.scalar
            def _(act):
                for i in range(VG + AG):
                    act.wait_ge(turned_in, i + 1)
                    src = bank[i % 4][:, :].rearrange("p (j e s) -> p j e s", j=4, e=2)
                    if i < VG:
                        nc.scalar.activation(U[:, :, 4 * i:4 * i + 4, :].rearrange("p e d s -> p d e s"),
                                             src, ACT.Copy).then_inc(taken_in, 1)
                    else:
                        n = min(4, SEQ - 4 * (i - VG))
                        nc.scalar.activation(AS[:, 4 * (i - VG):4 * (i - VG) + n], src[:, 0:n, :, 0:SEQ],
                                             ACT.Copy).then_inc(taken_in, 1)
                act.wait_ge(u_zero, 1)
                for i in range(2 * VG):
                    act.wait_ge(u_turned, i + 1)
                    e, d = i // VG, 4 * (i % VG)
                    nc.scalar.activation(
                        UB[e * PAD:(e + 1) * PAD].rearrange("p i g c -> p c (i g)")[:, e * HD + d:e * HD + d + 4, :],
                        bank[i % 4][0:PAD, :].rearrange("p (j c) -> p j c", j=4), ACT.Copy).then_inc(u_back, 1)
                for o in range(OG):
                    act.wait_ge(o_done, o + 1)
                    nc.scalar.activation(xh_q[:, :, quarter, 4 * o * SEQ:4 * (o + 1) * SEQ],
                                         bank[4 + o % 2][:, 0:8 * SEQ].rearrange("p (m t) -> p m t", m=HALVES),
                                         ACT.Copy).then_inc(o_hi, 1)

            @block.vector
            def _(dve):
                for t in range(1, SEQ):
                    dve.wait_ge(taken_in, VG + t // 4 + 1)
                    if t >= 2:
                        dve.wait_ge(solved, t - 1)
                    nc.vector.tensor_tensor(PD[:, :, :, 0:t], spread(AS[:, t, :, 0:t], 2, HD), U[:, :, :, 0:t],
                                            ALU.mult).then_inc(multiplied, 1)
                    dve.wait_ge(multiplied, t)
                    nc.vector.tensor_reduce(RD[:, :, :], PD[:, :, :, 0:t], AX.X, ALU.add).then_inc(reduced, 1)
                    dve.wait_ge(reduced, t)
                    nc.vector.tensor_tensor(U[:, :, :, t], U[:, :, :, t], RD[:, :, :], ALU.add).then_inc(solved, 1)
                for o in range(OG):
                    dve.wait_ge(o_hi, o + 1)
                    ts = slice(4 * o * SEQ, 4 * (o + 1) * SEQ)
                    nc.vector.tensor_tensor(xl_q[:, :, quarter, ts],
                                            bank[4 + o % 2][:, 0:8 * SEQ].rearrange("p (m t) -> p m t", m=HALVES),
                                            xh_q[:, :, quarter, ts].bitcast(F32), ALU.subtract).then_inc(o_lo, 1)

            @block.gpsimd
            def _(pool):
                nc.gpsimd.memset(UB[:], 0.0).then_inc(u_zero, 1)


def ternary_ffn(nc, sb, bank, ins, RES, XH, XL, out):
    with ExitStack() as ctx:
        w1t = sb(ctx, "w1_ternary", [P, HALVES, FF], F32R)
        w2t = sb(ctx, "w2_ternary", [P, FB, D], F32R)
        b1 = sb(ctx, "ffn_b1", [P, FB])
        b2 = sb(ctx, "ffn_b2", [P, D])
        with ExitStack() as raw:
            w1 = sb(raw, "ffn_w1", [P, HALVES, FF])
            w2 = sb(raw, "ffn_w2", [P, FB, D])
            up = sb(raw, "is_up", [P, HALVES * FF])
            down = sb(raw, "is_down", [P, HALVES * FF])
            ones = sb(raw, "ones", [P, P])
            S = sb(raw, "scales", [P, 4, 2])
            flat = (w1[:].rearrange("p k f -> p (k f)"), w2[:].rearrange("p f d -> p (f d)"))
            tern = (w1t[:].rearrange("p k f -> p (k f)"), w2t[:].rearrange("p f d -> p (f d)"))
            with stage(nc, "f_loaded", "f_step", "f_sum") as (block, loaded, step, total):
                @block.sync
                def _(sp):
                    for dst, src in ((w1, "ffn_w1"), (w2, "ffn_w2"), (b1, "ffn_b1"), (b2, "ffn_b2")):
                        sp.dma_start(dst[:], ins[src]).then_inc(loaded, 16)

                @block.tensor
                def _(pe):
                    pe.wait_ge(step, 3)
                    nc.tensor.matmul(bank[0][:, 0:2], ones[:, :], S[:, 0, :], start=True, stop=True).then_inc(total, 1)

                @block.vector
                def _(dve):
                    n = 0

                    def then(ins_):
                        nonlocal n
                        n += 1
                        ins_.then_inc(step, 1)
                        dve.wait_ge(step, n)

                    then(nc.vector.memset(ones[:], 1.0))
                    dve.wait_ge(loaded, 64)
                    for i in range(2):
                        then(nc.vector.tensor_reduce(S[:, 0, i:i + 1], flat[i], AX.X, ALU.add,
                                                     apply_absolute_value=True))
                    dve.wait_ge(total, 1)
                    then(nc.vector.tensor_scalar(S[:, 1, :], bank[0][:, 0:2], 1.0 / (D * FF), 1e-8,
                                                 ALU.mult, ALU.max))
                    then(nc.vector.tensor_scalar(S[:, 2, :], S[:, 1, :], 0.5, None, ALU.mult))
                    then(nc.vector.tensor_scalar(S[:, 3, :], S[:, 1, :], -0.5, None, ALU.mult))
                    for i in range(2):
                        then(nc.vector.tensor_scalar(up[:], flat[i], S[:, 2, i:i + 1], None, ALU.is_gt))
                        then(nc.vector.tensor_scalar(down[:], flat[i], S[:, 3, i:i + 1], None, ALU.is_lt))
                        then(nc.vector.tensor_tensor(tern[i], up[:], down[:], ALU.subtract))

        H = sb(ctx, "fhidden", [P, 4, MT * P])
        HH = sb(ctx, "fhidden_hi", [P, 2, FB, MT * P], F32R)
        HL = sb(ctx, "fhidden_lo", [P, 2, FB, MT * P], F32R)
        steps = [range(t, min(t + MT, TILES)) for t in range(0, TILES, MT)]
        with stage(nc, "f_up", "f_act", "f_hi", "f_lo", "f_down", "f_bias", "f_out", "stored") as (
                block, up_ready, acted, h_hi, h_lo, down_ready, biased, out_ready, stored):
            @block.tensor
            def _(pe):
                def hidden(c):
                    n = len(steps[c]) * P
                    ts = slice(steps[c][0] * P, steps[c][0] * P + n)
                    for f in range(FB):
                        i = FB * c + f
                        if i >= 4:
                            pe.wait_ge(acted, i - 3)
                        passes = [(w1t[:, k, f * P:(f + 1) * P], X[:, k, ts]) for k in range(HALVES) for X in (XH, XL)]
                        for j, (left, right) in enumerate(passes):
                            mm = nc.tensor.matmul(bank[i % 4][:, 0:n], left, right,
                                                  start=(j == 0), stop=(j == len(passes) - 1))
                        mm.then_inc(up_ready, 1)

                def output(c):
                    pe.wait_ge(h_lo, FB * (c + 1))
                    for j, t in enumerate(steps[c]):
                        if t >= 4:
                            pe.wait_ge(out_ready, t - 3)
                        passes = [(X[:, c % 2, f, j * P:(j + 1) * P], w2t[:, f, :]) for f in range(FB) for X in (HH, HL)]
                        for n, (left, right) in enumerate(passes):
                            mm = nc.tensor.matmul(bank[4 + t % 4][:, 0:D], left, right,
                                                  start=(n == 0), stop=(n == len(passes) - 1))
                        mm.then_inc(down_ready, 1)

                hidden(0)
                for c in range(len(steps)):
                    if c + 1 < len(steps):
                        hidden(c + 1)
                    output(c)

            @block.scalar
            def _(act):
                for c, st in enumerate(steps):
                    n = len(st) * P
                    for f in range(FB):
                        i = FB * c + f
                        act.wait_ge(up_ready, i + 1)
                        if i >= 4:
                            act.wait_ge(h_lo, i - 3)
                        nc.scalar.activation(H[:, i % 4, 0:n], bank[i % 4][:, 0:n], ACT.Gelu,
                                             bias=b1[:, f:f + 1]).then_inc(acted, 1)

            @block.vector
            def _(dve):
                def finish(c):
                    for t in steps[c]:
                        dve.wait_ge(down_ready, t + 1)
                        dve.wait_ge(biased, t + 1)
                        nc.vector.tensor_tensor(RES[:, t, :], RES[:, t, :], bank[4 + t % 4][:, 0:D],
                                                ALU.add).then_inc(out_ready, 1)

                for c, st in enumerate(steps):
                    n = len(st) * P
                    if c >= 2:
                        dve.wait_ge(down_ready, steps[c - 2][-1] + 1)
                    for f in range(FB):
                        i = FB * c + f
                        dve.wait_ge(acted, i + 1)
                        nc.vector.tensor_copy(HH[:, c % 2, f, 0:n], H[:, i % 4, 0:n]).then_inc(h_hi, 1)
                        dve.wait_ge(h_hi, i + 1)
                        nc.vector.tensor_tensor(HL[:, c % 2, f, 0:n], H[:, i % 4, 0:n],
                                                HH[:, c % 2, f, 0:n].bitcast(F32), ALU.subtract).then_inc(h_lo, 1)
                    if c >= 1:
                        finish(c - 1)
                finish(len(steps) - 1)

            @block.gpsimd
            def _(pool):
                for t in range(TILES):
                    nc.gpsimd.tensor_tensor(RES[:, t, :], RES[:, t, :], b2[:, :], ALU.add).then_inc(biased, 1)

            @block.sync
            def _(sp):
                for t in range(TILES):
                    sp.wait_ge(out_ready, t + 1)
                    sp.dma_start(out[t * P:(t + 1) * P, :], RES[:, t, :]).then_inc(stored, 16)
                sp.wait_ge(stored, 16 * TILES)



def _constants():
    one = np.float32
    base = one(10000.0)
    half = HD // 2
    inv_freq = one(1.0) / base ** (np.arange(half, dtype=np.float32) / one(half))
    ang = inv_freq[:, None] * np.arange(SEQ, dtype=np.float32)[None, :]
    cos = np.concatenate([np.cos(ang), np.cos(ang)], 0)
    sin = np.concatenate([-np.sin(ang), np.sin(ang)], 0)
    part = np.arange(P)
    step = np.arange(SEQ)
    row = part % PAD
    col = np.arange(P)
    same = (part[:, None] // PAD) == (col[None, :] // PAD)
    later = (part[:, None] % PAD) > (col[None, :] % PAD)
    real = (row[:, None] < SEQ) & ((col[None, :] % PAD) < SEQ)
    return {
        "ident": np.eye(P),
        "head_mask": (part[:, None] // HD) == np.arange(HPH)[None, :],
        "cos": np.tile(cos, (HPH, 1)),
        "sin": np.tile(sin, (HPH, 1)),
        "same_head": (part[:, None] // HD) == (col[None, :] // HD),
        "causal": np.where((row[:, None] < SEQ) & (step[None, :] > row[:, None]), MASKED, 0.0),
        "past": np.where((row[:, None] >= SEQ) | (step[None, :] < row[:, None]), MASKED, 0.0),
        "from_here": (row[:, None] <= step[None, :]),
        "after": same & later & real,
        "ties": np.tile((np.arange(EXPERTS)[None, :] <= np.arange(EXPERTS)[:, None]).reshape(1, -1), (P, 1)),
    }


def _lay_out(v):
    def rows(a):
        return a.reshape(-1, P, a.shape[-1]).transpose(1, 0, 2)

    def cols(a):
        return a.reshape(-1, P).T

    def swapped(a):
        return a.reshape(D, HEADS, 2, HD // 2)[:, :, ::-1].reshape(D, D)

    x = v["x"].reshape(IMAGES, 3, 6, 16, 6, 16).transpose(1, 3, 5, 0, 2, 4).reshape(KP, P, CHUNKS, CP)
    first = np.concatenate([v["cls_tok"].reshape(1, D), v["L0_tok_cls_token"].reshape(1, D),
                            np.repeat(v["L0_tok_b"].reshape(1, D), PATCHES, 0)], 0)
    wq, wk, wv, wo = (v[f"L0_attn_W{n}"].T for n in "qkvo")
    return {
        "patches": x.transpose(2, 1, 0, 3),
        "tok_w": rows(v["L0_tok_W"].T),
        "tok_bias": rows(first.T),
        "tok_pos": rows(v["L0_tok_pos_embedding"][0].T),
        "att_w": np.stack([rows(a) for a in (wq, swapped(wq), wk, swapped(wk), wv, wo)], 1),
        "wr": rows(v["L0_ffn_Wr"]),
        "br": np.repeat(v["L0_ffn_br"].reshape(1, EXPERTS), P, 0),
        "moe_w1": v["L0_ffn_W1"].reshape(EXPERTS, HALVES, P, FF).transpose(0, 2, 1, 3),
        "moe_b1": v["L0_ffn_b1"].reshape(EXPERTS, FB, P).transpose(2, 0, 1),
        "moe_w2": v["L0_ffn_W2"].reshape(EXPERTS, FB, P, D).transpose(0, 2, 1, 3),
        "moe_b2": v["L0_ffn_b2"],
        "delta_w": np.stack([rows(a) for a in (
            v["L1_attn_Wq"], v["L1_attn_Wk"], np.repeat(v["L1_attn_Wgamma"], HD, 1),
            np.repeat(v["L1_attn_Wf"], HD, 1), v["L1_attn_Wv"], v["L1_attn_Wo"])], 1),
        "delta_wf": rows(v["L1_attn_Wf"]),
        "delta_wg1": rows(v["L1_attn_Wg1"]),
        "delta_wg2": v["L1_attn_Wg2"],
        "norm_w": cols(v["L1_attn_norm_w"]),
        "ffn_w1": rows(v["L1_ffn_W1"].T),
        "ffn_b1": cols(v["L1_ffn_b1"]),
        "ffn_w2": rows(v["L1_ffn_W2"].T),
        "ffn_b2": np.repeat(v["L1_ffn_b2"].reshape(1, D), P, 0),
    }


def kernel(**inputs):
    import concourse.bacc as bacc
    from concourse.bass_utils import run_bass_kernel_spmd as run

    arrays = {n: np.ascontiguousarray(a) for n, a in _lay_out({k: np.asarray(a) for k, a in inputs.items()}).items()}
    for n, a in _constants().items():
        arrays[n] = np.ascontiguousarray(a, dtype=np.float32)
    for n, src in (("ident_bf16", "ident"), ("causal", "causal"), ("past", "past")):
        arrays[n] = arrays[src].astype(mybir.dt.np(BF16))
    nc = bacc.Bacc("TRN2", target_bir_lowering=False, num_devices=1)
    ins = {n: nc.dram_tensor(f"in_{n}", a.shape, mybir.dt.from_np(a.dtype), kind="ExternalInput").ap()
           for n, a in arrays.items()}
    out = nc.dram_tensor("out", (TOKENS, D), F32, kind="ExternalOutput").ap()
    build_tower(nc, ins, out)
    r = run(nc, [{f"in_{n}": a for n, a in arrays.items()}], core_ids=[0])
    return r.results[0]["out"].reshape(IMAGES, SEQ, D)
```

```python
from contextlib import ExitStack, contextmanager
from itertools import count

import numpy as np

import concourse.bass as bass
from concourse import mybir

F32 = mybir.dt.float32
F32R = mybir.dt.float32r
BF16 = mybir.dt.bfloat16
ALU = mybir.AluOpType
ACT = mybir.ActivationFunctionType
AX = mybir.AxisListType

P = 128
IMAGES = 64
SEQ = 38
PATCHES = SEQ - 2
D = 256
HALVES = D // P
HEADS = 16
PAIRS = HEADS // 2
HPH = HEADS // HALVES
PPH = PAIRS // HALVES
HD = D // HEADS
PAD = 64
TOKENS = IMAGES * SEQ
TILES = TOKENS // P
CHUNKS = 8
CB = IMAGES // CHUNKS
CT = CB * SEQ
CP = CB * PATCHES
IP = CB // 2
KP = 768 // P
EXPERTS = 8
FF = 1024
FB = FF // P
MT = 4
EPS = 1e-5
MASKED = -1e30


@contextmanager
def stage(nc, *names):
    with ExitStack() as own:
        sems = [own.enter_context(nc.semaphore(n)) for n in names]
        with nc.Block() as block:
            yield (block, *sems)
        for s in sems:
            nc.gpsimd.sem_clear(s)
        nc.all_engine_barrier()


def spread(ap, axis, n):
    wide = ap.unsqueeze(axis)
    shape = list(wide.shape)
    shape[axis] = n
    return wide.broadcast_to(shape)


def split_products(hi_l, lo_l, hi_r, lo_r):
    return ((hi_l, hi_r), (hi_l, lo_r), (lo_l, hi_r))


def layer_norm_turn(nc, bank, RES, STD, MV, XN, XH, XL, ident, name):
    xh = XH[:, :, 0:TOKENS]
    xl = XL[:, :, 0:TOKENS]
    with stage(nc, name + "_var", name + "_std", name + "_inv", name + "_normed", name + "_turned",
               name + "_hi", name + "_lo") as (block, var_ready, std_ready, inv_ready, normed,
                                               turned, hi_ready, lo_ready):
        @block.vector
        def _(dve):
            nc.vector.tensor_scalar(STD[:, 0, :], MV[:, :, 1], EPS, None, ALU.add).then_inc(var_ready, 1)
            dve.wait_ge(std_ready, 1)
            nc.vector.reciprocal(STD[:, 2, :], STD[:, 1, :]).then_inc(inv_ready, 1)
            dve.wait_ge(inv_ready, 1)

            def low_part(t):
                dve.wait_ge(hi_ready, t + 1)
                nc.vector.tensor_tensor(
                    xl[:, :, t * P:(t + 1) * P], bank[t % 4][:, 0:D].rearrange("p (m t) -> p m t", m=HALVES),
                    xh[:, :, t * P:(t + 1) * P].bitcast(F32), ALU.subtract).then_inc(lo_ready, 1)

            for t in range(TILES):
                if t >= 4:
                    dve.wait_ge(turned, t - 3)
                nc.vector.tensor_scalar(XN[:, t % 4, :], RES[:, t, :], MV[:, t, 0:1], STD[:, 2, t:t + 1],
                                        ALU.subtract, ALU.mult).then_inc(normed, 1)
                if t >= 2:
                    low_part(t - 2)
            low_part(TILES - 2)
            low_part(TILES - 1)

        @block.scalar
        def _(act):
            act.wait_ge(var_ready, 1)
            nc.scalar.activation(STD[:, 1, :], STD[:, 0, :], ACT.Sqrt).then_inc(std_ready, 1)
            for t in range(TILES):
                act.wait_ge(turned, t + 1)
                nc.scalar.activation(xh[:, :, t * P:(t + 1) * P],
                                     bank[t % 4][:, 0:D].rearrange("p (m t) -> p m t", m=HALVES),
                                     ACT.Copy).then_inc(hi_ready, 1)

        @block.tensor
        def _(pe):
            for t in range(TILES):
                pe.wait_ge(normed, t + 1)
                if t >= 4:
                    pe.wait_ge(lo_ready, t - 3)
                for m in range(HALVES):
                    turn = nc.tensor.transpose(bank[t % 4][:, m * P:(m + 1) * P],
                                               XN[:, t % 4, m * P:(m + 1) * P], ident[:, :])
                turn.then_inc(turned, 1)


def split_weights(nc, name, pairs):
    with stage(nc, name + "_hi", name + "_lo") as (block, hi_ready, lo_ready):
        @block.scalar
        def _(act):
            for raw, hi, lo in pairs:
                nc.scalar.activation(hi, raw, ACT.Copy).then_inc(hi_ready, 1)

        @block.vector
        def _(dve):
            for n, (raw, hi, lo) in enumerate(pairs):
                dve.wait_ge(hi_ready, n + 1)
                nc.vector.tensor_tensor(lo, raw, hi.bitcast(F32), ALU.subtract).then_inc(lo_ready, 1)


def add_product_and_stats(nc, bank, RES, BN, MV, OH, OL, wh, wl, name):
    oh = OH[:, :, 0:TOKENS]
    ol = OL[:, :, 0:TOKENS]
    with stage(nc, name + "_product", name + "_sum", name + "_bn", name + "_mv") as (
            block, product, summed, bn_ready, mv_ready):
        @block.tensor
        def _(pe):
            for t in range(TILES):
                if t >= 4:
                    pe.wait_ge(summed, t - 3)
                passes = [x for k in range(HALVES) for x in split_products(
                    oh[:, k, t * P:(t + 1) * P], ol[:, k, t * P:(t + 1) * P], wh[:, k, :], wl[:, k, :])]
                for n, (left, right) in enumerate(passes):
                    mm = nc.tensor.matmul(bank[t % 4][:, 0:D], left, right,
                                          start=(n == 0), stop=(n == len(passes) - 1))
                mm.then_inc(product, 1)

        @block.vector
        def _(dve):
            for t in range(TILES + 2):
                if t < TILES:
                    dve.wait_ge(product, t + 1)
                    nc.vector.tensor_tensor(RES[:, t, :], RES[:, t, :], bank[t % 4][:, 0:D],
                                            ALU.add).then_inc(summed, 1)
                if 1 <= t <= TILES:
                    dve.wait_ge(summed, t)
                    nc.vector.bn_stats(BN[:, t - 1, :], RES[:, t - 1, :]).then_inc(bn_ready, 1)
                if t >= 2:
                    dve.wait_ge(bn_ready, t - 1)
                    nc.vector.bn_aggr(MV[:, t - 2, :], BN[:, t - 2, :]).then_inc(mv_ready, 1)


def build_tower(nc, ins, out):
    with ExitStack() as whole:
        numbers = count()

        def sb(ctx, name, shape, dt=F32):
            name = f"{name}_{next(numbers)}"
            return ctx.enter_context(nc.sbuf_tensor(name, shape, dt))

        bank = [whole.enter_context(nc.psum_tensor(f"bank{i}", [P, 512], F32)) for i in range(8)]
        RES = sb(whole, "residual", [P, TILES, D])
        XH = sb(whole, "x_hi", [P, HALVES, TOKENS], F32R)
        XL = sb(whole, "x_lo", [P, HALVES, TOKENS], F32R)
        BN = sb(whole, "bn", [P, TILES, 6])
        MV = sb(whole, "mean_var", [P, TILES, 2])
        STD = sb(whole, "std", [P, 3, TILES])
        XN = sb(whole, "normed_tiles", [P, 4, D])
        ident = sb(whole, "ident", [P, P])
        identb = sb(whole, "ident_bf16", [P, P], BF16)
        hmask = sb(whole, "head_mask", [P, HPH])
        xh_c = XH[:, :, :].rearrange("p m (c t) -> p m c t", c=CHUNKS)
        xl_c = XL[:, :, :].rearrange("p m (c t) -> p m c t", c=CHUNKS)

        tokens_stage(nc, sb, bank, ins, RES, BN, MV, ident, identb, hmask)
        layer_norm_turn(nc, bank, RES, STD, MV, XN, XH, XL, ident, "ln0")
        softmax_attention(nc, sb, bank, ins, RES, BN, MV, XH, XL, xh_c, xl_c, ident, identb, hmask)
        layer_norm_turn(nc, bank, RES, STD, MV, XN, XH, XL, ident, "ln1")
        mixture(nc, sb, bank, ins, RES, BN, MV, XH, XL, ident)
        tile_stats(nc, RES, BN, MV, "moe")
        layer_norm_turn(nc, bank, RES, STD, MV, XN, XH, XL, ident, "ln2")
        delta_attention(nc, sb, bank, ins, RES, BN, MV, STD, XN, XH, XL, xh_c, xl_c, ident, identb, hmask)
        layer_norm_turn(nc, bank, RES, STD, MV, XN, XH, XL, ident, "ln3")
        ternary_ffn(nc, sb, bank, ins, RES, XH, XL, out)


def tokens_stage(nc, sb, bank, ins, RES, BN, MV, ident, identb, hmask):
    with ExitStack() as ctx:
        x = sb(ctx, "patches", [P, CHUNKS, KP, CP])
        w = sb(ctx, "tok_w", [P, KP, D])
        wh = sb(ctx, "tok_wh", [P, KP, D], F32R)
        wl = sb(ctx, "tok_wl", [P, KP, D], F32R)
        xh = sb(ctx, "patch_hi", [P, KP, CP], F32R)
        xl = sb(ctx, "patch_lo", [P, KP, CP], F32R)
        table = sb(ctx, "tok_bias", [P, HALVES, SEQ])
        pos = sb(ctx, "tok_pos", [P, HALVES, SEQ - 1])
        ET = sb(ctx, "tokens_t", [P, HALVES, CHUNKS, CB, SEQ])

        with stage(nc, "loaded", "table_ready") as (block, loaded, table_ready):
            @block.sync
            def _(sp):
                for dst, src in ((w, "tok_w"), (table, "tok_bias"), (pos, "tok_pos"), (ident, "ident"),
                                 (identb, "ident_bf16"), (hmask, "head_mask")):
                    sp.dma_start(dst[:], ins[src]).then_inc(loaded, 16)
                for c in range(0, CHUNKS, 2):
                    sp.dma_start(x[:, c], ins["patches"][c]).then_inc(loaded, 16)

            @block.scalar
            def _(act):
                for c in range(1, CHUNKS, 2):
                    act.dma_start(x[:, c], ins["patches"][c]).then_inc(loaded, 16)

            @block.vector
            def _(dve):
                dve.wait_ge(loaded, 16 * (6 + CHUNKS))
                nc.vector.tensor_tensor(table[:, :, 1:SEQ], table[:, :, 1:SEQ], pos[:, :, :],
                                        ALU.add).then_inc(table_ready, 1)
                dve.wait_ge(table_ready, 1)
                for m in range(HALVES):
                    nc.vector.tensor_copy(
                        ET[:, m].rearrange("p c b s -> p (c b) s")[:, :, 0:2],
                        spread(table[:, m, 0:2], 1, IMAGES)).then_inc(table_ready, 1)
        split_weights(nc, "tokw", [(w[:], wh[:], wl[:])])

        with nc.Fori(0, CHUNKS) as c:
            with stage(nc, "patch_hi", "patch_lo", "tok_product", "tok_done") as (
                    block, hi_ready, lo_ready, product, done):
                @block.scalar
                def _(act):
                    for k in range(KP):
                        nc.scalar.activation(xh[:, k, :], x[:, c, k, :], ACT.Copy).then_inc(hi_ready, 1)

                @block.vector
                def _(dve):
                    for k in range(KP):
                        dve.wait_ge(hi_ready, k + 1)
                        nc.vector.tensor_tensor(xl[:, k, :], x[:, c, k, :], xh[:, k, :].bitcast(F32),
                                                ALU.subtract).then_inc(lo_ready, 1)
                    for m in range(HALVES):
                        dve.wait_ge(product, m + 1)
                        nc.vector.tensor_tensor(
                            ET[:, m, c, :, 2:SEQ], bank[m][:, 0:CP].rearrange("p (b s) -> p b s", b=CB),
                            spread(table[:, m, 2:SEQ], 1, CB), ALU.add).then_inc(done, 1)

                @block.tensor
                def _(pe):
                    for k in range(KP):
                        pe.wait_ge(lo_ready, k + 1)
                        for m in range(HALVES):
                            for n, (left, right) in enumerate(split_products(
                                    wh[:, k, m * P:(m + 1) * P], wl[:, k, m * P:(m + 1) * P],
                                    xh[:, k, :], xl[:, k, :])):
                                mm = nc.tensor.matmul(bank[m][:, 0:CP], left, right,
                                                      start=(k == 0 and n == 0), stop=(k == KP - 1 and n == 2))
                            if k == KP - 1:
                                mm.then_inc(product, 1)

        et = [ET[:, m].rearrange("p c b s -> p (c b s)") for m in range(HALVES)]
        with stage(nc, "tok_turned", "tok_res", "tok_bn", "tok_mv") as (
                block, turned, res_ready, bn_ready, mv_ready):
            @block.tensor
            def _(pe):
                for t in range(TILES):
                    if t >= 4:
                        pe.wait_ge(res_ready, t - 3)
                    for m in range(HALVES):
                        turn = nc.tensor.transpose(bank[t % 4][:, m * P:(m + 1) * P],
                                                   et[m][:, t * P:(t + 1) * P], ident[:, :])
                    turn.then_inc(turned, 1)

            @block.scalar
            def _(act):
                for t in range(TILES):
                    act.wait_ge(turned, t + 1)
                    nc.scalar.activation(RES[:, t, :], bank[t % 4][:, 0:D], ACT.Copy).then_inc(res_ready, 1)

            @block.vector
            def _(dve):
                for t in range(TILES + 1):
                    if t < TILES:
                        dve.wait_ge(res_ready, t + 1)
                        nc.vector.bn_stats(BN[:, t, :], RES[:, t, :]).then_inc(bn_ready, 1)
                    if t >= 1:
                        dve.wait_ge(bn_ready, t)
                        nc.vector.bn_aggr(MV[:, t - 1, :], BN[:, t - 1, :]).then_inc(mv_ready, 1)


def softmax_attention(nc, sb, bank, ins, RES, BN, MV, XH, XL, xh_c, xl_c, ident, identb, hmask):
    with ExitStack() as ctx:
        wh = sb(ctx, "att_wh", [P, 6, HALVES, D], F32R)
        wl = sb(ctx, "att_wl", [P, 6, HALVES, D], F32R)
        cos = sb(ctx, "cos", [P, SEQ])
        sin = sb(ctx, "sin", [P, SEQ])
        causal = sb(ctx, "causal", [P, SEQ], BF16)
        with ExitStack() as raw:
            w = sb(raw, "att_w", [P, 6, HALVES, D])
            with stage(nc, "att_loaded") as (block, loaded):
                @block.sync
                def _(sp):
                    for dst, src in ((w, "att_w"), (cos, "cos"), (sin, "sin"), (causal, "causal")):
                        sp.dma_start(dst[:], ins[src]).then_inc(loaded, 16)
                    sp.wait_ge(loaded, 64)
            split_weights(nc, "attw", [(w[:, n], wh[:, n], wl[:, n]) for n in range(6)])

        b = dict(wh=wh, wl=wl, cos=cos, sin=sin, causal=causal)
        b["SH"] = sb(ctx, "chunk_hi", [P, HALVES, CB, PAD], F32R)
        b["SL"] = sb(ctx, "chunk_lo", [P, HALVES, CB, PAD], F32R)
        b["RC"] = sb(ctx, "rope_cos", [P, 2, CB, SEQ])
        b["RS"] = sb(ctx, "rope_sin", [P, 2, CB, SEQ])
        b["KT"] = sb(ctx, "k_t", [P, HALVES, CB, SEQ])
        b["PR"] = sb(ctx, "probs", [P, 2, HEADS, PAD])
        b["PT"] = sb(ctx, "probs_t", [P, PAIRS, P])
        b["MX"] = sb(ctx, "row_max", [P, 2, HEADS])
        b["SM"] = sb(ctx, "row_sum", [P, 2, HEADS])
        b["RI"] = sb(ctx, "row_inv", [P, 2, HEADS])
        QT = [sb(ctx, f"q_t{i}", [P, HALVES, CB, PAD]) for i in range(2)]
        KX = [sb(ctx, f"k_by_head{i}", [P, HALVES, CB, HPH, SEQ]) for i in range(2)]
        VB = [sb(ctx, f"v_pairs{i}", [P, CB, PAIRS, 2 * HD]) for i in range(2)]

        with stage(nc, "att_zero") as (block, zeroed):
            @block.gpsimd
            def _(pool):
                for t in (b["SH"][:].bitcast(F32), QT[0][:], VB[0][:], b["PR"][:]):
                    nc.gpsimd.memset(t, 0.0).then_inc(zeroed, 1)

            @block.vector
            def _(dve):
                for t in (b["SL"][:].bitcast(F32), QT[1][:], VB[1][:]):
                    nc.vector.memset(t, 0.0).then_inc(zeroed, 1)

        def step(attended, projected, parity):
            attention_step(nc, bank, xh_c, xl_c, ident, identb, hmask, b, attended, projected,
                           (QT[parity], KX[parity], VB[parity]), (QT[1 - parity], KX[1 - parity], VB[1 - parity]))

        step(None, 0, 1)
        with nc.Fori(0, CHUNKS // 2 - 1) as i:
            step(i * 2, i * 2 + 1, 0)
            step(i * 2 + 1, i * 2 + 2, 1)
        step(CHUNKS - 2, CHUNKS - 1, 0)
        step(CHUNKS - 1, None, 1)
        add_product_and_stats(nc, bank, RES, BN, MV, XH, XL, wh[:, 5], wl[:, 5], "att_o")


def attention_step(nc, bank, xh_c, xl_c, ident, identb, hmask, b, c, nxt, now, then):
    Q, QS, K, KS, V = range(5)
    wh, wl, cos, sin, causal = b["wh"], b["wl"], b["cos"], b["sin"], b["causal"]
    SH, SL, RC, RS, KT = b["SH"], b["SL"], b["RC"], b["RS"], b["KT"]
    PR, PT, MX, SM, RI = b["PR"], b["PT"], b["MX"], b["SM"], b["RI"]
    QT, KX, VB = now
    QTn, KXn, VBn = then
    jobs = ((Q, 0), (QS, 0), (K, 0), (KS, 0), (Q, 1), (QS, 1), (K, 1), (KS, 1))

    def half(s):
        return slice(s * PAD, (s + 1) * PAD)

    def out_bank(p):
        return bank[5][:, 0:4 * SEQ]

    with stage(nc, "in_hi", "in_lo", "proj", "roped_c", "roped_s", "roped", "k_wide",
               "v_proj", "v_out", "scores", "maxed", "shifted", "exped", "summed", "inverted",
               "normed", "p_turned", "p_out", "out_t", "out_hi", "out_lo") as (
            block, in_hi, in_lo, proj, roped_c, roped_s, roped, k_wide,
            v_proj, v_out, scores, maxed, shifted, exped, summed, inverted,
            normed, p_turned, p_out, out_t, out_hi, out_lo):

        @block.tensor
        def _(pe):
            def project(n):
                if nxt is None:
                    return
                if n == 0:
                    pe.wait_ge(in_hi, HALVES)
                    pe.wait_ge(in_lo, HALVES)
                if n >= 2:
                    pe.wait_ge(roped_c if n % 2 == 0 else roped_s, (n - 2) // 2 + 1)
                tensor, m = jobs[n]
                passes = [x for k in range(HALVES) for x in split_products(
                    wh[:, tensor, k, m * P:(m + 1) * P], wl[:, tensor, k, m * P:(m + 1) * P],
                    SH[:, k, :, 0:SEQ], SL[:, k, :, 0:SEQ])]
                for i, (left, right) in enumerate(passes):
                    mm = nc.tensor.matmul(bank[6 + n % 2][:, 0:CT], left, right,
                                          start=(i == 0), stop=(i == len(passes) - 1))
                mm.then_inc(proj, 1)

            def values(p):
                if nxt is None:
                    return
                if p < 2:
                    pe.wait_ge(roped_c if p == 0 else roped_s, 4)
                else:
                    pe.wait_ge(v_out, 4 * (p - 1))
                passes = [x for k in range(HALVES) for x in split_products(
                    SH[:, k, 2 * p:2 * p + 2, :].rearrange("p b s -> p (b s)"),
                    SL[:, k, 2 * p:2 * p + 2, :].rearrange("p b s -> p (b s)"),
                    wh[:, V, k, :], wl[:, V, k, :])]
                for i, (left, right) in enumerate(passes):
                    mm = nc.tensor.matmul(bank[6 + p % 2][:, 0:D], left, right,
                                          start=(i == 0), stop=(i == len(passes) - 1))
                mm.then_inc(v_proj, 1)

            def score(p):
                if c is None:
                    return
                for m in range(HALVES):
                    u = HALVES * p + m
                    sc = bank[u % 3]
                    if u >= 3:
                        pe.wait_ge(shifted, u - 2)
                    nc.tensor.matmul(sc[:, 0:CT], identb[:, :], spread(causal[:, :], 1, HPH),
                                     start=True, stop=True)
                    for s in range(2):
                        mm = nc.tensor.matmul(sc[half(s), 0:CT], QT[:, m, 2 * p + s, :],
                                              KX[:, m, 2 * p + s].rearrange("p h s -> p (h s)"),
                                              start=False, stop=True, skip_group_check=True)
                    mm.then_inc(scores, 1)

            def turn(p):
                if c is None:
                    return
                pe.wait_ge(normed, p + 1)
                for g in range(PAIRS):
                    if p >= 1 and g % 4 == 0:
                        pe.wait_ge(p_out, 2 * (p - 1) + g // 4 + 1)
                    mm = nc.tensor.transpose(
                        bank[3 + g // 4][:, (g % 4) * P:(g % 4 + 1) * P],
                        PR[:, p % 2, 2 * g:2 * g + 2, :].rearrange("p h k -> p (h k)"), ident[:, :])
                    if g % 4 == 3:
                        mm.then_inc(p_turned, 1)

            def attend(p):
                if c is None:
                    return
                if p >= 1:
                    pe.wait_ge(out_lo, p)
                for m in range(HALVES):
                    pe.wait_ge(p_out, 2 * p + m + 1)
                    for s in range(2):
                        for g in range(PPH):
                            mm = nc.tensor.matmul(
                                out_bank(p)[32 * g:32 * g + 32, (2 * m + s) * SEQ:(2 * m + s + 1) * SEQ],
                                VB[:, 2 * p + s, PPH * m + g, :], PT[:, PPH * m + g, s * PAD:s * PAD + SEQ],
                                start=True, stop=True)
                mm.then_inc(out_t, 1)

            score(0)
            project(0)
            project(1)
            score(1)
            project(2)
            project(3)
            turn(0)
            project(4)
            attend(0)
            score(2)
            project(5)
            project(6)
            turn(1)
            project(7)
            attend(1)
            score(3)
            values(0)
            turn(2)
            values(1)
            attend(2)
            values(2)
            turn(3)
            values(3)
            attend(3)

        @block.vector
        def _(dve):
            def low_in():
                if nxt is None:
                    return
                for m in range(HALVES):
                    nc.vector.tensor_copy(SL[:, m, :, 0:SEQ], xl_c[:, m, nxt, :].bitcast(F32).rearrange(
                        "p (b s) -> p b s", b=CB)).then_inc(in_lo, 1)

            def rope(r):
                if nxt is None:
                    return
                if r >= 2:
                    dve.wait_ge(roped, r - 1)
                dve.wait_ge(proj, 2 * r + 1)
                nc.vector.tensor_tensor(RC[:, r % 2], bank[6][:, 0:CT].rearrange("p (b s) -> p b s", b=CB),
                                        spread(cos[:, :], 1, CB), ALU.mult).then_inc(roped_c, 1)
                dve.wait_ge(proj, 2 * r + 2)
                nc.vector.tensor_tensor(RS[:, r % 2], bank[7][:, 0:CT].rearrange("p (b s) -> p b s", b=CB),
                                        spread(sin[:, :], 1, CB), ALU.mult).then_inc(roped_s, 1)

            def keys_by_head(heads):
                if nxt is None:
                    return
                dve.wait_ge(roped, 2)
                for h in heads:
                    nc.vector.tensor_scalar(KXn[:, 0, :, h, :], KT[:, 0], hmask[:, h:h + 1], None,
                                            ALU.mult).then_inc(k_wide, 1)

            def shift(p):
                if c is None:
                    return
                for m in range(HALVES):
                    u = HALVES * p + m
                    s3 = bank[u % 3][:, 0:CT].rearrange("p (h k) -> p h k", h=HPH)
                    hs = slice(HPH * m, HPH * (m + 1))
                    dve.wait_ge(scores, u + 1)
                    nc.vector.tensor_reduce(MX[:, p % 2, hs], s3, AX.X, ALU.max).then_inc(maxed, 1)
                    dve.wait_ge(maxed, u + 1)
                    if p >= 2:
                        dve.wait_ge(p_turned, HALVES * (p - 1))
                    nc.vector.tensor_tensor(PR[:, p % 2, hs, 0:SEQ], s3, spread(MX[:, p % 2, hs], 2, SEQ),
                                            ALU.subtract).then_inc(shifted, 1)

            def add_up(p):
                if c is None:
                    return
                dve.wait_ge(exped, p + 1)
                nc.vector.tensor_reduce(SM[:, p % 2, :], PR[:, p % 2, :, 0:SEQ], AX.X,
                                        ALU.add).then_inc(summed, 1)
                dve.wait_ge(summed, p + 1)
                nc.vector.reciprocal(RI[:, p % 2, :], SM[:, p % 2, :]).then_inc(inverted, 1)

            def low_out(p):
                if c is None:
                    return
                dve.wait_ge(out_hi, p + 1)
                ts = slice(2 * p * SEQ, 2 * (p + 1) * SEQ)
                nc.vector.tensor_tensor(xl_c[:, :, c, ts], out_bank(p).rearrange("p (m t) -> p m t", m=HALVES),
                                        xh_c[:, :, c, ts].bitcast(F32), ALU.subtract).then_inc(out_lo, 1)

            low_in()
            shift(0)
            rope(0)
            add_up(0)
            shift(1)
            rope(1)
            add_up(1)
            keys_by_head(range(0, 4))
            rope(2)
            shift(2)
            keys_by_head(range(4, HPH))
            add_up(2)
            low_out(0)
            rope(3)
            shift(3)
            add_up(3)
            low_out(1)
            low_out(2)
            low_out(3)

        @block.scalar
        def _(act):
            def high_in():
                if nxt is None:
                    return
                for m in range(HALVES):
                    nc.scalar.activation(SH[:, m, :, 0:SEQ], xh_c[:, m, nxt, :].bitcast(F32).rearrange(
                        "p (b s) -> p b s", b=CB), ACT.Copy).then_inc(in_hi, 1)

            def exponentials(p):
                if c is None:
                    return
                act.wait_ge(shifted, HALVES * (p + 1))
                nc.scalar.activation(PR[:, p % 2, :, 0:SEQ], PR[:, p % 2, :, 0:SEQ], ACT.Exp,
                                     scale=HD ** -0.5).then_inc(exped, 1)

            def copy_turned(p):
                if c is None:
                    return
                for q in range(2):
                    act.wait_ge(p_turned, 2 * p + q + 1)
                    if p >= 1 and q == 0:
                        act.wait_ge(out_t, p)
                    nc.scalar.activation(PT[:, 4 * q:4 * q + 4, :],
                                         bank[3 + q][:, :].rearrange("p (g t) -> p g t", g=4),
                                         ACT.Copy).then_inc(p_out, 1)

            def high_out(p):
                if c is None:
                    return
                act.wait_ge(out_t, p + 1)
                nc.scalar.activation(xh_c[:, :, c, 2 * p * SEQ:2 * (p + 1) * SEQ],
                                     out_bank(p).rearrange("p (m t) -> p m t", m=HALVES),
                                     ACT.Copy).then_inc(out_hi, 1)

            def values_out(p):
                if nxt is None:
                    return
                act.wait_ge(v_proj, p + 1)
                for s in range(2):
                    v4 = bank[6 + p % 2][half(s), 0:D].rearrange("p (g e d) -> p g e d", e=2, d=HD)
                    for e in range(2):
                        nc.scalar.activation(VBn[half(e), 2 * p + s, :, e * HD:(e + 1) * HD],
                                             v4[:, :, e, :], ACT.Copy).then_inc(v_out, 1)

            def keys_by_head(heads):
                if nxt is None:
                    return
                act.wait_ge(roped, 4)
                for h in heads:
                    nc.scalar.activation(KXn[:, 1, :, h, :], KT[:, 1], ACT.Copy,
                                         scale=hmask[:, h:h + 1]).then_inc(k_wide, 1)

            high_in()
            exponentials(0)
            exponentials(1)
            copy_turned(0)
            high_out(0)
            exponentials(2)
            copy_turned(1)
            high_out(1)
            exponentials(3)
            values_out(0)
            values_out(1)
            copy_turned(2)
            keys_by_head(range(0, 4))
            high_out(2)
            values_out(2)
            copy_turned(3)
            values_out(3)
            keys_by_head(range(4, HPH))
            high_out(3)

        @block.gpsimd
        def _(pool):
            def add_rotated(r):
                if nxt is None:
                    return
                m = r // 2
                dst = QTn[:, m, :, 0:SEQ] if r % 2 == 0 else KT[:, m]
                pool.wait_ge(roped_c, r + 1)
                pool.wait_ge(roped_s, r + 1)
                nc.gpsimd.tensor_tensor(dst, RC[:, r % 2], RS[:, r % 2], ALU.add).then_inc(roped, 1)

            def normalise(p):
                if c is None:
                    return
                pool.wait_ge(inverted, p + 1)
                nc.gpsimd.tensor_tensor(PR[:, p % 2, :, 0:SEQ], PR[:, p % 2, :, 0:SEQ],
                                        spread(RI[:, p % 2, :], 2, SEQ), ALU.mult).then_inc(normed, 1)

            normalise(0)
            add_rotated(0)
            add_rotated(1)
            normalise(1)
            add_rotated(2)
            normalise(2)
            add_rotated(3)
            normalise(3)


def mixture(nc, sb, bank, ins, RES, BN, MV, XH, XL, ident):
    with ExitStack() as ctx:
        G = sb(ctx, "gates", [P, TILES, EXPERTS])
        b1 = sb(ctx, "moe_b1", [P, EXPERTS, FB])
        w1 = sb(ctx, "moe_w1", [P, HALVES, FF])
        w2 = sb(ctx, "moe_w2", [P, FB, D])
        router(nc, sb, bank, ins, RES, G, XH, XL, ident, b1, w1, w2)
        w1h = sb(ctx, "moe_w1h", [P, HALVES, FF], F32R)
        w1l = sb(ctx, "moe_w1l", [P, HALVES, FF], F32R)
        w2h = sb(ctx, "moe_w2h", [P, FB, D], F32R)
        w2l = sb(ctx, "moe_w2l", [P, FB, D], F32R)
        H = sb(ctx, "hidden", [P, 4, MT * P])
        HH = sb(ctx, "hidden_hi", [P, 2, FB, MT * P], F32R)
        HL = sb(ctx, "hidden_lo", [P, 2, FB, MT * P], F32R)
        steps = [range(t, min(t + MT, TILES)) for t in range(0, TILES, MT)]
        split_weights(nc, "w1", [(w1[:], w1h[:], w1l[:])])

        with nc.Fori(0, EXPERTS) as e:
            with stage(nc, "w1_next", "w2_next", "w1_hi", "w1_lo", "w2_hi", "w2_lo", "up", "act", "h_hi", "h_lo",
                       "down", "gated") as (block, w1_next, w2_next, w1_hi, w1_lo, w2_hi, w2_lo,
                                            up, acted, h_hi, h_lo, down, gated):
                @block.sync
                def _(sp):
                    following = (e + 1) % EXPERTS
                    sp.dma_start(w1[:], ins["moe_w1"][following]).then_inc(w1_next, 16)
                    sp.wait_ge(w2_lo, 4)
                    sp.dma_start(w2[:], ins["moe_w2"][following]).then_inc(w2_next, 16)
                    sp.wait_ge(w2_next, 16)

                @block.tensor
                def _(pe):
                    def hidden(c):
                        n = len(steps[c]) * P
                        ts = slice(steps[c][0] * P, steps[c][0] * P + n)
                        for f in range(FB):
                            i = FB * c + f
                            if i >= 4:
                                pe.wait_ge(acted, i - 3)
                            passes = [x for k in range(HALVES) for x in split_products(
                                w1h[:, k, f * P:(f + 1) * P], w1l[:, k, f * P:(f + 1) * P],
                                XH[:, k, ts], XL[:, k, ts])]
                            for j, (left, right) in enumerate(passes):
                                mm = nc.tensor.matmul(bank[i % 4][:, 0:n], left, right,
                                                      start=(j == 0), stop=(j == len(passes) - 1))
                            mm.then_inc(up, 1)

                    def output(c):
                        pe.wait_ge(h_lo, FB * (c + 1))
                        if c == 0:
                            pe.wait_ge(w2_lo, 4)
                        for j, t in enumerate(steps[c]):
                            if t >= 4:
                                pe.wait_ge(gated, t - 3)
                            js = slice(j * P, (j + 1) * P)
                            passes = [x for f in range(FB) for x in split_products(
                                HH[:, c % 2, f, js], HL[:, c % 2, f, js], w2h[:, f, :], w2l[:, f, :])]
                            for n, (left, right) in enumerate(passes):
                                mm = nc.tensor.matmul(bank[4 + t % 4][:, 0:D], left, right,
                                                      start=(n == 0), stop=(n == len(passes) - 1))
                            mm.then_inc(down, 1)

                    hidden(0)
                    for c in range(len(steps)):
                        if c + 1 < len(steps):
                            hidden(c + 1)
                        output(c)

                @block.scalar
                def _(act):
                    for q in range(4):
                        nc.scalar.activation(w2h[:, 2 * q:2 * q + 2, :], w2[:, 2 * q:2 * q + 2, :],
                                             ACT.Copy).then_inc(w2_hi, 1)
                    for c, step in enumerate(steps):
                        n = len(step) * P
                        for f in range(FB):
                            i = FB * c + f
                            act.wait_ge(up, i + 1)
                            if i >= 4:
                                act.wait_ge(h_lo, i - 3)
                            nc.scalar.activation(H[:, i % 4, 0:n], bank[i % 4][:, 0:n], ACT.Relu,
                                                 bias=b1[:, e, f:f + 1]).then_inc(acted, 1)
                    act.wait_ge(w1_next, 16)
                    act.wait_ge(up, FB * len(steps))
                    nc.scalar.activation(w1h[:, :, :], w1[:, :, :], ACT.Copy).then_inc(w1_hi, 1)

                @block.vector
                def _(dve):
                    def gate(c):
                        for t in steps[c]:
                            dve.wait_ge(down, t + 1)
                            nc.vector.scalar_tensor_tensor(
                                out=RES[:, t, :], in0=bank[4 + t % 4][:, 0:D], scalar=G[:, t, bass.ds(e, 1)],
                                in1=RES[:, t, :], op0=ALU.mult, op1=ALU.add).then_inc(gated, 1)

                    for q in range(4):
                        dve.wait_ge(w2_hi, q + 1)
                        qs = slice(2 * q, 2 * q + 2)
                        nc.vector.tensor_tensor(w2l[:, qs, :], w2[:, qs, :], w2h[:, qs, :].bitcast(F32),
                                                ALU.subtract).then_inc(w2_lo, 1)
                    for c, step in enumerate(steps):
                        n = len(step) * P
                        if c >= 2:
                            dve.wait_ge(down, steps[c - 2][-1] + 1)
                        for f in range(FB):
                            i = FB * c + f
                            dve.wait_ge(acted, i + 1)
                            nc.vector.tensor_copy(HH[:, c % 2, f, 0:n], H[:, i % 4, 0:n]).then_inc(h_hi, 1)
                            dve.wait_ge(h_hi, i + 1)
                            nc.vector.tensor_tensor(HL[:, c % 2, f, 0:n], H[:, i % 4, 0:n],
                                                    HH[:, c % 2, f, 0:n].bitcast(F32),
                                                    ALU.subtract).then_inc(h_lo, 1)
                        if c >= 1:
                            gate(c - 1)
                    dve.wait_ge(w1_hi, 1)
                    nc.vector.tensor_tensor(w1l[:, :, :], w1[:, :, :], w1h[:, :, :].bitcast(F32),
                                            ALU.subtract).then_inc(w1_lo, 1)
                    gate(len(steps) - 1)


def router(nc, sb, bank, ins, RES, G, XH, XL, ident, b1, w1, w2):
    with ExitStack() as ctx:
        wr = sb(ctx, "wr", [P, HALVES, EXPERTS])
        wrh = sb(ctx, "wr_hi", [P, HALVES, EXPERTS], F32R)
        wrl = sb(ctx, "wr_lo", [P, HALVES, EXPERTS], F32R)
        br = sb(ctx, "br", [P, EXPERTS])
        b2 = sb(ctx, "moe_b2", [EXPERTS, D])
        ties = sb(ctx, "ties", [P, EXPERTS, EXPERTS])
        GT = sb(ctx, "gates_t", [EXPERTS, TILES, P])
        PB = sb(ctx, "router_probs", [P, TILES, EXPERTS])
        ST = sb(ctx, "router_stat", [P, 4, TILES])
        CUM = sb(ctx, "cumulated", [P, 2, TILES, EXPERTS])
        AH = sb(ctx, "ahead", [P, TILES, EXPERTS, EXPERTS])
        EQ = sb(ctx, "equal", [P, TILES, EXPERTS, EXPERTS])
        with stage(nc, "r_loaded", "r_w_next") as (block, loaded, w_next):
            @block.sync
            def _(sp):
                for dst, src in ((wr, "wr"), (br, "br"), (b2, "moe_b2"), (b1, "moe_b1")):
                    sp.dma_start(dst[:], ins[src]).then_inc(loaded, 16)
                sp.dma_start(ties[:].rearrange("p e j -> p (e j)"), ins["ties"]).then_inc(loaded, 16)
                sp.dma_start(w1[:], ins["moe_w1"][0]).then_inc(w_next, 16)
                sp.dma_start(w2[:], ins["moe_w2"][0]).then_inc(w_next, 16)
                sp.wait_ge(loaded, 80)
                sp.wait_ge(w_next, 32)
        split_weights(nc, "wr", [(wr[:], wrh[:], wrl[:])])

        with stage(nc, "logits", "r_step", "r_exp", "g_turned", "g_out", "b2_product", "b2_added") as (
                block, logits, step, exped, turned, g_out, product, added):
            @block.tensor
            def _(pe):
                def b2_term(t):
                    pe.wait_ge(g_out, t + 1)
                    if t >= 2:
                        pe.wait_ge(added, t - 1)
                    nc.tensor.matmul(bank[4 + t % 2][:, 0:D], GT[:, t, :], b2[:, :],
                                     start=True, stop=True).then_inc(product, 1)

                for t in range(TILES):
                    passes = [x for k in range(HALVES) for x in split_products(
                        XH[:, k, t * P:(t + 1) * P], XL[:, k, t * P:(t + 1) * P], wrh[:, k, :], wrl[:, k, :])]
                    for n, (left, right) in enumerate(passes):
                        mm = nc.tensor.matmul(bank[0][:, t * EXPERTS:(t + 1) * EXPERTS], left, right,
                                              start=(n == 0), stop=(n == len(passes) - 1))
                mm.then_inc(logits, 1)
                pe.wait_ge(step, 16)
                for t in range(TILES):
                    if t >= 2:
                        pe.wait_ge(g_out, t - 1)
                    nc.tensor.transpose(bank[1 + t % 2][0:EXPERTS, 0:P], G[:, t, :], ident[:, :]).then_inc(turned, 1)
                    if t >= 1:
                        b2_term(t - 1)
                b2_term(TILES - 1)

            @block.scalar
            def _(act):
                act.wait_ge(step, 3)
                nc.scalar.activation(PB[:], PB[:], ACT.Exp).then_inc(exped, 1)
                for t in range(TILES):
                    act.wait_ge(turned, t + 1)
                    nc.scalar.activation(GT[:, t, :], bank[1 + t % 2][0:EXPERTS, 0:P], ACT.Copy).then_inc(g_out, 1)

            @block.vector
            def _(dve):
                n = 0

                def then(ins):
                    nonlocal n
                    n += 1
                    ins.then_inc(step, 1)
                    dve.wait_ge(step, n)

                dve.wait_ge(logits, 1)
                then(nc.vector.tensor_tensor(PB[:], bank[0][:, 0:TILES * EXPERTS].rearrange(
                    "p (t e) -> p t e", e=EXPERTS), spread(br[:, :], 1, TILES), ALU.add))
                then(nc.vector.tensor_reduce(ST[:, 0, :], PB[:], AX.X, ALU.max))
                then(nc.vector.tensor_tensor(PB[:], PB[:], spread(ST[:, 0, :], 2, EXPERTS), ALU.subtract))
                dve.wait_ge(exped, 1)
                then(nc.vector.tensor_reduce(ST[:, 1, :], PB[:], AX.X, ALU.add))
                then(nc.vector.reciprocal(ST[:, 2, :], ST[:, 1, :]))
                then(nc.vector.tensor_tensor(PB[:], PB[:], spread(ST[:, 2, :], 2, EXPERTS), ALU.mult))
                other = spread(PB[:, :, :], 2, EXPERTS)
                own = spread(PB[:, :, :], 3, EXPERTS)
                then(nc.vector.tensor_tensor(EQ[:], other, own, ALU.is_equal))
                then(nc.vector.tensor_tensor(EQ[:], EQ[:], spread(ties[:, :, :], 1, TILES), ALU.mult))
                then(nc.vector.tensor_tensor(AH[:], other, own, ALU.is_gt))
                then(nc.vector.tensor_tensor(AH[:], AH[:], EQ[:], ALU.add))
                then(nc.vector.tensor_reduce(CUM[:, 0], AH[:], AX.X, ALU.add))
                then(nc.vector.tensor_scalar(CUM[:, 0], CUM[:, 0], 1.5, None, ALU.is_lt))
                then(nc.vector.tensor_tensor(AH[:], AH[:], other, ALU.mult))
                then(nc.vector.tensor_reduce(CUM[:, 1], AH[:], AX.X, ALU.add))
                then(nc.vector.scalar_tensor_tensor(out=CUM[:, 1].rearrange("p t e -> p (t e)"),
                                                    in0=CUM[:, 1].rearrange("p t e -> p (t e)"), scalar=0.8,
                                                    in1=CUM[:, 0].rearrange("p t e -> p (t e)"),
                                                    op0=ALU.is_lt, op1=ALU.max))
                then(nc.vector.tensor_tensor(G[:], PB[:], CUM[:, 1], ALU.mult))
                for t in range(TILES):
                    dve.wait_ge(product, t + 1)
                    nc.vector.tensor_tensor(RES[:, t, :], RES[:, t, :], bank[4 + t % 2][:, 0:D],
                                            ALU.add).then_inc(added, 1)


def tile_stats(nc, X, BN, MV, name):
    with stage(nc, name + "_bn", name + "_mv") as (block, bn_ready, mv_ready):
        @block.vector
        def _(dve):
            for t in range(TILES + 1):
                if t < TILES:
                    nc.vector.bn_stats(BN[:, t, :], X[:, t, :]).then_inc(bn_ready, 1)
                if t >= 1:
                    dve.wait_ge(bn_ready, t)
                    nc.vector.bn_aggr(MV[:, t - 1, :], BN[:, t - 1, :]).then_inc(mv_ready, 1)


QUARTER = IMAGES // 4
QC = QUARTER // CB


def delta_attention(nc, sb, bank, ins, RES, BN, MV, STD, XN, XH, XL, xh_c, xl_c, ident, identb, hmask):
    Q, K, GAMMA, F, O = range(5)
    with ExitStack() as ctx:
        wh = sb(ctx, "delta_wh", [P, 5, HALVES, D], F32R)
        wl = sb(ctx, "delta_wl", [P, 5, HALVES, D], F32R)
        wvfh = sb(ctx, "delta_wvfh", [P, HALVES, D + HEADS], F32R)
        wvfl = sb(ctx, "delta_wvfl", [P, HALVES, D + HEADS], F32R)
        wgh = sb(ctx, "delta_wgh", [P, HALVES, HD], F32R)
        wgl = sb(ctx, "delta_wgl", [P, HALVES, HD], F32R)
        wg2 = sb(ctx, "delta_wg2", [HD, D])
        identr = sb(ctx, "ident_r", [P, P], F32R)
        same = sb(ctx, "same_head", [P, P])
        after = sb(ctx, "after", [P, P])
        past = sb(ctx, "past", [P, SEQ], BF16)
        here = sb(ctx, "from_here", [P, SEQ])
        G1 = sb(ctx, "gate_low", [HD, TOKENS])
        delta_weights(nc, sb, ins, wh, wl, wvfh, wvfl, wgh, wgl, wg2, identr, same, after, past, here, ident)

        spans = [slice(t, min(t + 512, TOKENS)) for t in range(0, TOKENS, 512)]
        with stage(nc, "g1", "g1_out") as (block, g1_ready, g1_out):
            @block.tensor
            def _(pe):
                for i, ts in enumerate(spans):
                    if i >= 2:
                        pe.wait_ge(g1_out, i - 1)
                    passes = [x for k in range(HALVES) for x in split_products(
                        wgh[:, k, :], wgl[:, k, :], XH[:, k, ts], XL[:, k, ts])]
                    for n, (left, right) in enumerate(passes):
                        mm = nc.tensor.matmul(bank[i % 2][0:HD, 0:ts.stop - ts.start], left, right,
                                              start=(n == 0), stop=(n == len(passes) - 1))
                    mm.then_inc(g1_ready, 1)

            @block.scalar
            def _(act):
                for i, ts in enumerate(spans):
                    act.wait_ge(g1_ready, i + 1)
                    nc.scalar.activation(G1[:, ts], bank[i % 2][0:HD, 0:ts.stop - ts.start],
                                         ACT.Copy).then_inc(g1_out, 1)

        with ExitStack() as inner:
            PA = sb(inner, "qk_and_ak", [P, QUARTER, PAIRS, 2, SEQ])
            VH = sb(inner, "v_halves", [P, QUARTER, PAIRS, HD])
            even = chunk_buffers(sb, inner, 0)

            def quarter_step(quarter, more=True):
                with ExitStack() as own:
                    odd = chunk_buffers(sb, own, 1)
                    work = work_buffers(sb, own)
                    zero_pads(nc, "d_zero", (odd[0], odd[1], work["KX"]))
                    delta_step(nc, bank, wh, wl, wvfh, wvfl, same, after, past, here, identb, hmask, xh_c, xl_c,
                               PA, VH, work, True, quarter * QC + 1, 0, even, odd)
                    delta_step(nc, bank, wh, wl, wvfh, wvfl, same, after, past, here, identb, hmask, xh_c, xl_c,
                               PA, VH, work, True, quarter * QC + 2 if more else None, 1, odd, even)
                delta_solve(nc, sb, bank, ident, PA, VH, XH, XL, quarter)

            zero_pads(nc, "d_zero0", even[0:2])
            with ExitStack() as own:
                delta_step(nc, bank, wh, wl, wvfh, wvfl, same, after, past, here, identb, hmask, xh_c, xl_c,
                           PA, VH, work_buffers(sb, own), False, 0, 0, None, even)
            with nc.Fori(0, 3) as quarter:
                quarter_step(quarter)
            quarter_step(3, more=False)

        Y = sb(ctx, "gated_out", [P, TILES, D])
        SG = sb(ctx, "gate", [P, 2, D])
        with stage(nc, "o_tile", "g_tile", "gate_ready", "y_ready", "y_bn", "y_mv") as (
                block, o_ready, g_ready, gate_ready, y_ready, bn_ready, mv_ready):
            @block.tensor
            def _(pe):
                for t in range(TILES):
                    ts = slice(t * P, (t + 1) * P)
                    if t >= 2:
                        pe.wait_ge(gate_ready, t - 1)
                    nc.tensor.matmul(bank[4 + t % 2][:, 0:D], G1[:, ts], wg2[:, :],
                                     start=True, stop=True).then_inc(g_ready, 1)
                    if t >= 2:
                        pe.wait_ge(y_ready, t - 1)
                    for m in range(HALVES):
                        nc.tensor.matmul(bank[t % 2][:, m * P:(m + 1) * P], XH[:, m, ts], identr[:, :],
                                         start=True, stop=False)
                        mm = nc.tensor.matmul(bank[t % 2][:, m * P:(m + 1) * P], XL[:, m, ts], identr[:, :],
                                              start=False, stop=True)
                    mm.then_inc(o_ready, 1)

            @block.scalar
            def _(act):
                for t in range(TILES):
                    act.wait_ge(g_ready, t + 1)
                    if t >= 2:
                        act.wait_ge(y_ready, t - 1)
                    nc.scalar.activation(SG[:, t % 2, :], bank[4 + t % 2][:, 0:D],
                                         ACT.Sigmoid).then_inc(gate_ready, 1)

            @block.vector
            def _(dve):
                for t in range(TILES + 2):
                    if t < TILES:
                        dve.wait_ge(o_ready, t + 1)
                        dve.wait_ge(gate_ready, t + 1)
                        nc.vector.tensor_tensor(Y[:, t, :], bank[t % 2][:, 0:D], SG[:, t % 2, :],
                                                ALU.mult).then_inc(y_ready, 1)
                    if 1 <= t <= TILES:
                        dve.wait_ge(y_ready, t)
                        nc.vector.bn_stats(BN[:, t - 1, :], Y[:, t - 1, :]).then_inc(bn_ready, 1)
                    if t >= 2:
                        dve.wait_ge(bn_ready, t - 1)
                        nc.vector.bn_aggr(MV[:, t - 2, :], BN[:, t - 2, :]).then_inc(mv_ready, 1)
        layer_norm_turn(nc, bank, Y, STD, MV, XN, XH, XL, ident, "lno")
        add_product_and_stats(nc, bank, RES, BN, MV, XH, XL, wh[:, O], wl[:, O], "delta_o")


def delta_weights(nc, sb, ins, wh, wl, wvfh, wvfl, wgh, wgl, wg2, identr, same, after, past, here, ident):
    with ExitStack() as ctx:
        w = sb(ctx, "delta_w", [P, 5, HALVES, D])
        wvf = sb(ctx, "delta_wvf", [P, HALVES, D + HEADS])
        wg = sb(ctx, "delta_wg1", [P, HALVES, HD])
        nw = sb(ctx, "norm_w", [P, HALVES])
        with stage(nc, "d_loaded", "scaled") as (block, loaded, scaled):
            @block.sync
            def _(sp):
                for dst, src in ((w, "delta_w"), (wvf, "delta_wvf"), (wg, "delta_wg1"), (wg2, "delta_wg2"),
                                 (nw, "norm_w"), (same, "same_head"), (after, "after"), (past, "past"),
                                 (here, "from_here")):
                    sp.dma_start(dst[:], ins[src]).then_inc(loaded, 16)

            @block.vector
            def _(dve):
                dve.wait_ge(loaded, 16 * 9)
                nc.vector.tensor_copy(identr[:, :], ident[:, :]).then_inc(scaled, 1)
                for m in range(HALVES):
                    nc.vector.tensor_scalar(w[:, 4, m, :], w[:, 4, m, :], nw[:, m:m + 1], None,
                                            ALU.mult).then_inc(scaled, 1)
        split_weights(nc, "dw", [(w[:, n], wh[:, n], wl[:, n]) for n in range(5)]
                      + [(wvf[:], wvfh[:], wvfl[:]), (wg[:], wgh[:], wgl[:])])


def chunk_buffers(sb, ctx, i):
    return (sb(ctx, f"dchunk_hi{i}", [P, HALVES, CB, PAD], F32R),
            sb(ctx, f"dchunk_lo{i}", [P, HALVES, CB, PAD], F32R),
            sb(ctx, f"q_and_a{i}", [P, HALVES, CB, 2, SEQ]),
            sb(ctx, f"dk_t{i}", [P, HALVES, CB, SEQ]))


VALUE_BANKS = (6, 7, 4, 5)
NR = 2


def work_buffers(sb, ctx):
    return {
        "KQ": sb(ctx, "k_square_then_norm", [P, HALVES, CT]),
        "SQ": sb(ctx, "sig_qk", [P, 2, CT]),
        "GM": sb(ctx, "sig_gamma", [P, HALVES, CT]),
        "FM": sb(ctx, "sig_f", [P, HALVES, CT]),
        "KX": sb(ctx, "dk_by_head", [P, NR, PAIRS * 2, PAD]),
        "SV": sb(ctx, "sig_v", [P, IP, D]),
        "LZ": sb(ctx, "log_f", [P, 4, IP * HEADS]),
        "LF": sb(ctx, "log_f_pairs", [P, CB, PAIRS]),
        "MS": sb(ctx, "decay_steps", [P, 2, PAIRS, SEQ]),
        "DS": sb(ctx, "decay", [P, 2, PAIRS, SEQ]),
    }


def zero_pads(nc, name, tensors):
    with stage(nc, name) as (block, zeroed):
        @block.gpsimd
        def _(pool):
            for t in tensors[0::2]:
                nc.gpsimd.memset(t[:, :, :, SEQ:PAD].bitcast(F32), 0.0).then_inc(zeroed, 1)

        @block.vector
        def _(dve):
            for t in tensors[1::2]:
                nc.vector.memset(t[:, :, :, SEQ:PAD].bitcast(F32), 0.0).then_inc(zeroed, 1)


def delta_step(nc, bank, wh, wl, wvfh, wvfl, same, after, past, here, identb, hmask, xh_c, xl_c,
               PA, VH, work, attended, nxt, place, now, then):
    Q, K, GAMMA, F, O = range(5)
    KQ, SQ, GM, FM, KX, SV, LZ, LF, MS, DS = (work[n] for n in (
        "KQ", "SQ", "GM", "FM", "KX", "SV", "LZ", "LF", "MS", "DS"))
    NK = KQ
    if attended:
        SH, SL, QA, KT = now
    if nxt is not None:
        SHn, SLn, QAn, KTn = then
    jobs = ((K, 0), (K, 1), (Q, 0), (Q, 1), (GAMMA, 0), (F, 0), (GAMMA, 1), (F, 1))

    def half(s):
        return slice(s * PAD, (s + 1) * PAD)

    def pair(s, p, k):
        return s[:, k, 2 * p:2 * p + 2, :].rearrange("p b s -> p (b s)")

    def images(t):
        return t.rearrange("p (b s) -> p b s", b=CB)

    with stage(nc, "din_hi", "din_lo", "dproj", "sig", "silu", "k_sq", "k_n2", "k_max", "k_log", "k_inv",
               "k_unit", "gf", "qa_ready", "wide_v", "wide_p", "dv_proj", "dv_sig",
               "dv_out", "z_neg", "z_step", "z_act", "lf_ready", "steps_ready", "d_log", "d_exp",
               "dscores", "pa_ready") as (
            block, in_hi, in_lo, proj, sig, silu, k_sq, k_n2, k_max, k_log, k_inv,
            k_unit, gf, qa_ready, wide_v, wide_p, v_proj, v_sig,
            v_out, z_neg, z_step, z_act, lf_ready, steps_ready, d_log, d_exp,
            dscores, pa_ready):

        @block.tensor
        def _(pe):
            def project(n):
                if nxt is None:
                    return
                if n == 0:
                    pe.wait_ge(in_hi, HALVES)
                    pe.wait_ge(in_lo, HALVES)
                if n < 2 and attended:
                    pe.wait_ge(v_out, 4 * (n + 1))
                if 2 <= n < 6:
                    pe.wait_ge(silu, n - 1)
                if n >= 6:
                    pe.wait_ge(sig, n - 1)
                tensor, m = jobs[n]
                passes = [x for k in range(HALVES) for x in split_products(
                    wh[:, tensor, k, m * P:(m + 1) * P], wl[:, tensor, k, m * P:(m + 1) * P],
                    SHn[:, k, :, 0:SEQ], SLn[:, k, :, 0:SEQ])]
                for i, (left, right) in enumerate(passes):
                    mm = nc.tensor.matmul(bank[6 + n % 2][:, 0:CT], left, right,
                                          start=(i == 0), stop=(i == len(passes) - 1))
                mm.then_inc(proj, 1)

            def key_norm(m):
                if nxt is None:
                    return
                pe.wait_ge(k_sq, m + 1)
                if attended:
                    pe.wait_ge(v_out, 4 * (m + 3))
                nc.tensor.matmul(bank[4 + m][:, 0:CT], same[:, :], KQ[:, m, :],
                                 start=True, stop=True).then_inc(k_n2, 1)

            def values(p):
                if not attended:
                    return
                passes = [x for k in range(HALVES) for x in split_products(
                    pair(SH, p, k), pair(SL, p, k), wvfh[:, k, :], wvfl[:, k, :])]
                for i, (left, right) in enumerate(passes):
                    mm = nc.tensor.matmul(bank[VALUE_BANKS[p]][:, 0:D + HEADS], left, right,
                                          start=(i == 0), stop=(i == len(passes) - 1))
                mm.then_inc(v_proj, 1)

            def decay(b):
                if not attended:
                    return
                pe.wait_ge(steps_ready, b + 1)
                if b >= 2:
                    pe.wait_ge(d_exp, b - 1)
                elif nxt is not None:
                    pe.wait_ge(k_max, b + 1)
                else:
                    pe.wait_ge(v_out, 4 * (b + 3))
                nc.tensor.matmul(bank[4 + b % 2][:, 0:CT], identb[:, :], spread(past[:, :], 1, PAIRS),
                                 start=True, stop=False)
                nc.tensor.matmul(bank[4 + b % 2][:, 0:CT], after[:, :],
                                 MS[:, b % 2].rearrange("p g t -> p (g t)"),
                                 start=False, stop=True).then_inc(d_log, 1)

            def score(b):
                if not attended:
                    return
                for m in range(HALVES):
                    pe.wait_ge(wide_v if m == 0 else wide_p, b + 1)
                    if b >= 2:
                        pe.wait_ge(pa_ready, HALVES * (b - 2) + m + 1)
                    for g in range(PPH):
                        h = 2 * (PPH * m + g)
                        mm = nc.tensor.matmul(
                            bank[2 * (b % 2) + m][:, g * 2 * SEQ:(g + 1) * 2 * SEQ],
                            KX[:, b % NR, h:h + 2].rearrange("p e s -> p (e s)"),
                            QA[:, m, b].rearrange("p x t -> p (x t)"), start=True, stop=True)
                    mm.then_inc(dscores, 1)

            for p in range(IP):
                values(p)
            score(0)
            score(1)
            for n in range(6):
                project(n)
            key_norm(0)
            key_norm(1)
            project(6)
            project(7)
            decay(0)
            decay(1)
            for b in range(2, CB):
                decay(b)
                score(b)

        @block.scalar
        def _(act):
            if attended:
                act.wait_ge(z_step, 2 * IP)
                nc.scalar.activation(LZ[:, 1, :], LZ[:, 1, :], ACT.Exp).then_inc(z_act, 1)
                for p in range(IP):
                    act.wait_ge(v_proj, p + 1)
                    nc.scalar.activation(SV[:, p, :], bank[VALUE_BANKS[p]][:, 0:D], ACT.Sigmoid).then_inc(v_sig, 1)
            if nxt is not None:
                for n, (tensor, m) in enumerate(jobs):
                    act.wait_ge(proj, n + 1)
                    if n in (2, 3):
                        act.wait_ge(silu, n - 1)
                    dst = SQ[:, n % 2] if n < 4 else (GM if tensor == GAMMA else FM)[:, m]
                    nc.scalar.activation(dst, bank[6 + n % 2][:, 0:CT], ACT.Sigmoid).then_inc(sig, 1)
            if attended:
                act.wait_ge(z_step, 2 * IP + 1)
                nc.scalar.activation(LZ[:, 2, :], LZ[:, 2, :], ACT.Ln).then_inc(z_act, 1)
            if nxt is not None:
                for m in range(HALVES):
                    act.wait_ge(k_max, m + 1)
                    nc.scalar.activation(NK[:, m, :], NK[:, m, :], ACT.Ln).then_inc(k_log, 1)
                for m in range(HALVES):
                    act.wait_ge(k_log, m + 1)
                    nc.scalar.activation(NK[:, m, :], NK[:, m, :], ACT.Exp, scale=-0.5).then_inc(k_inv, 1)
            if attended:
                for b in range(CB):
                    act.wait_ge(d_log, b + 1)
                    if b >= 2:
                        act.wait_ge(pa_ready, HALVES * (b - 1))
                    nc.scalar.activation(DS[:, b % 2].rearrange("p g t -> p (g t)"),
                                         bank[4 + b % 2][:, 0:CT], ACT.Exp).then_inc(d_exp, 1)

        @block.vector
        def _(dve):
            def low_in():
                if nxt is None:
                    return
                for m in range(HALVES):
                    nc.vector.tensor_copy(SLn[:, m, :, 0:SEQ],
                                          images(xl_c[:, m, nxt, :].bitcast(F32))).then_inc(in_lo, 1)

            def forget_inputs(p):
                if not attended:
                    return
                dve.wait_ge(v_proj, p + 1)
                z = bank[VALUE_BANKS[p]][:, D:D + HEADS]
                zs = slice(p * HEADS, (p + 1) * HEADS)
                nc.vector.tensor_scalar(LZ[:, 0, zs], z, 0.0, None, ALU.min).then_inc(z_step, 1)
                nc.vector.tensor_scalar(LZ[:, 3, zs], z, -1.0, None, ALU.mult).then_inc(z_neg, 1)
                dve.wait_ge(z_neg, p + 1)
                nc.vector.tensor_tensor(LZ[:, 1, zs], z, LZ[:, 3, zs], ALU.min).then_inc(z_step, 1)

            def plus_one():
                if not attended:
                    return
                dve.wait_ge(z_act, 1)
                nc.vector.tensor_scalar(LZ[:, 2, :], LZ[:, 1, :], 1.0, None, ALU.add).then_inc(z_step, 1)

            def log_forget():
                if not attended:
                    return
                dve.wait_ge(z_act, 2)
                nc.vector.tensor_tensor(LZ[:, 3, :], LZ[:, 0, :], LZ[:, 2, :], ALU.subtract).then_inc(z_step, 1)
                dve.wait_ge(z_step, 2 * IP + 2)
                for s in range(2):
                    lz = LZ[half(s), 3, :].rearrange("p (i g e) -> p i g e", i=IP, e=2)
                    for e in range(2):
                        nc.vector.tensor_copy(LF[half(e)].rearrange("p (i s) g -> p i s g", s=2)[:, :, s, :],
                                              lz[:, :, :, e]).then_inc(lf_ready, 1)

            def silu_of(n):
                if nxt is None:
                    return
                tensor, m = jobs[n]
                dve.wait_ge(sig, n + 1)
                nc.vector.tensor_tensor(QAn[:, m, :, 0, :] if tensor == Q else KTn[:, m],
                                        images(bank[6 + n % 2][:, 0:CT]), images(SQ[:, n % 2]),
                                        ALU.mult).then_inc(silu, 1)

            def values_of(p):
                if not attended:
                    return
                dve.wait_ge(v_sig, p + 1)
                for s in range(2):
                    v4 = bank[VALUE_BANKS[p]][half(s), 0:D].rearrange("p (g e d) -> p g e d", e=2, d=HD)
                    s4 = SV[half(s), p, :].rearrange("p (g e d) -> p g e d", e=2, d=HD)
                    for e in range(2):
                        nc.vector.tensor_tensor(VH[half(e), place * CB + 2 * p + s], v4[:, :, e, :],
                                                s4[:, :, e, :], ALU.mult).then_inc(v_out, 1)

            def bounded(m):
                if nxt is None:
                    return
                dve.wait_ge(k_n2, m + 1)
                nc.vector.tensor_scalar(NK[:, m, :], bank[4 + m][:, 0:CT], 1e-24, None, ALU.max).then_inc(k_max, 1)

            def unit_key(m):
                if nxt is None:
                    return
                dve.wait_ge(k_inv, m + 1)
                flat = KTn[:, m].rearrange("p b s -> p (b s)")
                nc.vector.tensor_tensor(flat, flat, NK[:, m, :], ALU.mult).then_inc(k_unit, 1)

            def a_of(m):
                if nxt is None:
                    return
                dve.wait_ge(k_unit, m + 1)
                dve.wait_ge(gf, m + 1)
                nc.vector.scalar_tensor_tensor(
                    out=QAn[:, m, :, 1, :], in0=KTn[:, m], scalar=-1.0, in1=images(GM[:, m]),
                    op0=ALU.mult, op1=ALU.mult).then_inc(qa_ready, 1)

            def widen(b):
                if not attended or b >= CB:
                    return
                if b >= NR:
                    dve.wait_ge(dscores, HALVES * (b - NR) + 1)
                nc.vector.tensor_tensor(
                    KX[:, b % NR, 0:HPH, 0:SEQ], spread(KT[:, 0, b, :], 1, HPH), spread(hmask[:, :], 2, SEQ),
                    ALU.mult).then_inc(wide_v, 1)

            def weigh(b):
                if not attended:
                    return
                dve.wait_ge(d_exp, b + 1)
                for m in range(HALVES):
                    dve.wait_ge(dscores, HALVES * b + m + 1)
                    nc.vector.tensor_tensor(
                        PA[:, place * CB + b, PPH * m:PPH * (m + 1)],
                        bank[2 * (b % 2) + m][:, 0:CT].rearrange("p (g x t) -> p g x t", g=PPH, x=2),
                        spread(DS[:, b % 2, PPH * m:PPH * (m + 1)], 2, 2),
                        ALU.mult).then_inc(pa_ready, 1)

            low_in()
            widen(0)
            widen(1)
            for p in range(IP):
                forget_inputs(p)
            plus_one()
            for p in range(IP):
                values_of(p)
            for n in range(4):
                silu_of(n)
            bounded(0)
            bounded(1)
            widen(2)
            log_forget()
            unit_key(0)
            weigh(0)
            weigh(1)
            widen(3)
            unit_key(1)
            a_of(0)
            weigh(2)
            widen(4)
            a_of(1)
            for b in range(3, CB):
                weigh(b)
                widen(b + 2)

        @block.gpsimd
        def _(pool):
            def high_in():
                if nxt is None:
                    return
                for m in range(HALVES):
                    nc.gpsimd.tensor_copy(SHn[:, m, :, 0:SEQ],
                                          images(xh_c[:, m, nxt, :].bitcast(F32))).then_inc(in_hi, 1)

            def widen(b):
                if not attended:
                    return
                if b >= NR:
                    pool.wait_ge(dscores, HALVES * (b - NR) + 2)
                nc.gpsimd.tensor_tensor(
                    KX[:, b % NR, HPH:HEADS, 0:SEQ], spread(KT[:, 1, b, :], 1, HPH), spread(hmask[:, :], 2, SEQ),
                    ALU.mult).then_inc(wide_p, 1)

            def steps(b):
                if not attended:
                    return
                if b == 0:
                    pool.wait_ge(lf_ready, 4)
                if b >= 2:
                    pool.wait_ge(d_log, b - 1)
                nc.gpsimd.tensor_tensor(MS[:, b % 2], spread(LF[:, b, :], 2, SEQ),
                                        spread(here[:, :], 1, PAIRS), ALU.mult).then_inc(steps_ready, 1)

            def square(m):
                if nxt is None:
                    return
                pool.wait_ge(silu, m + 1)
                flat = KTn[:, m].rearrange("p b s -> p (b s)")
                nc.gpsimd.tensor_tensor(KQ[:, m, :], flat, flat, ALU.mult).then_inc(k_sq, 1)

            def gates(m):
                if nxt is None:
                    return
                pool.wait_ge(sig, 2 * m + 6)
                nc.gpsimd.tensor_tensor(GM[:, m, :], GM[:, m, :], FM[:, m, :], ALU.mult).then_inc(gf, 1)

            widen(0)
            high_in()
            widen(1)
            square(0)
            square(1)
            widen(2)
            gates(0)
            gates(1)
            steps(0)
            steps(1)
            for b in range(2, CB):
                steps(b)
                if b + 1 < CB:
                    widen(b + 1)


def delta_solve(nc, sb, bank, ident, PA, VH, XH, XL, quarter):
    DV = 11
    with ExitStack() as ctx:
        AS = sb(ctx, "a_rows", [P, SEQ, 2, SEQ])
        U = sb(ctx, "u", [P, 2, HD, PAD])
        UB = PA[:, :, :, 1, 0:2 * HD]
        AC = sb(ctx, "a_columns", [P, SEQ, 2, SEQ])
        PD = sb(ctx, "products", [P, 2, DV, SEQ])
        PP = sb(ctx, "pool_products", [P, 2, HD - DV, SEQ - 1])
        a_cols = PA[:].rearrange("p i g x t -> p (i g) x t")
        v_cols = VH[:].rearrange("p i g d -> p (i g) d")
        xh_q = XH[:, :, :].rearrange("p m (q t) -> p m q t", q=4)
        xl_q = XL[:, :, :].rearrange("p m (q t) -> p m q t", q=4)
        VG = HD // 4
        AG = (SEQ + 3) // 4
        OG = QUARTER // 4
        with stage(nc, "u_zero", "turned_in", "taken_in", "columns", "diagonal", "multiplied", "solved", "pool_multiplied",
                   "pool_solved",
                   "u_turned", "u_back", "u_back_v", "o_done", "o_hi", "o_lo") as (
                block, u_zero, turned_in, taken_in, columns, diagonal, multiplied, solved, pool_multiplied,
                pool_solved,
                u_turned, u_back, u_back_v, o_done, o_hi, o_lo):
            @block.tensor
            def _(pe):
                for i in range(VG + AG):
                    if i >= 4:
                        pe.wait_ge(taken_in, i - 3)
                    if i >= 4 + VG:
                        pe.wait_ge(columns, i - 3 - VG)
                    for j in range(4):
                        if i < VG:
                            col = v_cols[:, :, 4 * i + j]
                        else:
                            col = a_cols[:, :, 1, min(4 * (i - VG) + j, SEQ - 1)]
                        mm = nc.tensor.transpose(bank[i % 4][:, j * P:(j + 1) * P], col, ident[:, :])
                    mm.then_inc(turned_in, 1)
                pe.wait_ge(taken_in, VG + AG)
                pe.wait_ge(columns, AG)
                pe.wait_ge(solved, SEQ - 1)
                pe.wait_ge(pool_solved, SEQ - 1)
                for i in range(2 * VG):
                    if i >= 4:
                        pe.wait_ge(u_back if i % 2 == 0 else u_back_v, (i - 4) // 2 + 1)
                    for j in range(4):
                        mm = nc.tensor.transpose(bank[i % 4][0:PAD, j * P:(j + 1) * P],
                                                 U[:, i // VG, 4 * (i % VG) + j, :], ident[:, :])
                    mm.then_inc(u_turned, 1)
                pe.wait_ge(u_back, VG)
                pe.wait_ge(u_back_v, VG)
                pe.wait_ge(u_zero, 2)
                for o in range(OG):
                    if o >= 2:
                        pe.wait_ge(o_lo, o - 1)
                    for m in range(HALVES):
                        for j in range(4):
                            for g in range(PPH):
                                mm = nc.tensor.matmul(
                                    bank[4 + o % 2][32 * g:32 * g + 32, (4 * m + j) * SEQ:(4 * m + j + 1) * SEQ],
                                    UB[:, 4 * o + j, PPH * m + g, :], PA[:, 4 * o + j, PPH * m + g, 0, :],
                                    start=True, stop=True)
                    mm.then_inc(o_done, 1)

            @block.scalar
            def _(act):
                for i in range(VG + AG):
                    act.wait_ge(turned_in, i + 1)
                    src = bank[i % 4][:, :].rearrange("p (j e s) -> p j e s", j=4, e=2)
                    if i < VG:
                        nc.scalar.activation(U[:, :, 4 * i:4 * i + 4, :].rearrange("p e d s -> p d e s"),
                                             src, ACT.Copy).then_inc(taken_in, 1)
                    else:
                        n = min(4, SEQ - 4 * (i - VG))
                        ts = slice(4 * (i - VG), 4 * (i - VG) + n)
                        nc.scalar.activation(AS[:, ts], src[:, 0:n, :, 0:SEQ], ACT.Copy).then_inc(taken_in, 1)
                        nc.scalar.activation(AC[:, :, :, ts].rearrange("p s e t -> p t e s"),
                                             src[:, 0:n, :, 0:SEQ], ACT.Copy).then_inc(columns, 1)
                for e in range(2):
                    others = UB[e * PAD:(e + 1) * PAD, :, :, (1 - e) * HD:(2 - e) * HD]
                    nc.scalar.activation(others, others, ACT.Copy, scale=0.0).then_inc(u_zero, 1)
                for i in range(0, 2 * VG, 2):
                    act.wait_ge(u_turned, i + 1)
                    e, d = i // VG, 4 * (i % VG)
                    nc.scalar.activation(
                        UB[e * PAD:(e + 1) * PAD].rearrange("p i g c -> p c (i g)")[:, e * HD + d:e * HD + d + 4, :],
                        bank[i % 4][0:PAD, :].rearrange("p (j c) -> p j c", j=4), ACT.Copy).then_inc(u_back, 1)
                for o in range(OG):
                    act.wait_ge(o_done, o + 1)
                    nc.scalar.activation(xh_q[:, :, quarter, 4 * o * SEQ:4 * (o + 1) * SEQ],
                                         bank[4 + o % 2][:, 0:8 * SEQ].rearrange("p (m t) -> p m t", m=HALVES),
                                         ACT.Copy).then_inc(o_hi, 1)

            @block.vector
            def _(dve):
                def unit_diagonal(n):
                    dve.wait_ge(taken_in, VG + n + 1)
                    for t in range(4 * n, min(4 * n + 4, SEQ)):
                        last = nc.vector.memset(AS[:, t, :, t:t + 1], 1.0)
                    last.then_inc(diagonal, 1)

                unit_diagonal(0)
                for t in range(1, SEQ):
                    if t % 4 == 1 and t // 4 + 1 < AG:
                        unit_diagonal(t // 4 + 1)
                    dve.wait_ge(diagonal, t // 4 + 1)
                    if t >= 2:
                        dve.wait_ge(solved, t - 1)
                    nc.vector.tensor_tensor(PD[:, :, :, 0:t + 1], spread(AS[:, t, :, 0:t + 1], 2, DV),
                                            U[:, :, 0:DV, 0:t + 1], ALU.mult).then_inc(multiplied, 1)
                    dve.wait_ge(multiplied, t)
                    nc.vector.tensor_reduce(U[:, :, 0:DV, t], PD[:, :, :, 0:t + 1], AX.X,
                                            ALU.add).then_inc(solved, 1)
                for i in range(1, 2 * VG, 2):
                    dve.wait_ge(u_turned, i + 1)
                    e, d = i // VG, 4 * (i % VG)
                    nc.vector.tensor_copy(
                        UB[e * PAD:(e + 1) * PAD].rearrange("p i g c -> p c (i g)")[:, e * HD + d:e * HD + d + 4, :],
                        bank[i % 4][0:PAD, :].rearrange("p (j c) -> p j c", j=4)).then_inc(u_back_v, 1)
                for o in range(OG):
                    dve.wait_ge(o_hi, o + 1)
                    ts = slice(4 * o * SEQ, 4 * (o + 1) * SEQ)
                    nc.vector.tensor_tensor(xl_q[:, :, quarter, ts],
                                            bank[4 + o % 2][:, 0:8 * SEQ].rearrange("p (m t) -> p m t", m=HALVES),
                                            xh_q[:, :, quarter, ts].bitcast(F32), ALU.subtract).then_inc(o_lo, 1)

            @block.gpsimd
            def _(pool):
                pool.wait_ge(taken_in, VG)
                pool.wait_ge(columns, AG)
                for s in range(SEQ - 1):
                    later = slice(s + 1, SEQ)
                    if s >= 1:
                        pool.wait_ge(pool_solved, s)
                    nc.gpsimd.tensor_tensor(PP[:, :, :, s:SEQ - 1], spread(AC[:, s, :, later], 2, HD - DV),
                                            spread(U[:, :, DV:HD, s], 3, SEQ - 1 - s),
                                            ALU.mult).then_inc(pool_multiplied, 1)
                    pool.wait_ge(pool_multiplied, s + 1)
                    nc.gpsimd.tensor_tensor(U[:, :, DV:HD, later], U[:, :, DV:HD, later], PP[:, :, :, s:SEQ - 1],
                                            ALU.add).then_inc(pool_solved, 1)


def ternary_ffn(nc, sb, bank, ins, RES, XH, XL, out):
    with ExitStack() as ctx:
        w1t = sb(ctx, "w1_ternary", [P, HALVES, FF], F32R)
        w2t = sb(ctx, "w2_ternary", [P, FB, D], F32R)
        b1 = sb(ctx, "ffn_b1", [P, FB])
        b2 = sb(ctx, "ffn_b2", [P, D])
        with ExitStack() as raw:
            w1 = sb(raw, "ffn_w1", [P, HALVES, FF])
            w2 = sb(raw, "ffn_w2", [P, FB, D])
            up = sb(raw, "is_up", [P, HALVES * FF])
            down = sb(raw, "is_down", [P, HALVES * FF])
            ones = sb(raw, "ones", [P, P])
            S = sb(raw, "scales", [P, 4, 2])
            flat = (w1[:].rearrange("p k f -> p (k f)"), w2[:].rearrange("p f d -> p (f d)"))
            tern = (w1t[:].rearrange("p k f -> p (k f)"), w2t[:].rearrange("p f d -> p (f d)"))
            with stage(nc, "f_loaded", "f_step", "f_sum") as (block, loaded, step, total):
                @block.sync
                def _(sp):
                    for dst, src in ((w1, "ffn_w1"), (w2, "ffn_w2"), (b1, "ffn_b1"), (b2, "ffn_b2")):
                        sp.dma_start(dst[:], ins[src]).then_inc(loaded, 16)

                @block.tensor
                def _(pe):
                    pe.wait_ge(step, 3)
                    nc.tensor.matmul(bank[0][:, 0:2], ones[:, :], S[:, 0, :], start=True, stop=True).then_inc(total, 1)

                @block.vector
                def _(dve):
                    n = 0

                    def then(ins_):
                        nonlocal n
                        n += 1
                        ins_.then_inc(step, 1)
                        dve.wait_ge(step, n)

                    then(nc.vector.memset(ones[:], 1.0))
                    dve.wait_ge(loaded, 64)
                    for i in range(2):
                        then(nc.vector.tensor_reduce(S[:, 0, i:i + 1], flat[i], AX.X, ALU.add,
                                                     apply_absolute_value=True))
                    dve.wait_ge(total, 1)
                    then(nc.vector.tensor_scalar(S[:, 1, :], bank[0][:, 0:2], 1.0 / (D * FF), 1e-8,
                                                 ALU.mult, ALU.max))
                    then(nc.vector.tensor_scalar(S[:, 2, :], S[:, 1, :], 0.5, None, ALU.mult))
                    then(nc.vector.tensor_scalar(S[:, 3, :], S[:, 1, :], -0.5, None, ALU.mult))
                    for i in range(2):
                        then(nc.vector.tensor_scalar(up[:], flat[i], S[:, 2, i:i + 1], None, ALU.is_gt))
                        then(nc.vector.tensor_scalar(down[:], flat[i], S[:, 3, i:i + 1], None, ALU.is_lt))
                        then(nc.vector.tensor_tensor(tern[i], up[:], down[:], ALU.subtract))

        H = sb(ctx, "fhidden", [P, 4, MT * P])
        HH = sb(ctx, "fhidden_hi", [P, 2, FB, MT * P], F32R)
        HL = sb(ctx, "fhidden_lo", [P, 2, FB, MT * P], F32R)
        steps = [range(t, min(t + MT, TILES)) for t in range(0, TILES, MT)]
        with stage(nc, "f_up", "f_act", "f_hi", "f_lo", "f_down", "f_bias", "f_out", "stored") as (
                block, up_ready, acted, h_hi, h_lo, down_ready, biased, out_ready, stored):
            @block.tensor
            def _(pe):
                def hidden(c):
                    n = len(steps[c]) * P
                    ts = slice(steps[c][0] * P, steps[c][0] * P + n)
                    for f in range(FB):
                        i = FB * c + f
                        if i >= 4:
                            pe.wait_ge(acted, i - 3)
                        passes = [(w1t[:, k, f * P:(f + 1) * P], X[:, k, ts]) for k in range(HALVES) for X in (XH, XL)]
                        for j, (left, right) in enumerate(passes):
                            mm = nc.tensor.matmul(bank[i % 4][:, 0:n], left, right,
                                                  start=(j == 0), stop=(j == len(passes) - 1))
                        mm.then_inc(up_ready, 1)

                def output(c):
                    pe.wait_ge(h_lo, FB * (c + 1))
                    for j, t in enumerate(steps[c]):
                        if t >= 4:
                            pe.wait_ge(out_ready, t - 3)
                        passes = [(X[:, c % 2, f, j * P:(j + 1) * P], w2t[:, f, :]) for f in range(FB) for X in (HH, HL)]
                        for n, (left, right) in enumerate(passes):
                            mm = nc.tensor.matmul(bank[4 + t % 4][:, 0:D], left, right,
                                                  start=(n == 0), stop=(n == len(passes) - 1))
                        mm.then_inc(down_ready, 1)

                hidden(0)
                for c in range(len(steps)):
                    if c + 1 < len(steps):
                        hidden(c + 1)
                    output(c)

            @block.scalar
            def _(act):
                for c, st in enumerate(steps):
                    n = len(st) * P
                    for f in range(FB):
                        i = FB * c + f
                        act.wait_ge(up_ready, i + 1)
                        if i >= 4:
                            act.wait_ge(h_lo, i - 3)
                        nc.scalar.activation(H[:, i % 4, 0:n], bank[i % 4][:, 0:n], ACT.Gelu,
                                             bias=b1[:, f:f + 1]).then_inc(acted, 1)

            @block.vector
            def _(dve):
                def finish(c):
                    for t in steps[c]:
                        dve.wait_ge(down_ready, t + 1)
                        dve.wait_ge(biased, t + 1)
                        nc.vector.tensor_tensor(RES[:, t, :], RES[:, t, :], bank[4 + t % 4][:, 0:D],
                                                ALU.add).then_inc(out_ready, 1)

                for c, st in enumerate(steps):
                    n = len(st) * P
                    if c >= 2:
                        dve.wait_ge(down_ready, steps[c - 2][-1] + 1)
                    for f in range(FB):
                        i = FB * c + f
                        dve.wait_ge(acted, i + 1)
                        nc.vector.tensor_copy(HH[:, c % 2, f, 0:n], H[:, i % 4, 0:n]).then_inc(h_hi, 1)
                        dve.wait_ge(h_hi, i + 1)
                        nc.vector.tensor_tensor(HL[:, c % 2, f, 0:n], H[:, i % 4, 0:n],
                                                HH[:, c % 2, f, 0:n].bitcast(F32), ALU.subtract).then_inc(h_lo, 1)
                    if c >= 1:
                        finish(c - 1)
                finish(len(steps) - 1)

            @block.gpsimd
            def _(pool):
                for t in range(TILES):
                    nc.gpsimd.tensor_tensor(RES[:, t, :], RES[:, t, :], b2[:, :], ALU.add).then_inc(biased, 1)

            @block.sync
            def _(sp):
                for t in range(TILES):
                    sp.wait_ge(out_ready, t + 1)
                    sp.dma_start(out[t * P:(t + 1) * P, :], RES[:, t, :]).then_inc(stored, 16)
                sp.wait_ge(stored, 16 * TILES)



def _constants():
    one = np.float32
    base = one(10000.0)
    half = HD // 2
    inv_freq = one(1.0) / base ** (np.arange(half, dtype=np.float32) / one(half))
    ang = inv_freq[:, None] * np.arange(SEQ, dtype=np.float32)[None, :]
    cos = np.concatenate([np.cos(ang), np.cos(ang)], 0)
    sin = np.concatenate([-np.sin(ang), np.sin(ang)], 0)
    part = np.arange(P)
    step = np.arange(SEQ)
    row = part % PAD
    col = np.arange(P)
    same = (part[:, None] // PAD) == (col[None, :] // PAD)
    later = (part[:, None] % PAD) > (col[None, :] % PAD)
    real = (row[:, None] < SEQ) & ((col[None, :] % PAD) < SEQ)
    return {
        "ident": np.eye(P),
        "head_mask": (part[:, None] // HD) == np.arange(HPH)[None, :],
        "cos": np.tile(cos, (HPH, 1)),
        "sin": np.tile(sin, (HPH, 1)),
        "same_head": (part[:, None] // HD) == (col[None, :] // HD),
        "causal": np.where((row[:, None] < SEQ) & (step[None, :] > row[:, None]), MASKED, 0.0),
        "past": np.where((row[:, None] >= SEQ) | (step[None, :] < row[:, None]), MASKED, 0.0),
        "from_here": (row[:, None] <= step[None, :]),
        "after": same & later & real,
        "ties": np.tile((np.arange(EXPERTS)[None, :] <= np.arange(EXPERTS)[:, None]).reshape(1, -1), (P, 1)),
    }


def _lay_out(v):
    def rows(a):
        return a.reshape(-1, P, a.shape[-1]).transpose(1, 0, 2)

    def cols(a):
        return a.reshape(-1, P).T

    def swapped(a):
        return a.reshape(D, HEADS, 2, HD // 2)[:, :, ::-1].reshape(D, D)

    x = v["x"].reshape(IMAGES, 3, 6, 16, 6, 16).transpose(1, 3, 5, 0, 2, 4).reshape(KP, P, CHUNKS, CP)
    first = np.concatenate([v["cls_tok"].reshape(1, D), v["L0_tok_cls_token"].reshape(1, D),
                            np.repeat(v["L0_tok_b"].reshape(1, D), PATCHES, 0)], 0)
    wq, wk, wv, wo = (v[f"L0_attn_W{n}"].T for n in "qkvo")
    return {
        "patches": x.transpose(2, 1, 0, 3),
        "tok_w": rows(v["L0_tok_W"].T),
        "tok_bias": rows(first.T),
        "tok_pos": rows(v["L0_tok_pos_embedding"][0].T),
        "att_w": np.stack([rows(a) for a in (wq, swapped(wq), wk, swapped(wk), wv, wo)], 1),
        "wr": rows(v["L0_ffn_Wr"]),
        "br": np.repeat(v["L0_ffn_br"].reshape(1, EXPERTS), P, 0),
        "moe_w1": v["L0_ffn_W1"].reshape(EXPERTS, HALVES, P, FF).transpose(0, 2, 1, 3),
        "moe_b1": v["L0_ffn_b1"].reshape(EXPERTS, FB, P).transpose(2, 0, 1),
        "moe_w2": v["L0_ffn_W2"].reshape(EXPERTS, FB, P, D).transpose(0, 2, 1, 3),
        "moe_b2": v["L0_ffn_b2"],
        "delta_w": np.stack([rows(a) for a in (
            v["L1_attn_Wq"], v["L1_attn_Wk"], np.repeat(v["L1_attn_Wgamma"], HD, 1),
            np.repeat(v["L1_attn_Wf"], HD, 1), v["L1_attn_Wo"])], 1),
        "delta_wvf": rows(np.concatenate([v["L1_attn_Wv"], v["L1_attn_Wf"]], 1)),
        "delta_wg1": rows(v["L1_attn_Wg1"]),
        "delta_wg2": v["L1_attn_Wg2"],
        "norm_w": cols(v["L1_attn_norm_w"]),
        "ffn_w1": rows(v["L1_ffn_W1"].T),
        "ffn_b1": cols(v["L1_ffn_b1"]),
        "ffn_w2": rows(v["L1_ffn_W2"].T),
        "ffn_b2": np.repeat(v["L1_ffn_b2"].reshape(1, D), P, 0),
    }


def kernel(**inputs):
    import concourse.bacc as bacc
    from concourse.bass_utils import run_bass_kernel_spmd as run

    arrays = {n: np.ascontiguousarray(a) for n, a in _lay_out({k: np.asarray(a) for k, a in inputs.items()}).items()}
    for n, a in _constants().items():
        arrays[n] = np.ascontiguousarray(a, dtype=np.float32)
    for n, src in (("ident_bf16", "ident"), ("causal", "causal"), ("past", "past")):
        arrays[n] = arrays[src].astype(mybir.dt.np(BF16))
    nc = bacc.Bacc("TRN2", target_bir_lowering=False, num_devices=1)
    ins = {n: nc.dram_tensor(f"in_{n}", a.shape, mybir.dt.from_np(a.dtype), kind="ExternalInput").ap()
           for n, a in arrays.items()}
    out = nc.dram_tensor("out", (TOKENS, D), F32, kind="ExternalOutput").ap()
    build_tower(nc, ins, out)
    r = run(nc, [{f"in_{n}": a for n, a in arrays.items()}], core_ids=[0])
    return r.results[0]["out"].reshape(IMAGES, SEQ, D)
```

```python
from contextlib import ExitStack, contextmanager
from itertools import count

import numpy as np

import concourse.bass as bass
from concourse import mybir

F32 = mybir.dt.float32
F32R = mybir.dt.float32r
BF16 = mybir.dt.bfloat16
ALU = mybir.AluOpType
ACT = mybir.ActivationFunctionType
AX = mybir.AxisListType

P = 128
IMAGES = 64
SEQ = 38
PATCHES = SEQ - 2
D = 256
HALVES = D // P
HEADS = 16
PAIRS = HEADS // 2
HPH = HEADS // HALVES
PPH = PAIRS // HALVES
HD = D // HEADS
PAD = 64
TOKENS = IMAGES * SEQ
TILES = TOKENS // P
CHUNKS = 8
CB = IMAGES // CHUNKS
CT = CB * SEQ
CP = CB * PATCHES
IP = CB // 2
KP = 768 // P
EXPERTS = 8
FF = 1024
FB = FF // P
MT = 4
EPS = 1e-5
MASKED = -1e30


@contextmanager
def stage(nc, *names):
    with ExitStack() as own:
        sems = [own.enter_context(nc.semaphore(n)) for n in names]
        with nc.Block() as block:
            yield (block, *sems)
        numbers = sorted(s.num for s in sems)
        firsts = [n for n in numbers if n - 1 not in numbers]
        lasts = [n for n in numbers if n + 1 not in numbers]
        for first, last in zip(firsts, lasts):
            nc.sync.sem_clear(range(first, last + 1))
        nc.all_engine_barrier()


def spread(ap, axis, n):
    wide = ap.unsqueeze(axis)
    shape = list(wide.shape)
    shape[axis] = n
    return wide.broadcast_to(shape)


def split_products(hi_l, lo_l, hi_r, lo_r):
    return ((hi_l, hi_r), (hi_l, lo_r), (lo_l, hi_r))


def layer_norm_turn(nc, bank, RES, STD, MV, XN, XH, XL, ident, name, loads=(), splits=(),
                    prepare=None, pool_first=None, pool_work=None):
    xh = XH[:, :, 0:TOKENS]
    xl = XL[:, :, 0:TOKENS]
    first = TILES - len(splits) - 5
    with stage(nc, name + "_var", name + "_std", name + "_inv", name + "_normed", name + "_turned",
               name + "_hi", name + "_lo", name + "_loaded", name + "_prepared",
               name + "_w_hi", name + "_w_lo") as (
            block, var_ready, std_ready, inv_ready, normed, turned, hi_ready, lo_ready,
            loaded, prepared, w_hi, w_lo):
        if loads:
            @block.sync
            def _(sp):
                for dst, src in loads:
                    sp.dma_start(dst, src).then_inc(loaded, 16)
                sp.wait_ge(loaded, 16 * len(loads))

        if splits or pool_work:
            @block.gpsimd
            def _(pool):
                if pool_first:
                    pool_first(w_lo)
                for n, (raw, hi, lo) in enumerate(splits):
                    pool.wait_ge(w_hi, n + 1)
                    nc.gpsimd.tensor_tensor(lo, raw, hi.bitcast(F32), ALU.subtract).then_inc(w_lo, 1)
                if pool_work:
                    pool_work(pool, w_lo)

        @block.vector
        def _(dve):
            nc.vector.tensor_scalar(STD[:, 0, :], MV[:, :, 1], EPS, None, ALU.add).then_inc(var_ready, 1)
            dve.wait_ge(std_ready, 1)
            nc.vector.reciprocal(STD[:, 2, :], STD[:, 1, :]).then_inc(inv_ready, 1)
            dve.wait_ge(inv_ready, 1)

            def low_part(t):
                dve.wait_ge(hi_ready, t + 1)
                nc.vector.tensor_tensor(
                    xl[:, :, t * P:(t + 1) * P], bank[t % 4][:, 0:D].rearrange("p (m t) -> p m t", m=HALVES),
                    xh[:, :, t * P:(t + 1) * P].bitcast(F32), ALU.subtract).then_inc(lo_ready, 1)

            for t in range(TILES):
                if prepare and t == first - 1:
                    dve.wait_ge(loaded, 16 * len(loads))
                    prepare[0](prepared)
                if t >= 4:
                    dve.wait_ge(turned, t - 3)
                nc.vector.tensor_scalar(XN[:, t % 4, :], RES[:, t, :], MV[:, t, 0:1], STD[:, 2, t:t + 1],
                                        ALU.subtract, ALU.mult).then_inc(normed, 1)
                if t >= 2:
                    low_part(t - 2)
            low_part(TILES - 2)
            low_part(TILES - 1)

        @block.scalar
        def _(act):
            act.wait_ge(var_ready, 1)
            nc.scalar.activation(STD[:, 1, :], STD[:, 0, :], ACT.Sqrt).then_inc(std_ready, 1)
            for t in range(TILES):
                act.wait_ge(turned, t + 1)
                nc.scalar.activation(xh[:, :, t * P:(t + 1) * P],
                                     bank[t % 4][:, 0:D].rearrange("p (m t) -> p m t", m=HALVES),
                                     ACT.Copy).then_inc(hi_ready, 1)
                if t == first and splits:
                    act.wait_ge(loaded, 16 * len(loads))
                    if prepare:
                        act.wait_ge(prepared, prepare[1])
                if 0 <= t - first < len(splits):
                    raw, hi, lo = splits[t - first]
                    nc.scalar.activation(hi, raw, ACT.Copy).then_inc(w_hi, 1)

        @block.tensor
        def _(pe):
            for t in range(TILES):
                pe.wait_ge(normed, t + 1)
                if t >= 4:
                    pe.wait_ge(lo_ready, t - 3)
                for m in range(HALVES):
                    turn = nc.tensor.transpose(bank[t % 4][:, m * P:(m + 1) * P],
                                               XN[:, t % 4, m * P:(m + 1) * P], ident[:, :])
                turn.then_inc(turned, 1)


def add_product_and_stats(nc, bank, RES, BN, MV, OH, OL, wh, wl, name, pool_work=None):
    oh = OH[:, :, 0:TOKENS]
    ol = OL[:, :, 0:TOKENS]
    with stage(nc, name + "_product", name + "_sum", name + "_bn", name + "_mv", name + "_side") as (
            block, product, summed, bn_ready, mv_ready, side):
        if pool_work:
            @block.gpsimd
            def _(pool):
                pool_work(pool, side)

        @block.tensor
        def _(pe):
            for t in range(TILES):
                if t >= 4:
                    pe.wait_ge(summed, t - 3)
                passes = [x for k in range(HALVES) for x in split_products(
                    oh[:, k, t * P:(t + 1) * P], ol[:, k, t * P:(t + 1) * P], wh[:, k, :], wl[:, k, :])]
                for n, (left, right) in enumerate(passes):
                    mm = nc.tensor.matmul(bank[t % 4][:, 0:D], left, right,
                                          start=(n == 0), stop=(n == len(passes) - 1))
                mm.then_inc(product, 1)

        @block.vector
        def _(dve):
            for t in range(TILES + 2):
                if t < TILES:
                    dve.wait_ge(product, t + 1)
                    nc.vector.tensor_tensor(RES[:, t, :], RES[:, t, :], bank[t % 4][:, 0:D],
                                            ALU.add).then_inc(summed, 1)
                if 1 <= t <= TILES:
                    dve.wait_ge(summed, t)
                    nc.vector.bn_stats(BN[:, t - 1, :], RES[:, t - 1, :]).then_inc(bn_ready, 1)
                if t >= 2:
                    dve.wait_ge(bn_ready, t - 1)
                    nc.vector.bn_aggr(MV[:, t - 2, :], BN[:, t - 2, :]).then_inc(mv_ready, 1)


def build_tower(nc, ins, out):
    with ExitStack() as whole:
        numbers = count()

        def sb(ctx, name, shape, dt=F32):
            name = f"{name}_{next(numbers)}"
            return ctx.enter_context(nc.sbuf_tensor(name, shape, dt))

        bank = [whole.enter_context(nc.psum_tensor(f"bank{i}", [P, 512], F32)) for i in range(8)]
        RES = sb(whole, "residual", [P, TILES, D])
        XH = sb(whole, "x_hi", [P, HALVES, TOKENS], F32R)
        XL = sb(whole, "x_lo", [P, HALVES, TOKENS], F32R)
        BN = sb(whole, "bn", [P, TILES, 6])
        MV = sb(whole, "mean_var", [P, TILES, 2])
        STD = sb(whole, "std", [P, 3, TILES])
        XN = sb(whole, "normed_tiles", [P, 4, D])
        ident = sb(whole, "ident", [P, P])
        identb = sb(whole, "ident_bf16", [P, P], BF16)
        hmask = sb(whole, "head_mask", [P, HPH])
        xh_c = XH[:, :, :].rearrange("p m (c t) -> p m c t", c=CHUNKS)
        xl_c = XL[:, :, :].rearrange("p m (c t) -> p m c t", c=CHUNKS)

        tokens_stage(nc, sb, bank, ins, RES, BN, MV, ident, identb, hmask)
        softmax_attention(nc, sb, bank, ins, RES, BN, MV, STD, XN, XH, XL, xh_c, xl_c, ident, identb, hmask)
        mixture(nc, sb, bank, ins, RES, BN, MV, STD, XN, XH, XL, ident)
        last_layer(nc, sb, bank, ins, RES, BN, MV, STD, XN, XH, XL, xh_c, xl_c, ident, identb, hmask, out)


def tokens_stage(nc, sb, bank, ins, RES, BN, MV, ident, identb, hmask):
    with ExitStack() as ctx:
        x = sb(ctx, "patches", [P, CHUNKS, KP, CP])
        w = sb(ctx, "tok_w", [P, KP, D])
        wh = sb(ctx, "tok_wh", [P, KP, D], F32R)
        wl = sb(ctx, "tok_wl", [P, KP, D], F32R)
        XHI = [sb(ctx, f"patch_hi{i}", [P, KP, CP], F32R) for i in range(2)]
        XLO = [sb(ctx, f"patch_lo{i}", [P, KP, CP], F32R) for i in range(2)]
        table = sb(ctx, "tok_bias", [P, HALVES, SEQ])
        pos = sb(ctx, "tok_pos", [P, HALVES, SEQ - 1])
        ET = sb(ctx, "tokens_t", [P, HALVES, CHUNKS, CB, SEQ])

        with stage(nc, "loaded", "table_ready", "tokw_hi", "tokw_lo") as (
                block, loaded, table_ready, w_hi, w_lo):
            @block.sync
            def _(sp):
                for dst, src in ((w, "tok_w"), (table, "tok_bias"), (pos, "tok_pos"), (ident, "ident"),
                                 (identb, "ident_bf16"), (hmask, "head_mask")):
                    sp.dma_start(dst[:], ins[src]).then_inc(loaded, 16)
                for c in range(2):
                    sp.dma_start(x[:, c], ins["patches"][c]).then_inc(loaded, 16)
                sp.wait_ge(loaded, 16 * 8)

            @block.scalar
            def _(act):
                act.wait_ge(loaded, 16 * 8)
                for k in range(KP):
                    nc.scalar.activation(wh[:, k], w[:, k], ACT.Copy).then_inc(w_hi, 1)

            @block.vector
            def _(dve):
                dve.wait_ge(loaded, 16 * 8)
                nc.vector.tensor_tensor(table[:, :, 1:SEQ], table[:, :, 1:SEQ], pos[:, :, :],
                                        ALU.add).then_inc(table_ready, 1)
                for k in range(KP):
                    dve.wait_ge(w_hi, k + 1)
                    nc.vector.tensor_tensor(wl[:, k], w[:, k], wh[:, k].bitcast(F32),
                                            ALU.subtract).then_inc(w_lo, 1)

            @block.gpsimd
            def _(pool):
                pool.wait_ge(table_ready, 1)
                for m in range(HALVES):
                    nc.gpsimd.tensor_copy(
                        ET[:, m].rearrange("p c b s -> p (c b) s")[:, :, 0:2],
                        spread(table[:, m, 0:2], 1, IMAGES)).then_inc(table_ready, 1)

        def project(c, parity, split, load):
            xh, xl = XHI[parity], XLO[parity]
            xh_next, xl_next = XHI[1 - parity], XLO[1 - parity]
            with stage(nc, "patch_hi", "patch_lo", "tok_product", "tok_done", "x_loaded") as (
                    block, hi_ready, lo_ready, product, done, loaded):
                if load is not None:
                    @block.sync
                    def _(sp):
                        sp.dma_start(x[:, load], ins["patches"][load]).then_inc(loaded, 16)
                        sp.wait_ge(loaded, 16)

                if split is not None:
                    @block.scalar
                    def _(act):
                        for k in range(KP):
                            nc.scalar.activation(xh_next[:, k, :], x[:, split, k, :], ACT.Copy).then_inc(hi_ready, 1)

                @block.vector
                def _(dve):
                    if split is not None:
                        for k in range(KP):
                            dve.wait_ge(hi_ready, k + 1)
                            nc.vector.tensor_tensor(xl_next[:, k, :], x[:, split, k, :],
                                                    xh_next[:, k, :].bitcast(F32), ALU.subtract).then_inc(lo_ready, 1)
                    if c is not None:
                        for m in range(HALVES):
                            dve.wait_ge(product, m + 1)
                            nc.vector.tensor_tensor(
                                ET[:, m, c, :, 2:SEQ], bank[m][:, 0:CP].rearrange("p (b s) -> p b s", b=CB),
                                spread(table[:, m, 2:SEQ], 1, CB), ALU.add).then_inc(done, 1)

                if c is not None:
                    @block.tensor
                    def _(pe):
                        for m in range(HALVES):
                            passes = [x for k in range(KP) for x in split_products(
                                wh[:, k, m * P:(m + 1) * P], wl[:, k, m * P:(m + 1) * P], xh[:, k, :], xl[:, k, :])]
                            for n, (left, right) in enumerate(passes):
                                mm = nc.tensor.matmul(bank[m][:, 0:CP], left, right,
                                                      start=(n == 0), stop=(n == len(passes) - 1))
                            mm.then_inc(product, 1)

        project(None, 1, 0, None)
        with nc.Fori(0, CHUNKS // 2 - 1) as i:
            project(i * 2, 0, i * 2 + 1, i * 2 + 2)
            project(i * 2 + 1, 1, i * 2 + 2, i * 2 + 3)
        project(CHUNKS - 2, 0, CHUNKS - 1, None)
        project(CHUNKS - 1, 1, None, None)

        et = [ET[:, m].rearrange("p c b s -> p (c b s)") for m in range(HALVES)]
        with stage(nc, "tok_turned", "tok_res", "tok_bn", "tok_mv") as (
                block, turned, res_ready, bn_ready, mv_ready):
            @block.tensor
            def _(pe):
                for t in range(TILES):
                    if t >= 4:
                        pe.wait_ge(res_ready, t - 3)
                    for m in range(HALVES):
                        turn = nc.tensor.transpose(bank[t % 4][:, m * P:(m + 1) * P],
                                                   et[m][:, t * P:(t + 1) * P], ident[:, :])
                    turn.then_inc(turned, 1)

            @block.scalar
            def _(act):
                for t in range(TILES):
                    act.wait_ge(turned, t + 1)
                    nc.scalar.activation(RES[:, t, :], bank[t % 4][:, 0:D], ACT.Copy).then_inc(res_ready, 1)

            @block.vector
            def _(dve):
                for t in range(TILES + 1):
                    if t < TILES:
                        dve.wait_ge(res_ready, t + 1)
                        nc.vector.bn_stats(BN[:, t, :], RES[:, t, :]).then_inc(bn_ready, 1)
                    if t >= 1:
                        dve.wait_ge(bn_ready, t)
                        nc.vector.bn_aggr(MV[:, t - 1, :], BN[:, t - 1, :]).then_inc(mv_ready, 1)


def softmax_attention(nc, sb, bank, ins, RES, BN, MV, STD, XN, XH, XL, xh_c, xl_c, ident, identb, hmask):
    with ExitStack() as ctx:
        wh = sb(ctx, "att_wh", [P, 6, HALVES, D], F32R)
        wl = sb(ctx, "att_wl", [P, 6, HALVES, D], F32R)
        cos = sb(ctx, "cos", [P, SEQ])
        sin = sb(ctx, "sin", [P, SEQ])
        causal = sb(ctx, "causal", [P, SEQ], BF16)
        b = dict(wh=wh, wl=wl, cos=cos, sin=sin, causal=causal)
        b["SH"] = sb(ctx, "chunk_hi", [P, HALVES, CB, PAD], F32R)
        b["SL"] = sb(ctx, "chunk_lo", [P, HALVES, CB, PAD], F32R)
        b["RC"] = sb(ctx, "rope_cos", [P, 2, CB, SEQ])
        b["RS"] = sb(ctx, "rope_sin", [P, 2, CB, SEQ])
        b["KT"] = sb(ctx, "k_t", [P, HALVES, CB, SEQ])
        b["PR"] = sb(ctx, "probs", [P, 2, HEADS, PAD])
        b["PT"] = sb(ctx, "probs_t", [P, PAIRS, P])
        b["MX"] = sb(ctx, "row_max", [P, 2, HEADS])
        b["SM"] = sb(ctx, "row_sum", [P, 2, HEADS])
        b["RI"] = sb(ctx, "row_inv", [P, 2, HEADS])
        QT = [sb(ctx, f"q_t{i}", [P, HALVES, CB, PAD]) for i in range(2)]
        KX = [sb(ctx, f"k_by_head{i}", [P, HALVES, CB, HPH, SEQ]) for i in range(2)]
        VB = [sb(ctx, f"v_pairs{i}", [P, CB, PAIRS, 2 * HD]) for i in range(2)]

        with ExitStack() as raw:
            w = sb(raw, "att_w", [P, 6, HALVES, D])

            def zero(done):
                for t in (b["SH"][:].bitcast(F32), b["SL"][:].bitcast(F32), QT[0][:], QT[1][:], VB[0][:], VB[1][:],
                          b["PR"][:]):
                    nc.gpsimd.memset(t, 0.0).then_inc(done, 1)

            layer_norm_turn(nc, bank, RES, STD, MV, XN, XH, XL, ident, "ln0", pool_first=zero,
                            loads=[(dst[:], ins[src]) for dst, src in (
                                (w, "att_w"), (cos, "cos"), (sin, "sin"), (causal, "causal"))],
                            splits=[(w[:, n], wh[:, n], wl[:, n]) for n in range(6)])

        def step(attended, projected, parity):
            attention_step(nc, bank, xh_c, xl_c, ident, identb, hmask, b, attended, projected,
                           (QT[parity], KX[parity], VB[parity]), (QT[1 - parity], KX[1 - parity], VB[1 - parity]))

        step(None, 0, 1)
        with nc.Fori(0, CHUNKS // 2 - 1) as i:
            step(i * 2, i * 2 + 1, 0)
            step(i * 2 + 1, i * 2 + 2, 1)
        step(CHUNKS - 2, CHUNKS - 1, 0)
        step(CHUNKS - 1, None, 1)
        add_product_and_stats(nc, bank, RES, BN, MV, XH, XL, wh[:, 5], wl[:, 5], "att_o")


def attention_step(nc, bank, xh_c, xl_c, ident, identb, hmask, b, c, nxt, now, then):
    Q, QS, K, KS, V = range(5)
    wh, wl, cos, sin, causal = b["wh"], b["wl"], b["cos"], b["sin"], b["causal"]
    SH, SL, RC, RS, KT = b["SH"], b["SL"], b["RC"], b["RS"], b["KT"]
    PR, PT, MX, SM, RI = b["PR"], b["PT"], b["MX"], b["SM"], b["RI"]
    QT, KX, VB = now
    QTn, KXn, VBn = then
    jobs = ((Q, 0), (QS, 0), (K, 0), (KS, 0), (Q, 1), (QS, 1), (K, 1), (KS, 1))

    def half(s):
        return slice(s * PAD, (s + 1) * PAD)

    def out_bank(p):
        return bank[5][:, 0:4 * SEQ]

    with stage(nc, "in_hi", "in_lo", "proj", "roped_c", "roped_s", "roped", "k_wide",
               "v_proj", "v_out", "scores", "maxed", "shifted", "exped", "summed", "inverted",
               "normed", "p_turned", "p_out", "out_t", "out_hi", "out_lo") as (
            block, in_hi, in_lo, proj, roped_c, roped_s, roped, k_wide,
            v_proj, v_out, scores, maxed, shifted, exped, summed, inverted,
            normed, p_turned, p_out, out_t, out_hi, out_lo):

        @block.tensor
        def _(pe):
            def project(n):
                if nxt is None:
                    return
                if n == 0:
                    pe.wait_ge(in_hi, HALVES)
                    pe.wait_ge(in_lo, HALVES)
                if n >= 2:
                    pe.wait_ge(roped_c if n % 2 == 0 else roped_s, (n - 2) // 2 + 1)
                tensor, m = jobs[n]
                passes = [x for k in range(HALVES) for x in split_products(
                    wh[:, tensor, k, m * P:(m + 1) * P], wl[:, tensor, k, m * P:(m + 1) * P],
                    SH[:, k, :, 0:SEQ], SL[:, k, :, 0:SEQ])]
                for i, (left, right) in enumerate(passes):
                    mm = nc.tensor.matmul(bank[6 + n % 2][:, 0:CT], left, right,
                                          start=(i == 0), stop=(i == len(passes) - 1))
                mm.then_inc(proj, 1)

            def values(p):
                if nxt is None:
                    return
                if p < 2:
                    pe.wait_ge(roped_c if p == 0 else roped_s, 4)
                else:
                    pe.wait_ge(v_out, 4 * (p - 1))
                passes = [x for k in range(HALVES) for x in split_products(
                    SH[:, k, 2 * p:2 * p + 2, :].rearrange("p b s -> p (b s)"),
                    SL[:, k, 2 * p:2 * p + 2, :].rearrange("p b s -> p (b s)"),
                    wh[:, V, k, :], wl[:, V, k, :])]
                for i, (left, right) in enumerate(passes):
                    mm = nc.tensor.matmul(bank[6 + p % 2][:, 0:D], left, right,
                                          start=(i == 0), stop=(i == len(passes) - 1))
                mm.then_inc(v_proj, 1)

            def score(p):
                if c is None:
                    return
                for m in range(HALVES):
                    u = HALVES * p + m
                    sc = bank[u % 3]
                    if u >= 3:
                        pe.wait_ge(shifted, u - 2)
                    nc.tensor.matmul(sc[:, 0:CT], identb[:, :], spread(causal[:, :], 1, HPH),
                                     start=True, stop=True)
                    for s in range(2):
                        mm = nc.tensor.matmul(sc[half(s), 0:CT], QT[:, m, 2 * p + s, :],
                                              KX[:, m, 2 * p + s].rearrange("p h s -> p (h s)"),
                                              start=False, stop=True, skip_group_check=True)
                    mm.then_inc(scores, 1)

            def turn(p):
                if c is None:
                    return
                pe.wait_ge(normed, p + 1)
                for g in range(PAIRS):
                    if p >= 1 and g % 4 == 0:
                        pe.wait_ge(p_out, 2 * (p - 1) + g // 4 + 1)
                    mm = nc.tensor.transpose(
                        bank[3 + g // 4][:, (g % 4) * P:(g % 4 + 1) * P],
                        PR[:, p % 2, 2 * g:2 * g + 2, :].rearrange("p h k -> p (h k)"), ident[:, :])
                    if g % 4 == 3:
                        mm.then_inc(p_turned, 1)

            def attend(p):
                if c is None:
                    return
                if p >= 1:
                    pe.wait_ge(out_lo, p)
                for m in range(HALVES):
                    pe.wait_ge(p_out, 2 * p + m + 1)
                    for s in range(2):
                        for g in range(PPH):
                            mm = nc.tensor.matmul(
                                out_bank(p)[32 * g:32 * g + 32, (2 * m + s) * SEQ:(2 * m + s + 1) * SEQ],
                                VB[:, 2 * p + s, PPH * m + g, :], PT[:, PPH * m + g, s * PAD:s * PAD + SEQ],
                                start=True, stop=True)
                mm.then_inc(out_t, 1)

            score(0)
            project(0)
            project(1)
            score(1)
            project(2)
            project(3)
            turn(0)
            project(4)
            attend(0)
            score(2)
            project(5)
            project(6)
            turn(1)
            project(7)
            attend(1)
            score(3)
            values(0)
            turn(2)
            values(1)
            attend(2)
            values(2)
            turn(3)
            values(3)
            attend(3)

        @block.vector
        def _(dve):
            def low_in():
                if nxt is None:
                    return
                for m in range(HALVES):
                    nc.vector.tensor_copy(SL[:, m, :, 0:SEQ], xl_c[:, m, nxt, :].bitcast(F32).rearrange(
                        "p (b s) -> p b s", b=CB)).then_inc(in_lo, 1)

            def rope(r):
                if nxt is None:
                    return
                if r >= 2:
                    dve.wait_ge(roped, r - 1)
                dve.wait_ge(proj, 2 * r + 1)
                nc.vector.tensor_tensor(RC[:, r % 2], bank[6][:, 0:CT].rearrange("p (b s) -> p b s", b=CB),
                                        spread(cos[:, :], 1, CB), ALU.mult).then_inc(roped_c, 1)
                dve.wait_ge(proj, 2 * r + 2)
                nc.vector.tensor_tensor(RS[:, r % 2], bank[7][:, 0:CT].rearrange("p (b s) -> p b s", b=CB),
                                        spread(sin[:, :], 1, CB), ALU.mult).then_inc(roped_s, 1)

            def keys_by_head(m, heads):
                if nxt is None:
                    return
                dve.wait_ge(roped, 2 * m + 2)
                for h in heads:
                    nc.vector.tensor_scalar(KXn[:, m, :, h, :], KT[:, m], hmask[:, h:h + 1], None,
                                            ALU.mult).then_inc(k_wide, 1)

            def shift(p):
                if c is None:
                    return
                for m in range(HALVES):
                    u = HALVES * p + m
                    s3 = bank[u % 3][:, 0:CT].rearrange("p (h k) -> p h k", h=HPH)
                    hs = slice(HPH * m, HPH * (m + 1))
                    dve.wait_ge(scores, u + 1)
                    nc.vector.tensor_reduce(MX[:, p % 2, hs], s3, AX.X, ALU.max).then_inc(maxed, 1)
                    dve.wait_ge(maxed, u + 1)
                    if p >= 2:
                        dve.wait_ge(p_turned, HALVES * (p - 1))
                    nc.vector.tensor_tensor(PR[:, p % 2, hs, 0:SEQ], s3, spread(MX[:, p % 2, hs], 2, SEQ),
                                            ALU.subtract).then_inc(shifted, 1)

            def add_up(p):
                if c is None:
                    return
                dve.wait_ge(exped, p + 1)
                nc.vector.tensor_reduce(SM[:, p % 2, :], PR[:, p % 2, :, 0:SEQ], AX.X,
                                        ALU.add).then_inc(summed, 1)
                dve.wait_ge(summed, p + 1)
                nc.vector.reciprocal(RI[:, p % 2, :], SM[:, p % 2, :]).then_inc(inverted, 1)

            def low_out(p):
                if c is None:
                    return
                dve.wait_ge(out_hi, p + 1)
                ts = slice(2 * p * SEQ, 2 * (p + 1) * SEQ)
                nc.vector.tensor_tensor(xl_c[:, :, c, ts], out_bank(p).rearrange("p (m t) -> p m t", m=HALVES),
                                        xh_c[:, :, c, ts].bitcast(F32), ALU.subtract).then_inc(out_lo, 1)

            low_in()
            shift(0)
            rope(0)
            add_up(0)
            shift(1)
            rope(1)
            add_up(1)
            rope(2)
            low_out(0)
            shift(2)
            rope(3)
            add_up(2)
            keys_by_head(0, range(0, 4))
            shift(3)
            add_up(3)
            low_out(1)
            keys_by_head(0, range(4, HPH))
            low_out(2)
            keys_by_head(1, range(4, HPH))
            low_out(3)

        @block.scalar
        def _(act):
            def high_in():
                if nxt is None:
                    return
                for m in range(HALVES):
                    nc.scalar.activation(SH[:, m, :, 0:SEQ], xh_c[:, m, nxt, :].bitcast(F32).rearrange(
                        "p (b s) -> p b s", b=CB), ACT.Copy).then_inc(in_hi, 1)

            def exponentials(p):
                if c is None:
                    return
                act.wait_ge(shifted, HALVES * (p + 1))
                nc.scalar.activation(PR[:, p % 2, :, 0:SEQ], PR[:, p % 2, :, 0:SEQ], ACT.Exp,
                                     scale=HD ** -0.5).then_inc(exped, 1)

            def copy_turned(p):
                if c is None:
                    return
                for q in range(2):
                    act.wait_ge(p_turned, 2 * p + q + 1)
                    if p >= 1 and q == 0:
                        act.wait_ge(out_t, p)
                    nc.scalar.activation(PT[:, 4 * q:4 * q + 4, :],
                                         bank[3 + q][:, :].rearrange("p (g t) -> p g t", g=4),
                                         ACT.Copy).then_inc(p_out, 1)

            def high_out(p):
                if c is None:
                    return
                act.wait_ge(out_t, p + 1)
                nc.scalar.activation(xh_c[:, :, c, 2 * p * SEQ:2 * (p + 1) * SEQ],
                                     out_bank(p).rearrange("p (m t) -> p m t", m=HALVES),
                                     ACT.Copy).then_inc(out_hi, 1)

            def values_out(p):
                if nxt is None:
                    return
                act.wait_ge(v_proj, p + 1)
                for s in range(2):
                    v4 = bank[6 + p % 2][half(s), 0:D].rearrange("p (g e d) -> p g e d", e=2, d=HD)
                    for e in range(2):
                        nc.scalar.activation(VBn[half(e), 2 * p + s, :, e * HD:(e + 1) * HD],
                                             v4[:, :, e, :], ACT.Copy).then_inc(v_out, 1)

            def keys_by_head(heads):
                if nxt is None:
                    return
                act.wait_ge(roped, 4)
                for h in heads:
                    nc.scalar.activation(KXn[:, 1, :, h, :], KT[:, 1], ACT.Copy,
                                         scale=hmask[:, h:h + 1]).then_inc(k_wide, 1)

            high_in()
            exponentials(0)
            exponentials(1)
            copy_turned(0)
            high_out(0)
            copy_turned(1)
            exponentials(2)
            high_out(1)
            exponentials(3)
            copy_turned(2)
            values_out(0)
            values_out(1)
            high_out(2)
            keys_by_head(range(0, 4))
            values_out(2)
            copy_turned(3)
            values_out(3)
            high_out(3)

        @block.gpsimd
        def _(pool):
            def add_rotated(r):
                if nxt is None:
                    return
                m = r // 2
                dst = QTn[:, m, :, 0:SEQ] if r % 2 == 0 else KT[:, m]
                pool.wait_ge(roped_c, r + 1)
                pool.wait_ge(roped_s, r + 1)
                nc.gpsimd.tensor_tensor(dst, RC[:, r % 2], RS[:, r % 2], ALU.add).then_inc(roped, 1)

            def normalise(p):
                if c is None:
                    return
                pool.wait_ge(inverted, p + 1)
                nc.gpsimd.tensor_tensor(PR[:, p % 2, :, 0:SEQ], PR[:, p % 2, :, 0:SEQ],
                                        spread(RI[:, p % 2, :], 2, SEQ), ALU.mult).then_inc(normed, 1)

            normalise(0)
            add_rotated(0)
            add_rotated(1)
            normalise(1)
            add_rotated(2)
            normalise(2)
            add_rotated(3)
            normalise(3)


TOGETHER = 4


def mixture(nc, sb, bank, ins, RES, BN, MV, STD, XN, XH, XL, ident):
    with ExitStack() as ctx:
        G = sb(ctx, "gates", [P, TILES, EXPERTS])
        b1 = sb(ctx, "moe_b1", [P, EXPERTS, FB])
        w1 = sb(ctx, "moe_w1", [P, HALVES, FF])
        w2 = sb(ctx, "moe_w2", [P, FB, D])
        w1h = sb(ctx, "moe_w1h", [P, HALVES, FF], F32R)
        w1l = sb(ctx, "moe_w1l", [P, HALVES, FF], F32R)
        router(nc, sb, bank, ins, RES, MV, STD, XN, G, XH, XL, ident, b1, w1, w2, w1h, w1l)
        w2h = sb(ctx, "moe_w2h", [P, FB, D], F32R)
        w2l = sb(ctx, "moe_w2l", [P, FB, D], F32R)
        H = sb(ctx, "hidden", [P, 4, MT * P])
        HH = sb(ctx, "hidden_hi", [P, 2, FB, MT * P], F32R)
        HL = sb(ctx, "hidden_lo", [P, 2, FB, MT * P], F32R)
        spans = [range(t, min(t + MT, TILES)) for t in range(0, TILES, MT)]
        SP = len(spans)
        steps = [(x, c) for x in range(TOGETHER) for c in range(SP)]

        def tiles_before(k):
            return steps[k][0] * TILES + spans[steps[k][1]][0] if k < len(steps) else TOGETHER * TILES

        with nc.Fori(0, EXPERTS // TOGETHER) as group:
            with stage(nc, "w1_next", "w2_next", "w1_hi", "w1_lo", "w2_hi", "w2_lo", "up", "act", "h_hi", "h_lo",
                       "down", "gated", "moe_bn", "moe_mv") as (block, w1_next, w2_next, w1_hi, w1_lo, w2_hi, w2_lo,
                                            up, acted, h_hi, h_lo, down, gated, bn_ready,
                                            mv_ready):
                @block.sync
                def _(sp):
                    for x in range(TOGETHER):
                        following = (group * TOGETHER + (x + 1)) % EXPERTS
                        if x >= 1:
                            sp.wait_ge(w1_lo, x)
                        sp.dma_start(w1[:], ins["moe_w1"][following]).then_inc(w1_next, 16)
                        sp.wait_ge(w2_lo, 4 * (x + 1))
                        sp.dma_start(w2[:], ins["moe_w2"][following]).then_inc(w2_next, 16)
                    sp.wait_ge(w2_next, 16 * TOGETHER)

                @block.tensor
                def _(pe):
                    def hidden(k):
                        x, c = steps[k]
                        n = len(spans[c]) * P
                        ts = slice(spans[c][0] * P, spans[c][0] * P + n)
                        if c == 0 and x >= 1:
                            pe.wait_ge(w1_lo, x)
                        for f in range(FB):
                            i = FB * k + f
                            if i >= 4:
                                pe.wait_ge(acted, i - 3)
                            passes = [y for k2 in range(HALVES) for y in split_products(
                                w1h[:, k2, f * P:(f + 1) * P], w1l[:, k2, f * P:(f + 1) * P],
                                XH[:, k2, ts], XL[:, k2, ts])]
                            for j, (left, right) in enumerate(passes):
                                mm = nc.tensor.matmul(bank[i % 4][:, 0:n], left, right,
                                                      start=(j == 0), stop=(j == len(passes) - 1))
                            mm.then_inc(up, 1)

                    def output(k):
                        x, c = steps[k]
                        pe.wait_ge(h_lo, FB * (k + 1))
                        if c == 0:
                            pe.wait_ge(w2_lo, 4 * (x + 1))
                        for j, t in enumerate(spans[c]):
                            n = x * TILES + t
                            if n >= 4:
                                pe.wait_ge(gated, n - 3)
                            js = slice(j * P, (j + 1) * P)
                            passes = [y for f in range(FB) for y in split_products(
                                HH[:, k % 2, f, js], HL[:, k % 2, f, js], w2h[:, f, :], w2l[:, f, :])]
                            for i, (left, right) in enumerate(passes):
                                mm = nc.tensor.matmul(bank[4 + n % 4][:, 0:D], left, right,
                                                      start=(i == 0), stop=(i == len(passes) - 1))
                            mm.then_inc(down, 1)

                    hidden(0)
                    for k in range(len(steps)):
                        if k + 1 < len(steps):
                            hidden(k + 1)
                        output(k)

                @block.scalar
                def _(act):
                    for k, (x, c) in enumerate(steps):
                        if (k == 0 if x == 0 else c == 1):
                            if x >= 1:
                                act.wait_ge(w2_next, 16 * x)
                                act.wait_ge(down, TILES * x)
                            for q in range(4):
                                nc.scalar.activation(w2h[:, 2 * q:2 * q + 2, :], w2[:, 2 * q:2 * q + 2, :],
                                                     ACT.Copy).then_inc(w2_hi, 1)
                        n = len(spans[c]) * P
                        for f in range(FB):
                            i = FB * k + f
                            act.wait_ge(up, i + 1)
                            if i >= 4:
                                act.wait_ge(h_lo, i - 3)
                            nc.scalar.activation(H[:, i % 4, 0:n], bank[i % 4][:, 0:n], ACT.Relu,
                                                 bias=b1[:, group * TOGETHER + x, f:f + 1]).then_inc(acted, 1)
                        if c == SP - 1:
                            act.wait_ge(w1_next, 16 * (x + 1))
                            act.wait_ge(up, FB * (k + 1))
                            nc.scalar.activation(w1h[:, :, :], w1[:, :, :], ACT.Copy).then_inc(w1_hi, 1)

                @block.vector
                def _(dve):
                    def gate(k):
                        x, c = steps[k]
                        for t in spans[c]:
                            n = x * TILES + t
                            dve.wait_ge(down, n + 1)
                            nc.vector.scalar_tensor_tensor(
                                out=RES[:, t, :], in0=bank[4 + n % 4][:, 0:D],
                                scalar=G[:, t, bass.ds(group * TOGETHER + x, 1)],
                                in1=RES[:, t, :], op0=ALU.mult, op1=ALU.add).then_inc(gated, 1)
                        if x == TOGETHER - 1:
                            for t in spans[c]:
                                dve.wait_ge(gated, x * TILES + t + 1)
                                nc.vector.bn_stats(BN[:, t, :], RES[:, t, :]).then_inc(bn_ready, 1)
                            for t in spans[c]:
                                dve.wait_ge(bn_ready, t + 1)
                                nc.vector.bn_aggr(MV[:, t, :], BN[:, t, :]).then_inc(mv_ready, 1)

                    for k, (x, c) in enumerate(steps):
                        if (k == 0 if x == 0 else c == 1):
                            for q in range(4):
                                dve.wait_ge(w2_hi, 4 * x + q + 1)
                                qs = slice(2 * q, 2 * q + 2)
                                nc.vector.tensor_tensor(w2l[:, qs, :], w2[:, qs, :], w2h[:, qs, :].bitcast(F32),
                                                        ALU.subtract).then_inc(w2_lo, 1)
                        n = len(spans[c]) * P
                        if k >= 2:
                            dve.wait_ge(down, tiles_before(k - 1))
                        for f in range(FB):
                            i = FB * k + f
                            dve.wait_ge(acted, i + 1)
                            nc.vector.tensor_copy(HH[:, k % 2, f, 0:n], H[:, i % 4, 0:n]).then_inc(h_hi, 1)
                            dve.wait_ge(h_hi, i + 1)
                            nc.vector.tensor_tensor(HL[:, k % 2, f, 0:n], H[:, i % 4, 0:n],
                                                    HH[:, k % 2, f, 0:n].bitcast(F32),
                                                    ALU.subtract).then_inc(h_lo, 1)
                        if c == SP - 1:
                            dve.wait_ge(w1_hi, x + 1)
                            nc.vector.tensor_tensor(w1l[:, :, :], w1[:, :, :], w1h[:, :, :].bitcast(F32),
                                                    ALU.subtract).then_inc(w1_lo, 1)
                        if k >= 1:
                            gate(k - 1)
                    gate(len(steps) - 1)


def router(nc, sb, bank, ins, RES, MV, STD, XN, G, XH, XL, ident, b1, w1, w2, w1h, w1l):
    with ExitStack() as ctx:
        wr = sb(ctx, "wr", [P, HALVES, EXPERTS])
        wrh = sb(ctx, "wr_hi", [P, HALVES, EXPERTS], F32R)
        wrl = sb(ctx, "wr_lo", [P, HALVES, EXPERTS], F32R)
        br = sb(ctx, "br", [P, EXPERTS])
        b2 = sb(ctx, "moe_b2", [EXPERTS, D])
        ties = sb(ctx, "ties", [P, EXPERTS, EXPERTS])
        GT = sb(ctx, "gates_t", [EXPERTS, TILES, P])
        PB = sb(ctx, "router_probs", [P, TILES, EXPERTS])
        ST = sb(ctx, "router_stat", [P, 4, TILES])
        CUM = sb(ctx, "cumulated", [P, 2, TILES, EXPERTS])
        AH = sb(ctx, "ahead", [P, TILES, EXPERTS, EXPERTS])
        EQ = sb(ctx, "equal", [P, TILES, EXPERTS, EXPERTS])
        layer_norm_turn(nc, bank, RES, STD, MV, XN, XH, XL, ident, "ln1",
                        loads=[(wr[:], ins["wr"]), (w1[:], ins["moe_w1"][0]), (br[:], ins["br"]),
                               (b2[:], ins["moe_b2"]), (b1[:], ins["moe_b1"]),
                               (ties[:].rearrange("p e j -> p (e j)"), ins["ties"]), (w2[:], ins["moe_w2"][0])],
                        splits=[(wr[:], wrh[:], wrl[:]),
                                (w1[:, 0], w1h[:, 0], w1l[:, 0]), (w1[:, 1], w1h[:, 1], w1l[:, 1])])

        flat = GT[:].rearrange("e t p -> e (t p)")
        spans = [slice(t, min(t + 512, TOKENS)) for t in range(0, TOKENS, 512)]
        groups = [range(t, min(t + 4, TILES)) for t in range(0, TILES, 4)]
        with stage(nc, "logits_t", "l_out", "logits", "r_step", "r_exp", "g_turned", "g_out", "b2_product",
                   "b2_added") as (block, logits_t, l_out, logits, step, exped, turned, g_out, product, added):
            @block.tensor
            def _(pe):
                for i, ts in enumerate(spans):
                    if i >= 2:
                        pe.wait_ge(l_out, i - 1)
                    passes = [x for k in range(HALVES) for x in split_products(
                        wrh[:, k, :], wrl[:, k, :], XH[:, k, ts], XL[:, k, ts])]
                    for n, (left, right) in enumerate(passes):
                        mm = nc.tensor.matmul(bank[1 + i % 2][0:EXPERTS, 0:ts.stop - ts.start], left, right,
                                              start=(n == 0), stop=(n == len(passes) - 1))
                    mm.then_inc(logits_t, 1)
                pe.wait_ge(l_out, len(spans))
                for t in range(TILES):
                    mm = nc.tensor.transpose(bank[0][:, t * EXPERTS:(t + 1) * EXPERTS], GT[:, t, :],
                                             ident[0:EXPERTS, 0:EXPERTS])
                mm.then_inc(logits, 1)
                pe.wait_ge(step, 16)
                for q, group in enumerate(groups):
                    if q >= 2:
                        pe.wait_ge(g_out, q - 1)
                    for j, t in enumerate(group):
                        mm = nc.tensor.transpose(bank[1 + q % 2][0:EXPERTS, j * P:(j + 1) * P], G[:, t, :],
                                                 ident[:, :])
                    mm.then_inc(turned, 1)
                for t in range(TILES):
                    pe.wait_ge(g_out, t // 4 + 1)
                    if t >= 4:
                        pe.wait_ge(added, t - 3)
                    nc.tensor.matmul(bank[4 + t % 4][:, 0:D], GT[:, t, :], b2[:, :],
                                     start=True, stop=True).then_inc(product, 1)

            @block.scalar
            def _(act):
                for i, ts in enumerate(spans):
                    act.wait_ge(logits_t, i + 1)
                    nc.scalar.activation(flat[:, ts], bank[1 + i % 2][0:EXPERTS, 0:ts.stop - ts.start],
                                         ACT.Copy).then_inc(l_out, 1)
                act.wait_ge(step, 3)
                nc.scalar.activation(PB[:], PB[:], ACT.Exp).then_inc(exped, 1)
                for q, group in enumerate(groups):
                    act.wait_ge(turned, q + 1)
                    nc.scalar.activation(flat[:, group[0] * P:(group[-1] + 1) * P],
                                         bank[1 + q % 2][0:EXPERTS, 0:len(group) * P], ACT.Copy).then_inc(g_out, 1)

            @block.vector
            def _(dve):
                n = 0

                def then(ins):
                    nonlocal n
                    n += 1
                    ins.then_inc(step, 1)
                    dve.wait_ge(step, n)

                dve.wait_ge(logits, 1)
                then(nc.vector.tensor_tensor(PB[:], bank[0][:, 0:TILES * EXPERTS].rearrange(
                    "p (t e) -> p t e", e=EXPERTS), spread(br[:, :], 1, TILES), ALU.add))
                then(nc.vector.tensor_reduce(ST[:, 0, :], PB[:], AX.X, ALU.max))
                then(nc.vector.tensor_tensor(PB[:], PB[:], spread(ST[:, 0, :], 2, EXPERTS), ALU.subtract))
                dve.wait_ge(exped, 1)
                then(nc.vector.tensor_reduce(ST[:, 1, :], PB[:], AX.X, ALU.add))
                then(nc.vector.reciprocal(ST[:, 2, :], ST[:, 1, :]))
                then(nc.vector.tensor_tensor(PB[:], PB[:], spread(ST[:, 2, :], 2, EXPERTS), ALU.mult))
                other = spread(PB[:, :, :], 2, EXPERTS)
                own = spread(PB[:, :, :], 3, EXPERTS)
                then(nc.vector.tensor_tensor(EQ[:], other, own, ALU.is_equal))
                then(nc.vector.tensor_tensor(EQ[:], EQ[:], spread(ties[:, :, :], 1, TILES), ALU.mult))
                then(nc.vector.tensor_tensor(AH[:], other, own, ALU.is_gt))
                then(nc.vector.tensor_tensor(AH[:], AH[:], EQ[:], ALU.add))
                then(nc.vector.tensor_reduce(CUM[:, 0], AH[:], AX.X, ALU.add))
                then(nc.vector.tensor_scalar(CUM[:, 0], CUM[:, 0], 1.5, None, ALU.is_lt))
                then(nc.vector.tensor_tensor(AH[:], AH[:], other, ALU.mult))
                then(nc.vector.tensor_reduce(CUM[:, 1], AH[:], AX.X, ALU.add))
                then(nc.vector.scalar_tensor_tensor(out=CUM[:, 1].rearrange("p t e -> p (t e)"),
                                                    in0=CUM[:, 1].rearrange("p t e -> p (t e)"), scalar=0.8,
                                                    in1=CUM[:, 0].rearrange("p t e -> p (t e)"),
                                                    op0=ALU.is_lt, op1=ALU.max))
                then(nc.vector.tensor_tensor(G[:], PB[:], CUM[:, 1], ALU.mult))
                for t in range(TILES):
                    dve.wait_ge(product, t + 1)
                    nc.vector.tensor_tensor(RES[:, t, :], RES[:, t, :], bank[4 + t % 4][:, 0:D],
                                            ALU.add).then_inc(added, 1)


QUARTER = IMAGES // 4
QC = QUARTER // CB


GATE_PARTS = (slice(0, HD), slice(32, 32 + HD), slice(64, 64 + HD))
GATE_ROWS = 64 + HD


def last_layer(nc, sb, bank, ins, RES, BN, MV, STD, XN, XH, XL, xh_c, xl_c, ident, identb, hmask, out):
    Q, K, GAMMA, F, O = range(5)
    with ExitStack() as ctx:
        identr = sb(ctx, "ident_r", [P, P], F32R)
        wh = sb(ctx, "delta_wh", [P, 5, HALVES, D], F32R)
        wl = sb(ctx, "delta_wl", [P, 5, HALVES, D], F32R)
        wvfh = sb(ctx, "delta_wvfh", [P, HALVES, D + HEADS], F32R)
        wvfl = sb(ctx, "delta_wvfl", [P, HALVES, D + HEADS], F32R)
        wgh = sb(ctx, "delta_wgh", [P, HALVES, HD], F32R)
        wgl = sb(ctx, "delta_wgl", [P, HALVES, HD], F32R)
        wg2 = sb(ctx, "delta_wg2", [HD, D])
        same = sb(ctx, "same_head", [P, P])
        after = sb(ctx, "after", [P, P])
        past = sb(ctx, "past", [P, SEQ], BF16)
        here = sb(ctx, "from_here", [P, SEQ])
        G1 = sb(ctx, "gate_low", [GATE_ROWS, TOKENS], F32R)
        wg2s = sb(ctx, "delta_wg2_parts", [GATE_ROWS, D], F32R)
        nw = sb(ctx, "norm_w", [P, HALVES])
        with ExitStack() as raw:
            w = sb(raw, "delta_w", [P, 5, HALVES, D])
            wvf = sb(raw, "delta_wvf", [P, HALVES, D + HEADS])
            wg = sb(raw, "delta_wg1", [P, HALVES, HD])

            def norm_into_output(scaled):
                for m in range(HALVES):
                    nc.vector.tensor_scalar(w[:, 4, m, :], w[:, 4, m, :], nw[:, m:m + 1], None,
                                            ALU.mult).then_inc(scaled, 1)
                nc.vector.tensor_copy(identr[:, :], ident[:, :]).then_inc(scaled, 1)

            def zero_gate(done):
                nc.gpsimd.memset(G1[:].bitcast(F32), 0.0).then_inc(done, 1)
                nc.gpsimd.memset(wg2s[:].bitcast(F32), 0.0).then_inc(done, 1)

            layer_norm_turn(nc, bank, RES, STD, MV, XN, XH, XL, ident, "ln2", 
                            prepare=(norm_into_output, 3), pool_first=zero_gate,
                            loads=[(dst[:], ins[src]) for dst, src in (
                                (w, "delta_w"), (wvf, "delta_wvf"), (wg, "delta_wg1"), (wg2, "delta_wg2"),
                                (nw, "norm_w"), (same, "same_head"), (after, "after"), (past, "past"),
                                (here, "from_here"))],
                            splits=[(wg[:], wgh[:], wgl[:]), (wvf[:], wvfh[:], wvfl[:])]
                            + [(w[:, n], wh[:, n], wl[:, n]) for n in range(5)])

        with ExitStack() as inner:
            PA = sb(inner, "qk_and_ak", [P, QUARTER, PAIRS, 2, SEQ])
            VH = sb(inner, "v_halves", [P, QUARTER, PAIRS, HD])
            even = chunk_buffers(sb, inner, 0)

            def quarter_step(quarter, more=True):
                with ExitStack() as own:
                    odd = chunk_buffers(sb, own, 1)
                    work = work_buffers(sb, own)
                    zero_pads(nc, "d_zero", (odd[0], odd[1], work["KX"]))
                    delta_step(nc, bank, wh, wl, wvfh, wvfl, same, after, past, here, identb, hmask, xh_c, xl_c,
                               PA, VH, work, True, quarter * QC + 1, 0, even, odd)
                    delta_step(nc, bank, wh, wl, wvfh, wvfl, same, after, past, here, identb, hmask, xh_c, xl_c,
                               PA, VH, work, True, quarter * QC + 2 if more else None, 1, odd, even)
                delta_solve(nc, sb, bank, ident, PA, VH, XH, XL, quarter)

            zero_pads(nc, "d_zero0", even[0:2])
            with ExitStack() as own:
                delta_step(nc, bank, wh, wl, wvfh, wvfl, same, after, past, here, identb, hmask, xh_c, xl_c,
                           PA, VH, work_buffers(sb, own), False, 0, 0, None, even, (wgh, wgl, XH, XL, G1, wg2, wg2s))
            with nc.Fori(0, 3) as quarter:
                quarter_step(quarter)
            quarter_step(3, more=False)

        w1t = sb(ctx, "w1_ternary", [P, HALVES, FF], F32R)
        w2t = sb(ctx, "w2_ternary", [P, FB, D], F32R)
        b1 = sb(ctx, "ffn_b1", [P, FB])
        b2 = sb(ctx, "ffn_b2", [P, D])
        with ExitStack() as own:
            w1 = sb(own, "ffn_w1", [P, HALVES, FF])
            w2 = sb(own, "ffn_w2", [P, FB, D])
            up = sb(own, "is_up", [P, HALVES * FF])
            down = sb(own, "is_down", [P, HALVES * FF])
            ones = sb(own, "ones", [P, P])
            S = sb(own, "scales", [P, 4, 2])
            flat = (w1[:].rearrange("p k f -> p (k f)"), w2[:].rearrange("p f d -> p (f d)"))
            tern = (w1t[:].rearrange("p k f -> p (k f)"), w2t[:].rearrange("p f d -> p (f d)"))
            Y = sb(own, "gated_out", [P, TILES, D])
            SG = sb(own, "gate", [P, 4, D])
            with stage(nc, "o_tile", "g_tile", "gate_ready", "y_ready", "y_bn", "y_mv", "f_loaded", "f_step",
                       "f_sum") as (
                    block, o_ready, g_ready, gate_ready, y_ready, bn_ready, mv_ready, loaded, step, total):
                @block.sync
                def _(sp):
                    for dst, src in ((w1, "ffn_w1"), (w2, "ffn_w2"), (b1, "ffn_b1"), (b2, "ffn_b2")):
                        sp.dma_start(dst[:], ins[src]).then_inc(loaded, 16)
                    sp.wait_ge(loaded, 64)

                @block.tensor
                def _(pe):
                    for t in range(TILES):
                        if t == TILES - 2:
                            pe.wait_ge(step, 3)
                            nc.tensor.matmul(bank[6][:, 0:2], ones[:, :], S[:, 0, :],
                                             start=True, stop=True).then_inc(total, 1)
                        ts = slice(t * P, (t + 1) * P)
                        if t >= 2:
                            pe.wait_ge(gate_ready, t - 1)
                        nc.tensor.matmul(bank[4 + t % 2][:, 0:D], G1[:, ts], wg2s[:, :],
                                         start=True, stop=True).then_inc(g_ready, 1)
                        if t >= 4:
                            pe.wait_ge(y_ready, t - 3)
                        for m in range(HALVES):
                            nc.tensor.matmul(bank[t % 4][:, m * P:(m + 1) * P], XH[:, m, ts], identr[:, :],
                                             start=True, stop=False)
                            mm = nc.tensor.matmul(bank[t % 4][:, m * P:(m + 1) * P], XL[:, m, ts], identr[:, :],
                                                  start=False, stop=True)
                        mm.then_inc(o_ready, 1)

                @block.scalar
                def _(act):
                    for t in range(TILES):
                        act.wait_ge(g_ready, t + 1)
                        if t >= 4:
                            act.wait_ge(y_ready, t - 3)
                        nc.scalar.activation(SG[:, t % 4, :], bank[4 + t % 2][:, 0:D],
                                             ACT.Sigmoid).then_inc(gate_ready, 1)

                @block.vector
                def _(dve):
                    nc.vector.memset(ones[:], 1.0).then_inc(step, 1)
                    for t in range(TILES + 2):
                        if t in (TILES - 5, TILES - 4):
                            i = t - (TILES - 5)
                            dve.wait_ge(loaded, 64)
                            nc.vector.tensor_reduce(S[:, 0, i:i + 1], flat[i], AX.X, ALU.add,
                                                    apply_absolute_value=True).then_inc(step, 1)
                        if t == TILES:
                            dve.wait_ge(total, 1)
                            nc.vector.tensor_scalar(S[:, 1, :], bank[6][:, 0:2], 1.0 / (D * FF), 1e-8,
                                                    ALU.mult, ALU.max).then_inc(step, 1)
                            dve.wait_ge(step, 4)
                            nc.vector.tensor_scalar(S[:, 2, :], S[:, 1, :], 0.5, None, ALU.mult).then_inc(step, 1)
                            nc.vector.tensor_scalar(S[:, 3, :], S[:, 1, :], -0.5, None, ALU.mult).then_inc(step, 1)
                        if t < TILES:
                            dve.wait_ge(o_ready, t + 1)
                            dve.wait_ge(gate_ready, t + 1)
                            nc.vector.tensor_tensor(Y[:, t, :], bank[t % 4][:, 0:D], SG[:, t % 4, :],
                                                    ALU.mult).then_inc(y_ready, 1)
                        if 1 <= t <= TILES:
                            dve.wait_ge(y_ready, t)
                            nc.vector.bn_stats(BN[:, t - 1, :], Y[:, t - 1, :]).then_inc(bn_ready, 1)
                        if t >= 2:
                            dve.wait_ge(bn_ready, t - 1)
                            nc.vector.bn_aggr(MV[:, t - 2, :], BN[:, t - 2, :]).then_inc(mv_ready, 1)

            def ternary(i):
                def work(pool, done):
                    nc.gpsimd.tensor_scalar(up[:], flat[i], S[:, 2, i:i + 1], None, ALU.is_gt).then_inc(done, 1)
                    nc.gpsimd.tensor_scalar(down[:], flat[i], S[:, 3, i:i + 1], None, ALU.is_lt).then_inc(done, 1)
                    pool.wait_ge(done, 2)
                    nc.gpsimd.tensor_tensor(tern[i], up[:], down[:], ALU.subtract).then_inc(done, 1)
                return work

            layer_norm_turn(nc, bank, Y, STD, MV, XN, XH, XL, ident, "lno", pool_work=ternary(0))
            add_product_and_stats(nc, bank, RES, BN, MV, XH, XL, wh[:, O], wl[:, O], "delta_o", pool_work=ternary(1))
        layer_norm_turn(nc, bank, RES, STD, MV, XN, XH, XL, ident, "ln3")
        ternary_ffn(nc, sb, bank, RES, XH, XL, out, w1t, w2t, b1, b2)


def chunk_buffers(sb, ctx, i):
    return (sb(ctx, f"dchunk_hi{i}", [P, HALVES, CB, PAD], F32R),
            sb(ctx, f"dchunk_lo{i}", [P, HALVES, CB, PAD], F32R),
            sb(ctx, f"q_and_a{i}", [P, HALVES, CB, 2, SEQ]),
            sb(ctx, f"dk_t{i}", [P, HALVES, CB, SEQ]))


VALUE_BANKS = (6, 7, 4, 5)
NR = 2


def work_buffers(sb, ctx):
    return {
        "KQ": sb(ctx, "k_square_then_norm", [P, HALVES, CT]),
        "SQ": sb(ctx, "sig_qk", [P, 2, CT]),
        "GM": sb(ctx, "sig_gamma", [P, HALVES, CT]),
        "FM": sb(ctx, "sig_f", [P, HALVES, CT]),
        "KX": sb(ctx, "dk_by_head", [P, NR, PAIRS * 2, PAD]),
        "SV": sb(ctx, "sig_v", [P, IP, D]),
        "LZ": sb(ctx, "log_f", [P, 4, IP * HEADS]),
        "LF": sb(ctx, "log_f_pairs", [P, CB, PAIRS]),
        "MS": sb(ctx, "decay_steps", [P, 2, PAIRS, SEQ]),
        "DS": sb(ctx, "decay", [P, 2, PAIRS, SEQ]),
    }


def zero_pads(nc, name, tensors):
    with stage(nc, name) as (block, zeroed):
        @block.gpsimd
        def _(pool):
            for t in tensors[0::2]:
                nc.gpsimd.memset(t[:, :, :, SEQ:PAD].bitcast(F32), 0.0).then_inc(zeroed, 1)

        @block.vector
        def _(dve):
            for t in tensors[1::2]:
                nc.vector.memset(t[:, :, :, SEQ:PAD].bitcast(F32), 0.0).then_inc(zeroed, 1)


def delta_step(nc, bank, wh, wl, wvfh, wvfl, same, after, past, here, identb, hmask, xh_c, xl_c,
               PA, VH, work, attended, nxt, place, now, then, low_gate=None):
    Q, K, GAMMA, F, O = range(5)
    KQ, SQ, GM, FM, KX, SV, LZ, LF, MS, DS = (work[n] for n in (
        "KQ", "SQ", "GM", "FM", "KX", "SV", "LZ", "LF", "MS", "DS"))
    NK = KQ
    if attended:
        SH, SL, QA, KT = now
    if nxt is not None:
        SHn, SLn, QAn, KTn = then
    spans = [slice(t, min(t + 512, TOKENS)) for t in range(0, TOKENS, 512)] if low_gate else []
    jobs = ((K, 0), (K, 1), (Q, 0), (Q, 1), (GAMMA, 0), (F, 0), (GAMMA, 1), (F, 1))

    def half(s):
        return slice(s * PAD, (s + 1) * PAD)

    def pair(s, p, k):
        return s[:, k, 2 * p:2 * p + 2, :].rearrange("p b s -> p (b s)")

    def images(t):
        return t.rearrange("p (b s) -> p b s", b=CB)

    with stage(nc, "din_hi", "din_lo", "dproj", "sig", "silu", "k_sq", "k_n2", "k_max", "k_log", "k_inv",
               "k_unit", "gf", "qa_ready", "wide_v", "wide_p", "dv_proj", "dv_sig",
               "dv_out", "z_neg", "z_step", "z_act", "lf_ready", "steps_ready", "d_log", "d_exp",
               "dscores", "pa_ready", "g1", "g1_out", "g1_again", "g1_lo", "wg2_hi",
               "wg2_lo") as (
            block, in_hi, in_lo, proj, sig, silu, k_sq, k_n2, k_max, k_log, k_inv,
            k_unit, gf, qa_ready, wide_v, wide_p, v_proj, v_sig,
            v_out, z_neg, z_step, z_act, lf_ready, steps_ready, d_log, d_exp,
            dscores, pa_ready, g1_ready, g1_out, g1_again, g1_lo, wg2_hi, wg2_lo):

        @block.tensor
        def _(pe):
            def project(n):
                if nxt is None:
                    return
                if n == 0:
                    pe.wait_ge(in_hi, HALVES)
                    pe.wait_ge(in_lo, HALVES)
                if n < 2 and attended:
                    pe.wait_ge(v_out, 4 * (n + 1))
                if n in (2, 3):
                    pe.wait_ge(silu, n - 1)
                if n in (4, 5):
                    pe.wait_ge(k_max, n - 3)
                if n >= 6:
                    pe.wait_ge(sig, n - 1)
                tensor, m = jobs[n]
                passes = [x for k in range(HALVES) for x in split_products(
                    wh[:, tensor, k, m * P:(m + 1) * P], wl[:, tensor, k, m * P:(m + 1) * P],
                    SHn[:, k, :, 0:SEQ], SLn[:, k, :, 0:SEQ])]
                for i, (left, right) in enumerate(passes):
                    mm = nc.tensor.matmul(bank[6 + n % 2][:, 0:CT], left, right,
                                          start=(i == 0), stop=(i == len(passes) - 1))
                mm.then_inc(proj, 1)

            def key_norm(m):
                if nxt is None:
                    return
                pe.wait_ge(k_sq, m + 1)
                pe.wait_ge(silu, m + 3)
                nc.tensor.matmul(bank[6 + m][:, 0:CT], same[:, :], KQ[:, m, :],
                                 start=True, stop=True).then_inc(k_n2, 1)

            def values(p):
                if not attended:
                    return
                passes = [x for k in range(HALVES) for x in split_products(
                    pair(SH, p, k), pair(SL, p, k), wvfh[:, k, :], wvfl[:, k, :])]
                for i, (left, right) in enumerate(passes):
                    mm = nc.tensor.matmul(bank[VALUE_BANKS[p]][:, 0:D + HEADS], left, right,
                                          start=(i == 0), stop=(i == len(passes) - 1))
                mm.then_inc(v_proj, 1)

            def decay(b):
                if not attended:
                    return
                pe.wait_ge(steps_ready, b + 1)
                if b >= 2:
                    pe.wait_ge(d_exp, b - 1)
                else:
                    pe.wait_ge(v_out, 4 * (b + 3))
                nc.tensor.matmul(bank[4 + b % 2][:, 0:CT], identb[:, :], spread(past[:, :], 1, PAIRS),
                                 start=True, stop=False)
                nc.tensor.matmul(bank[4 + b % 2][:, 0:CT], after[:, :],
                                 MS[:, b % 2].rearrange("p g t -> p (g t)"),
                                 start=False, stop=True).then_inc(d_log, 1)

            def score(b):
                if not attended:
                    return
                for m in range(HALVES):
                    pe.wait_ge(wide_v if m == 0 else wide_p, b + 1)
                    if b >= 2:
                        pe.wait_ge(pa_ready, HALVES * (b - 2) + m + 1)
                    for g in range(PPH):
                        h = 2 * (PPH * m + g)
                        mm = nc.tensor.matmul(
                            bank[2 * (b % 2) + m][:, g * 2 * SEQ:(g + 1) * 2 * SEQ],
                            KX[:, b % NR, h:h + 2].rearrange("p e s -> p (e s)"),
                            QA[:, m, b].rearrange("p x t -> p (x t)"), start=True, stop=True)
                    mm.then_inc(dscores, 1)

            def low_part(i):
                if not low_gate:
                    return
                wgh, wgl, XH, XL = low_gate[0:4]
                passes = [x for k in range(HALVES) for x in split_products(
                    wgh[:, k, :], wgl[:, k, :], XH[:, k, spans[i]], XL[:, k, spans[i]])]
                for n, (left, right) in enumerate(passes):
                    mm = nc.tensor.matmul(bank[i][0:HD, 0:spans[i].stop - spans[i].start], left, right,
                                          start=(n == 0), stop=(n == len(passes) - 1))
                mm.then_inc(g1_ready, 1)

            for p in range(IP):
                values(p)
            low_part(0)
            project(0)
            project(1)
            low_part(1)
            score(0)
            score(1)
            project(2)
            project(3)
            low_part(2)
            decay(0)
            decay(1)
            key_norm(0)
            key_norm(1)
            low_part(3)
            low_part(4)
            project(4)
            project(5)
            score(2)
            decay(2)
            project(6)
            project(7)
            score(3)
            for b in range(3, CB):
                decay(b)
                if b > 3:
                    score(b)

        @block.scalar
        def _(act):
            nc.scalar.preload_act_table_set("sigmoid_and_others")
            if nxt is not None:
                for m in range(HALVES):
                    nc.scalar.activation(SHn[:, m, :, 0:SEQ], images(xh_c[:, m, nxt, :].bitcast(F32)),
                                         ACT.Copy).then_inc(in_hi, 1)
            if attended:
                for p in range(IP):
                    act.wait_ge(v_proj, p + 1)
                    act.wait_ge(z_step, 2 * p + 2)
                    nc.scalar.activation(SV[:, p, :], bank[VALUE_BANKS[p]][:, 0:D], ACT.Sigmoid).then_inc(v_sig, 1)
                nc.scalar.preload_act_table_set("natural_log_exp_and_others")
                nc.scalar.activation(LZ[:, 1, :], LZ[:, 1, :], ACT.Exp).then_inc(z_act, 1)
                act.wait_ge(z_step, 2 * IP + 1)
                nc.scalar.activation(LZ[:, 2, :], LZ[:, 2, :], ACT.Ln).then_inc(z_act, 1)

            def sigmoids(numbers):
                if nxt is None:
                    return
                for n in numbers:
                    tensor, m = jobs[n]
                    act.wait_ge(proj, n + 1)
                    if n in (2, 3):
                        act.wait_ge(silu, n - 1)
                    dst = SQ[:, n % 2] if n < 4 else (GM if tensor == GAMMA else FM)[:, m]
                    nc.scalar.activation(dst, bank[6 + n % 2][:, 0:CT], ACT.Sigmoid).then_inc(sig, 1)

            def decay(b):
                if not attended:
                    return
                act.wait_ge(d_log, b + 1)
                if b >= 2:
                    act.wait_ge(pa_ready, HALVES * (b - 1))
                nc.scalar.activation(DS[:, b % 2].rearrange("p g t -> p (g t)"),
                                     bank[4 + b % 2][:, 0:CT], ACT.Exp).then_inc(d_exp, 1)

            def low_high(parts):
                for ts in parts:
                    i = spans.index(ts)
                    act.wait_ge(g1_ready, i + 1)
                    nc.scalar.activation(low_gate[4][GATE_PARTS[0], ts], bank[i][0:HD, 0:ts.stop - ts.start],
                                         ACT.Copy).then_inc(g1_out, 1)

            sigmoids(range(0, 4))
            low_high(spans[0:3])
            nc.scalar.preload_act_table_set("natural_log_exp_and_others")
            decay(0)
            decay(1)
            if nxt is not None:
                for m in range(HALVES):
                    act.wait_ge(k_max, m + 1)
                    nc.scalar.activation(NK[:, m, :], NK[:, m, :], ACT.Ln).then_inc(k_log, 1)
                for m in range(HALVES):
                    act.wait_ge(k_log, m + 1)
                    nc.scalar.activation(NK[:, m, :], NK[:, m, :], ACT.Exp, scale=-0.5).then_inc(k_inv, 1)
                low_high(spans[3:])
                sigmoids(range(4, 8))
                nc.scalar.preload_act_table_set("natural_log_exp_and_others")
            for b in range(2, CB):
                decay(b)

        @block.vector
        def _(dve):
            def low_in():
                if nxt is None:
                    return
                for m in range(HALVES):
                    nc.vector.tensor_copy(SLn[:, m, :, 0:SEQ],
                                          images(xl_c[:, m, nxt, :].bitcast(F32))).then_inc(in_lo, 1)

            def forget_inputs(p):
                if not attended:
                    return
                dve.wait_ge(v_proj, p + 1)
                z = bank[VALUE_BANKS[p]][:, D:D + HEADS]
                zs = slice(p * HEADS, (p + 1) * HEADS)
                nc.vector.tensor_scalar(LZ[:, 0, zs], z, 0.0, None, ALU.min).then_inc(z_step, 1)
                nc.vector.tensor_scalar(LZ[:, 3, zs], z, -1.0, None, ALU.mult).then_inc(z_neg, 1)
                dve.wait_ge(z_neg, p + 1)
                nc.vector.tensor_tensor(LZ[:, 1, zs], z, LZ[:, 3, zs], ALU.min).then_inc(z_step, 1)

            def plus_one():
                if not attended:
                    return
                dve.wait_ge(z_act, 1)
                nc.vector.tensor_scalar(LZ[:, 2, :], LZ[:, 1, :], 1.0, None, ALU.add).then_inc(z_step, 1)

            def log_forget():
                if not attended:
                    return
                dve.wait_ge(z_act, 2)
                nc.vector.tensor_tensor(LZ[:, 3, :], LZ[:, 0, :], LZ[:, 2, :], ALU.subtract).then_inc(z_step, 1)
                dve.wait_ge(z_step, 2 * IP + 2)
                for s in range(2):
                    lz = LZ[half(s), 3, :].rearrange("p (i g e) -> p i g e", i=IP, e=2)
                    for e in range(2):
                        nc.vector.tensor_copy(LF[half(e)].rearrange("p (i s) g -> p i s g", s=2)[:, :, s, :],
                                              lz[:, :, :, e]).then_inc(lf_ready, 1)

            def silu_of(n):
                if nxt is None:
                    return
                tensor, m = jobs[n]
                dve.wait_ge(sig, n + 1)
                nc.vector.tensor_tensor(QAn[:, m, :, 0, :] if tensor == Q else KTn[:, m],
                                        images(bank[6 + n % 2][:, 0:CT]), images(SQ[:, n % 2]),
                                        ALU.mult).then_inc(silu, 1)

            def values_of(p):
                if not attended:
                    return
                dve.wait_ge(v_sig, p + 1)
                for s in range(2):
                    v4 = bank[VALUE_BANKS[p]][half(s), 0:D].rearrange("p (g e d) -> p g e d", e=2, d=HD)
                    s4 = SV[half(s), p, :].rearrange("p (g e d) -> p g e d", e=2, d=HD)
                    for e in range(2):
                        nc.vector.tensor_tensor(VH[half(e), place * CB + 2 * p + s], v4[:, :, e, :],
                                                s4[:, :, e, :], ALU.mult).then_inc(v_out, 1)

            def bounded(m):
                if nxt is None:
                    return
                dve.wait_ge(k_n2, m + 1)
                nc.vector.tensor_scalar(NK[:, m, :], bank[6 + m][:, 0:CT], 1e-24, None, ALU.max).then_inc(k_max, 1)

            def unit_key(m):
                if nxt is None:
                    return
                dve.wait_ge(k_inv, m + 1)
                flat = KTn[:, m].rearrange("p b s -> p (b s)")
                nc.vector.tensor_tensor(flat, flat, NK[:, m, :], ALU.mult).then_inc(k_unit, 1)

            def a_of(m):
                if nxt is None:
                    return
                dve.wait_ge(k_unit, m + 1)
                dve.wait_ge(gf, m + 1)
                nc.vector.scalar_tensor_tensor(
                    out=QAn[:, m, :, 1, :], in0=KTn[:, m], scalar=-1.0, in1=images(GM[:, m]),
                    op0=ALU.mult, op1=ALU.mult).then_inc(qa_ready, 1)

            def widen(b):
                if not attended or b >= CB:
                    return
                if b >= NR:
                    dve.wait_ge(dscores, HALVES * (b - NR) + 1)
                nc.vector.tensor_tensor(
                    KX[:, b % NR, 0:HPH, 0:SEQ], spread(KT[:, 0, b, :], 1, HPH), spread(hmask[:, :], 2, SEQ),
                    ALU.mult).then_inc(wide_v, 1)

            def weigh(b):
                if not attended:
                    return
                dve.wait_ge(d_exp, b + 1)
                for m in range(HALVES):
                    dve.wait_ge(dscores, HALVES * b + m + 1)
                    nc.vector.tensor_tensor(
                        PA[:, place * CB + b, PPH * m:PPH * (m + 1)],
                        bank[2 * (b % 2) + m][:, 0:CT].rearrange("p (g x t) -> p g x t", g=PPH, x=2),
                        spread(DS[:, b % 2, PPH * m:PPH * (m + 1)], 2, 2),
                        ALU.mult).then_inc(pa_ready, 1)

            low_in()
            widen(0)
            for p in range(IP):
                forget_inputs(p)
            widen(1)
            values_of(0)
            values_of(1)
            plus_one()
            values_of(2)
            values_of(3)
            log_forget()
            silu_of(0)
            silu_of(1)
            widen(2)
            silu_of(2)
            silu_of(3)
            widen(3)
            bounded(0)
            bounded(1)
            if low_gate:
                G1, wg2, wg2s = low_gate[4:7]
                dve.wait_ge(wg2_hi, 1)
                nc.vector.tensor_tensor(wg2s[GATE_PARTS[1], :], wg2[:, :],
                                        wg2s[GATE_PARTS[0], :].bitcast(F32), ALU.subtract).then_inc(wg2_lo, 1)
                for i, ts in enumerate(spans):
                    dve.wait_ge(g1_out, i + 1)
                    nc.vector.tensor_tensor(G1[GATE_PARTS[2], ts], bank[i][0:HD, 0:ts.stop - ts.start],
                                            G1[GATE_PARTS[0], ts].bitcast(F32), ALU.subtract).then_inc(g1_lo, 1)
            weigh(0)
            weigh(1)
            unit_key(0)
            unit_key(1)
            widen(4)
            weigh(2)
            a_of(0)
            a_of(1)
            for b in range(3, CB):
                weigh(b)
                widen(b + 2)

        @block.gpsimd
        def _(pool):
            def widen(b):
                if not attended:
                    return
                if b >= NR:
                    pool.wait_ge(dscores, HALVES * (b - NR) + 2)
                nc.gpsimd.tensor_tensor(
                    KX[:, b % NR, HPH:HEADS, 0:SEQ], spread(KT[:, 1, b, :], 1, HPH), spread(hmask[:, :], 2, SEQ),
                    ALU.mult).then_inc(wide_p, 1)

            def steps(b):
                if not attended:
                    return
                if b == 0:
                    pool.wait_ge(lf_ready, 4)
                if b >= 2:
                    pool.wait_ge(d_log, b - 1)
                nc.gpsimd.tensor_tensor(MS[:, b % 2], spread(LF[:, b, :], 2, SEQ),
                                        spread(here[:, :], 1, PAIRS), ALU.mult).then_inc(steps_ready, 1)

            def square(m):
                if nxt is None:
                    return
                pool.wait_ge(silu, m + 1)
                flat = KTn[:, m].rearrange("p b s -> p (b s)")
                nc.gpsimd.tensor_tensor(KQ[:, m, :], flat, flat, ALU.mult).then_inc(k_sq, 1)

            def gates(m):
                if nxt is None:
                    return
                pool.wait_ge(sig, 2 * m + 6)
                nc.gpsimd.tensor_tensor(GM[:, m, :], GM[:, m, :], FM[:, m, :], ALU.mult).then_inc(gf, 1)

            widen(0)
            widen(1)
            steps(0)
            steps(1)
            square(0)
            square(1)
            widen(2)
            widen(3)
            steps(2)
            steps(3)
            if low_gate:
                G1, wg2, wg2s = low_gate[4:7]
                pool.wait_ge(k_sq, HALVES)
                for n, part in enumerate((0, 2)):
                    nc.gpsimd.tensor_copy(wg2s[GATE_PARTS[part], :], wg2[:, :]).then_inc(wg2_hi, 1)
                    pool.wait_ge(wg2_hi, n + 1)
                for i, ts in enumerate(spans):
                    pool.wait_ge(g1_out, i + 1)
                    nc.gpsimd.tensor_copy(G1[GATE_PARTS[1], ts], G1[GATE_PARTS[0], ts].bitcast(F32)
                                          ).then_inc(g1_again, 1)
                    pool.wait_ge(g1_again, i + 1)
            gates(0)
            gates(1)
            for b in range(4, CB):
                widen(b)
                steps(b)


def delta_solve(nc, sb, bank, ident, PA, VH, XH, XL, quarter):
    DV = 12
    with ExitStack() as ctx:
        AS = sb(ctx, "a_rows", [P, SEQ, 2, SEQ])
        U = sb(ctx, "u", [P, 2, HD, PAD])
        UB = PA[:, :, :, 1, 0:2 * HD]
        AC = sb(ctx, "a_columns", [P, SEQ, 2, SEQ])
        PD = sb(ctx, "products", [P, 2, DV, SEQ])
        PP = sb(ctx, "pool_products", [P, 2, HD - DV, SEQ - 1])
        a_cols = PA[:].rearrange("p i g x t -> p (i g) x t")
        v_cols = VH[:].rearrange("p i g d -> p (i g) d")
        xh_q = XH[:, :, :].rearrange("p m (q t) -> p m q t", q=4)
        xl_q = XL[:, :, :].rearrange("p m (q t) -> p m q t", q=4)
        VG = HD // 4
        AG = (SEQ + 3) // 4
        OG = QUARTER // 4
        with stage(nc, "u_zero", "turned_in", "taken_in", "columns", "diagonal", "multiplied", "solved", "pool_multiplied",
                   "pool_solved",
                   "u_turned", "u_back", "u_back_v", "o_done", "o_hi", "o_lo") as (
                block, u_zero, turned_in, taken_in, columns, diagonal, multiplied, solved, pool_multiplied,
                pool_solved,
                u_turned, u_back, u_back_v, o_done, o_hi, o_lo):
            @block.tensor
            def _(pe):
                for i in range(VG + AG):
                    if i >= 4:
                        pe.wait_ge(taken_in, i - 3)
                    if i >= 4 + VG:
                        pe.wait_ge(columns, i - 3 - VG)
                    for j in range(4):
                        if i < VG:
                            col = v_cols[:, :, 4 * i + j]
                        else:
                            col = a_cols[:, :, 1, min(4 * (i - VG) + j, SEQ - 1)]
                        mm = nc.tensor.transpose(bank[i % 4][:, j * P:(j + 1) * P], col, ident[:, :])
                    mm.then_inc(turned_in, 1)
                pe.wait_ge(taken_in, VG + AG)
                pe.wait_ge(columns, AG)
                pe.wait_ge(solved, 2 * (SEQ - 1))
                pe.wait_ge(pool_solved, SEQ - 1)
                for i in range(2 * VG):
                    if i >= 4:
                        pe.wait_ge(u_back if i % 2 == 0 else u_back_v, (i - 4) // 2 + 1)
                    for j in range(4):
                        mm = nc.tensor.transpose(bank[i % 4][0:PAD, j * P:(j + 1) * P],
                                                 U[:, i // VG, 4 * (i % VG) + j, :], ident[:, :])
                    mm.then_inc(u_turned, 1)
                pe.wait_ge(u_back, VG)
                pe.wait_ge(u_back_v, VG)
                pe.wait_ge(u_zero, 2)
                for o in range(OG):
                    if o >= 2:
                        pe.wait_ge(o_lo, o - 1)
                    for m in range(HALVES):
                        for j in range(4):
                            for g in range(PPH):
                                mm = nc.tensor.matmul(
                                    bank[4 + o % 2][32 * g:32 * g + 32, (4 * m + j) * SEQ:(4 * m + j + 1) * SEQ],
                                    UB[:, 4 * o + j, PPH * m + g, :], PA[:, 4 * o + j, PPH * m + g, 0, :],
                                    start=True, stop=True)
                    mm.then_inc(o_done, 1)

            @block.scalar
            def _(act):
                for i in range(VG + AG):
                    act.wait_ge(turned_in, i + 1)
                    src = bank[i % 4][:, :].rearrange("p (j e s) -> p j e s", j=4, e=2)
                    if i < VG:
                        nc.scalar.activation(U[:, :, 4 * i:4 * i + 4, :].rearrange("p e d s -> p d e s"),
                                             src, ACT.Copy).then_inc(taken_in, 1)
                    else:
                        n = min(4, SEQ - 4 * (i - VG))
                        ts = slice(4 * (i - VG), 4 * (i - VG) + n)
                        nc.scalar.activation(AS[:, ts], src[:, 0:n, :, 0:SEQ], ACT.Copy).then_inc(taken_in, 1)
                        nc.scalar.activation(AC[:, :, :, ts].rearrange("p s e t -> p t e s"),
                                             src[:, 0:n, :, 0:SEQ], ACT.Copy).then_inc(columns, 1)
                for e in range(2):
                    others = UB[e * PAD:(e + 1) * PAD, :, :, (1 - e) * HD:(2 - e) * HD]
                    nc.scalar.activation(others, others, ACT.Copy, scale=0.0).then_inc(u_zero, 1)
                for i in range(0, 2 * VG, 2):
                    act.wait_ge(u_turned, i + 1)
                    e, d = i // VG, 4 * (i % VG)
                    nc.scalar.activation(
                        UB[e * PAD:(e + 1) * PAD].rearrange("p i g c -> p c (i g)")[:, e * HD + d:e * HD + d + 4, :],
                        bank[i % 4][0:PAD, :].rearrange("p (j c) -> p j c", j=4), ACT.Copy).then_inc(u_back, 1)
                for o in range(OG):
                    act.wait_ge(o_done, o + 1)
                    nc.scalar.activation(xh_q[:, :, quarter, 4 * o * SEQ:4 * (o + 1) * SEQ],
                                         bank[4 + o % 2][:, 0:8 * SEQ].rearrange("p (m t) -> p m t", m=HALVES),
                                         ACT.Copy).then_inc(o_hi, 1)

            @block.vector
            def _(dve):
                def unit_diagonal(n):
                    dve.wait_ge(taken_in, VG + n + 1)
                    for t in range(4 * n, min(4 * n + 4, SEQ)):
                        last = nc.vector.memset(AS[:, t, :, t:t + 1], 1.0)
                    last.then_inc(diagonal, 1)

                unit_diagonal(0)
                for t in range(1, SEQ):
                    if t % 4 == 1 and t // 4 + 1 < AG:
                        unit_diagonal(t // 4 + 1)
                    dve.wait_ge(diagonal, t // 4 + 1)
                    for e in range(2):
                        if t >= 2:
                            dve.wait_ge(solved, 2 * (t - 2) + e + 1)
                        nc.vector.tensor_tensor(PD[:, e, :, 0:t + 1], spread(AS[:, t, e, 0:t + 1], 1, DV),
                                                U[:, e, 0:DV, 0:t + 1], ALU.mult).then_inc(multiplied, 1)
                    for e in range(2):
                        dve.wait_ge(multiplied, 2 * (t - 1) + e + 1)
                        nc.vector.tensor_reduce(U[:, e, 0:DV, t], PD[:, e, :, 0:t + 1], AX.X,
                                                ALU.add).then_inc(solved, 1)
                for i in range(1, 2 * VG, 2):
                    dve.wait_ge(u_turned, i + 1)
                    e, d = i // VG, 4 * (i % VG)
                    nc.vector.tensor_copy(
                        UB[e * PAD:(e + 1) * PAD].rearrange("p i g c -> p c (i g)")[:, e * HD + d:e * HD + d + 4, :],
                        bank[i % 4][0:PAD, :].rearrange("p (j c) -> p j c", j=4)).then_inc(u_back_v, 1)
                for o in range(OG):
                    dve.wait_ge(o_hi, o + 1)
                    ts = slice(4 * o * SEQ, 4 * (o + 1) * SEQ)
                    nc.vector.tensor_tensor(xl_q[:, :, quarter, ts],
                                            bank[4 + o % 2][:, 0:8 * SEQ].rearrange("p (m t) -> p m t", m=HALVES),
                                            xh_q[:, :, quarter, ts].bitcast(F32), ALU.subtract).then_inc(o_lo, 1)

            @block.gpsimd
            def _(pool):
                pool.wait_ge(taken_in, VG)
                pool.wait_ge(columns, AG)
                for s in range(SEQ - 1):
                    later = slice(s + 1, SEQ)
                    if s >= 1:
                        pool.wait_ge(pool_solved, s)
                    nc.gpsimd.tensor_tensor(PP[:, :, :, s:SEQ - 1], spread(AC[:, s, :, later], 2, HD - DV),
                                            spread(U[:, :, DV:HD, s], 3, SEQ - 1 - s),
                                            ALU.mult).then_inc(pool_multiplied, 1)
                    pool.wait_ge(pool_multiplied, s + 1)
                    nc.gpsimd.tensor_tensor(U[:, :, DV:HD, later], U[:, :, DV:HD, later], PP[:, :, :, s:SEQ - 1],
                                            ALU.add).then_inc(pool_solved, 1)


def ternary_ffn(nc, sb, bank, RES, XH, XL, out, w1t, w2t, b1, b2):
    with ExitStack() as ctx:
        H = sb(ctx, "fhidden", [P, 4, MT * P])
        HH = sb(ctx, "fhidden_hi", [P, 2, FB, MT * P], F32R)
        HL = sb(ctx, "fhidden_lo", [P, 2, FB, MT * P], F32R)
        steps = [range(t, min(t + MT, TILES)) for t in range(0, TILES, MT)]
        with stage(nc, "f_up", "f_act", "f_hi", "f_lo", "f_down", "f_bias", "f_out", "stored") as (
                block, up_ready, acted, h_hi, h_lo, down_ready, biased, out_ready, stored):
            @block.tensor
            def _(pe):
                def hidden(c):
                    n = len(steps[c]) * P
                    ts = slice(steps[c][0] * P, steps[c][0] * P + n)
                    for f in range(FB):
                        i = FB * c + f
                        if i >= 4:
                            pe.wait_ge(acted, i - 3)
                        passes = [(w1t[:, k, f * P:(f + 1) * P], X[:, k, ts]) for k in range(HALVES) for X in (XH, XL)]
                        for j, (left, right) in enumerate(passes):
                            mm = nc.tensor.matmul(bank[i % 4][:, 0:n], left, right,
                                                  start=(j == 0), stop=(j == len(passes) - 1))
                        mm.then_inc(up_ready, 1)

                def output(c):
                    pe.wait_ge(h_lo, FB * (c + 1))
                    for j, t in enumerate(steps[c]):
                        if t >= 4:
                            pe.wait_ge(out_ready, t - 3)
                        passes = [(X[:, c % 2, f, j * P:(j + 1) * P], w2t[:, f, :]) for f in range(FB) for X in (HH, HL)]
                        for n, (left, right) in enumerate(passes):
                            mm = nc.tensor.matmul(bank[4 + t % 4][:, 0:D], left, right,
                                                  start=(n == 0), stop=(n == len(passes) - 1))
                        mm.then_inc(down_ready, 1)

                hidden(0)
                for c in range(len(steps)):
                    if c + 1 < len(steps):
                        hidden(c + 1)
                    output(c)

            @block.scalar
            def _(act):
                for c, st in enumerate(steps):
                    n = len(st) * P
                    for f in range(FB):
                        i = FB * c + f
                        act.wait_ge(up_ready, i + 1)
                        if i >= 4:
                            act.wait_ge(h_lo, i - 3)
                        nc.scalar.activation(H[:, i % 4, 0:n], bank[i % 4][:, 0:n], ACT.Gelu,
                                             bias=b1[:, f:f + 1]).then_inc(acted, 1)

            @block.vector
            def _(dve):
                def finish(c):
                    for t in steps[c]:
                        dve.wait_ge(down_ready, t + 1)
                        dve.wait_ge(biased, t + 1)
                        nc.vector.tensor_tensor(RES[:, t, :], RES[:, t, :], bank[4 + t % 4][:, 0:D],
                                                ALU.add).then_inc(out_ready, 1)

                for c, st in enumerate(steps):
                    n = len(st) * P
                    if c >= 2:
                        dve.wait_ge(down_ready, steps[c - 2][-1] + 1)
                    for f in range(FB):
                        i = FB * c + f
                        dve.wait_ge(acted, i + 1)
                        nc.vector.tensor_copy(HH[:, c % 2, f, 0:n], H[:, i % 4, 0:n]).then_inc(h_hi, 1)
                        dve.wait_ge(h_hi, i + 1)
                        nc.vector.tensor_tensor(HL[:, c % 2, f, 0:n], H[:, i % 4, 0:n],
                                                HH[:, c % 2, f, 0:n].bitcast(F32), ALU.subtract).then_inc(h_lo, 1)
                    if c >= 1:
                        finish(c - 1)
                finish(len(steps) - 1)

            @block.gpsimd
            def _(pool):
                for t in range(TILES):
                    nc.gpsimd.tensor_tensor(RES[:, t, :], RES[:, t, :], b2[:, :], ALU.add).then_inc(biased, 1)

            @block.sync
            def _(sp):
                for t in range(TILES):
                    sp.wait_ge(out_ready, t + 1)
                    sp.dma_start(out[t * P:(t + 1) * P, :], RES[:, t, :]).then_inc(stored, 16)
                sp.wait_ge(stored, 16 * TILES)



def _constants():
    one = np.float32
    base = one(10000.0)
    half = HD // 2
    inv_freq = one(1.0) / base ** (np.arange(half, dtype=np.float32) / one(half))
    ang = inv_freq[:, None] * np.arange(SEQ, dtype=np.float32)[None, :]
    cos = np.concatenate([np.cos(ang), np.cos(ang)], 0)
    sin = np.concatenate([-np.sin(ang), np.sin(ang)], 0)
    part = np.arange(P)
    step = np.arange(SEQ)
    row = part % PAD
    col = np.arange(P)
    same = (part[:, None] // PAD) == (col[None, :] // PAD)
    later = (part[:, None] % PAD) > (col[None, :] % PAD)
    real = (row[:, None] < SEQ) & ((col[None, :] % PAD) < SEQ)
    return {
        "ident": np.eye(P),
        "head_mask": (part[:, None] // HD) == np.arange(HPH)[None, :],
        "cos": np.tile(cos, (HPH, 1)),
        "sin": np.tile(sin, (HPH, 1)),
        "same_head": (part[:, None] // HD) == (col[None, :] // HD),
        "causal": np.where((row[:, None] < SEQ) & (step[None, :] > row[:, None]), MASKED, 0.0),
        "past": np.where((row[:, None] >= SEQ) | (step[None, :] < row[:, None]), MASKED, 0.0),
        "from_here": (row[:, None] <= step[None, :]),
        "after": same & later & real,
        "ties": np.tile((np.arange(EXPERTS)[None, :] <= np.arange(EXPERTS)[:, None]).reshape(1, -1), (P, 1)),
    }


def _lay_out(v):
    def rows(a):
        return a.reshape(-1, P, a.shape[-1]).transpose(1, 0, 2)

    def cols(a):
        return a.reshape(-1, P).T

    def swapped(a):
        return a.reshape(D, HEADS, 2, HD // 2)[:, :, ::-1].reshape(D, D)

    x = v["x"].reshape(IMAGES, 3, 6, 16, 6, 16).transpose(1, 3, 5, 0, 2, 4).reshape(KP, P, CHUNKS, CP)
    first = np.concatenate([v["cls_tok"].reshape(1, D), v["L0_tok_cls_token"].reshape(1, D),
                            np.repeat(v["L0_tok_b"].reshape(1, D), PATCHES, 0)], 0)
    wq, wk, wv, wo = (v[f"L0_attn_W{n}"].T for n in "qkvo")
    return {
        "patches": x.transpose(2, 1, 0, 3),
        "tok_w": rows(v["L0_tok_W"].T),
        "tok_bias": rows(first.T),
        "tok_pos": rows(v["L0_tok_pos_embedding"][0].T),
        "att_w": np.stack([rows(a) for a in (wq, swapped(wq), wk, swapped(wk), wv, wo)], 1),
        "wr": rows(v["L0_ffn_Wr"]),
        "br": np.repeat(v["L0_ffn_br"].reshape(1, EXPERTS), P, 0),
        "moe_w1": v["L0_ffn_W1"].reshape(EXPERTS, HALVES, P, FF).transpose(0, 2, 1, 3),
        "moe_b1": v["L0_ffn_b1"].reshape(EXPERTS, FB, P).transpose(2, 0, 1),
        "moe_w2": v["L0_ffn_W2"].reshape(EXPERTS, FB, P, D).transpose(0, 2, 1, 3),
        "moe_b2": v["L0_ffn_b2"],
        "delta_w": np.stack([rows(a) for a in (
            v["L1_attn_Wq"], v["L1_attn_Wk"], np.repeat(v["L1_attn_Wgamma"], HD, 1),
            np.repeat(v["L1_attn_Wf"], HD, 1), v["L1_attn_Wo"])], 1),
        "delta_wvf": rows(np.concatenate([v["L1_attn_Wv"], v["L1_attn_Wf"]], 1)),
        "delta_wg1": rows(v["L1_attn_Wg1"]),
        "delta_wg2": v["L1_attn_Wg2"],
        "norm_w": cols(v["L1_attn_norm_w"]),
        "ffn_w1": rows(v["L1_ffn_W1"].T),
        "ffn_b1": cols(v["L1_ffn_b1"]),
        "ffn_w2": rows(v["L1_ffn_W2"].T),
        "ffn_b2": np.repeat(v["L1_ffn_b2"].reshape(1, D), P, 0),
    }


def kernel(**inputs):
    import concourse.bacc as bacc
    from concourse.bass_utils import run_bass_kernel_spmd as run

    arrays = {n: np.ascontiguousarray(a) for n, a in _lay_out({k: np.asarray(a) for k, a in inputs.items()}).items()}
    for n, a in _constants().items():
        arrays[n] = np.ascontiguousarray(a, dtype=np.float32)
    for n, src in (("ident_bf16", "ident"), ("causal", "causal"), ("past", "past")):
        arrays[n] = arrays[src].astype(mybir.dt.np(BF16))
    nc = bacc.Bacc("TRN2", target_bir_lowering=False, num_devices=1)
    ins = {n: nc.dram_tensor(f"in_{n}", a.shape, mybir.dt.from_np(a.dtype), kind="ExternalInput").ap()
           for n, a in arrays.items()}
    out = nc.dram_tensor("out", (TOKENS, D), F32, kind="ExternalOutput").ap()
    build_tower(nc, ins, out)
    r = run(nc, [{f"in_{n}": a for n, a in arrays.items()}], core_ids=[0])
    return r.results[0]["out"].reshape(IMAGES, SEQ, D)
```
